# Optimizing a Trainium2 kernel written in Bass

```python
import numpy as np
import jax
import jax.numpy as jnp

def _softmax(x, axis=-1):
    return jax.nn.softmax(x, axis=axis)

def _gelu(x):
    return jax.nn.gelu(x, approximate=True)

def _silu(x):
    return jax.nn.silu(x)

def _sigmoid(x):
    return jax.nn.sigmoid(x)

def _layernorm(x, axis=-1, eps=1e-05):
    m = jnp.mean(x, axis=axis, keepdims=True)
    v = jnp.var(x, axis=axis, keepdims=True)
    return (x - m) / jnp.sqrt(v + eps)

def _scatter_add(tgt, idx, src, axis=0):
    return tgt.at[idx].add(src)

def _segment_sum(src, seg, n):
    return jax.ops.segment_sum(src, seg, n)
kernel_name = 'mk_gnn_resnorm_d4_gnn_r64_44fae6'

def setup_inputs(seed: int=0):
    np.random.seed(seed)
    _w = jnp.asarray

    def _rec_inputs():
        import jax
        import jax.numpy as jnp
        _gk = jax.random.key(seed)
        x = -0.000202 + 1 * jax.random.normal(jax.random.fold_in(_gk, 1), (50000, 128), jnp.float32)
        src = jax.random.randint(jax.random.fold_in(_gk, 2), (12500,), 0, 50000, jnp.int32)
        dst = jnp.minimum((50000 * jax.random.uniform(jax.random.fold_in(_gk, 3), (12500,)) ** 2.0).astype(jnp.int32), 49999)
        _o = jnp.argsort(dst, stable=True)
        src = src[_o]
        dst = dst[_o]
        edge_attr_128 = 2.93046e-05 + 1.00006 * jax.random.normal(jax.random.fold_in(_gk, 11), (12500, 128), jnp.float32)
        edge_attr_16 = 0.000254156 + 0.999948 * jax.random.normal(jax.random.fold_in(_gk, 12), (12500, 16), jnp.float32)
        return (x, src, dst, edge_attr_128, edge_attr_16)
    x, src, dst, edge_attr_128, edge_attr_16 = _rec_inputs()

    def _L0_gnn_setup():
        import jax, jax.numpy as jnp
        import numpy as np
        N_NODES = 50000
        N_EDGES = 12500
        IN_DIM = 128
        HIDDEN = 256
        OUT_DIM = HIDDEN // 2

        def gcn_conv(x, edge_index, W, b, num_nodes):
            src, dst = (edge_index[0], edge_index[1])
            loops = jnp.arange(num_nodes, dtype=src.dtype)
            src = jnp.concatenate([src, loops])
            dst = jnp.concatenate([dst, loops])
            deg = jax.ops.segment_sum(jnp.ones_like(dst, dtype=x.dtype), dst, num_segments=num_nodes)
            deg_inv_sqrt = jnp.where(deg > 0, jax.lax.rsqrt(jnp.maximum(deg, 1e-12)), 0.0)
            norm = deg_inv_sqrt[src] * deg_inv_sqrt[dst]
            h = x @ W.T
            msgs = norm[:, None] * h[src]
            out = jax.ops.segment_sum(msgs, dst, num_segments=num_nodes)
            return out + b
        key = jax.random.key(seed)
        k_x, k_e, k_w1, k_b1, k_w2, k_b2 = jax.random.split(key, 6)
        x = jax.random.normal(k_x, (N_NODES, IN_DIM), dtype=jnp.float32)
        edge_index = jax.random.randint(k_e, (2, N_EDGES), 0, N_NODES, dtype=jnp.int32)
        s1 = 1.0 / np.sqrt(IN_DIM)
        s2 = 1.0 / np.sqrt(HIDDEN)
        W1 = jax.random.uniform(k_w1, (HIDDEN, IN_DIM), jnp.float32, -s1, s1)
        b1 = jax.random.uniform(k_b1, (HIDDEN,), jnp.float32, -s1, s1)
        W2 = jax.random.uniform(k_w2, (OUT_DIM, HIDDEN), jnp.float32, -s2, s2)
        b2 = jax.random.uniform(k_b2, (OUT_DIM,), jnp.float32, -s2, s2)
        return {'x': x, 'edge_index': edge_index, 'W1': W1, 'b1': b1, 'W2': W2, 'b2': b2}
    _L0_gnn_all = _L0_gnn_setup()
    _L0_gnn_in = {k: v for k, v in _L0_gnn_all.items() if k in ('W1', 'b1', 'W2', 'b2')}
    del _L0_gnn_all

    def _L1_gnn_setup():
        import jax, jax.numpy as jnp
        import numpy as np
        HIDDEN = 128
        N_NODES = 10000
        N_EDGES = 10000
        EPS = 0.0
        key = jax.random.key(seed)
        k = jax.random.split(key, 8)
        x = jax.random.normal(k[0], (N_NODES, HIDDEN), dtype=jnp.float32)
        edge_index = jax.random.randint(k[1], (2, N_EDGES), 0, N_NODES, dtype=jnp.int64)
        edge_attr = jax.random.normal(k[2], (N_EDGES, HIDDEN), dtype=jnp.float32)
        s = 1.0 / np.sqrt(HIDDEN)
        W1 = jax.random.uniform(k[3], (HIDDEN, HIDDEN), jnp.float32, -s, s)
        b1 = jax.random.uniform(k[4], (HIDDEN,), jnp.float32, -s, s)
        W2 = jax.random.uniform(k[5], (HIDDEN, HIDDEN), jnp.float32, -s, s)
        b2 = jax.random.uniform(k[6], (HIDDEN,), jnp.float32, -s, s)
        return {'x': x, 'edge_index': edge_index, 'edge_attr': edge_attr, 'W1': W1, 'b1': b1, 'W2': W2, 'b2': b2}
    _L1_gnn_all = _L1_gnn_setup()
    _L1_gnn_in = {k: v for k, v in _L1_gnn_all.items() if k in ('W1', 'b1', 'W2', 'b2')}
    del _L1_gnn_all

    def _L2_gnn_setup():
        import jax, jax.numpy as jnp
        import numpy as np
        N_NODES = 50000
        N_EDGES = 12500
        IN_C = 128
        OUT_C = 128
        EDGE_F = 16
        NEG_SLOPE = 0.2
        BN_EPS = 1e-05
        key = jax.random.key(seed)
        ks = jax.random.split(key, 8)
        x = jax.random.normal(ks[0], (N_NODES, IN_C), dtype=jnp.float32)
        edge_index = jax.random.randint(ks[1], (2, N_EDGES), 0, N_NODES, dtype=jnp.int64)
        edge_attr = jax.random.normal(ks[2], (N_EDGES, EDGE_F), dtype=jnp.float32)
        W = jax.random.normal(ks[3], (IN_C, OUT_C), dtype=jnp.float32) / np.sqrt(IN_C)
        att_src = jax.random.normal(ks[4], (OUT_C,), dtype=jnp.float32) / np.sqrt(OUT_C)
        att_dst = jax.random.normal(ks[5], (OUT_C,), dtype=jnp.float32) / np.sqrt(OUT_C)
        bias = jnp.zeros((OUT_C,), dtype=jnp.float32)
        gamma = jnp.ones((OUT_C,), dtype=jnp.float32)
        beta = jnp.zeros((OUT_C,), dtype=jnp.float32)
        return {'x': x, 'edge_index': edge_index, 'edge_attr': edge_attr, 'W': W, 'att_src': att_src, 'att_dst': att_dst, 'bias': bias, 'gamma': gamma, 'beta': beta}
    _L2_gnn_all = _L2_gnn_setup()
    _L2_gnn_in = {k: v for k, v in _L2_gnn_all.items() if k in ('W', 'att_src', 'att_dst', 'bias', 'gamma', 'beta')}
    del _L2_gnn_all

    def _L3_gnn_setup():
        import jax, jax.numpy as jnp
        import numpy as np
        N, DIM, K = (50000, 128, 9)
        FFN = 4 * DIM
        EPS = 1e-05

        def layer_norm(x, g, b):
            mu = jnp.mean(x, axis=-1, keepdims=True)
            var = jnp.mean(jnp.square(x - mu), axis=-1, keepdims=True)
            return (x - mu) * jax.lax.rsqrt(var + EPS) * g + b
        key = jax.random.key(seed)
        ks = jax.random.split(key, 12)
        E = N * K
        src = jax.random.randint(ks[0], (E,), 0, N)
        dst = jnp.repeat(jnp.arange(N), K)
        edge_index = jnp.stack([src, dst]).astype(jnp.int64)
        s = lambda k, shape, fan_in: jax.random.normal(k, shape, jnp.float32) / np.sqrt(fan_in)
        return {'x': jax.random.normal(ks[1], (N, DIM), jnp.float32), 'edge_index': edge_index, 'W_in_w': s(ks[2], (DIM, DIM), DIM), 'W_in_b': jnp.zeros((DIM,), jnp.float32), 'W_upd_w': s(ks[3], (2 * DIM, DIM), 2 * DIM), 'W_upd_b': jnp.zeros((DIM,), jnp.float32), 'W_out_w': s(ks[4], (DIM, DIM), DIM), 'W_out_b': jnp.zeros((DIM,), jnp.float32), 'ln1_g': jnp.ones((DIM,), jnp.float32), 'ln1_b': jnp.zeros((DIM,), jnp.float32), 'ln2_g': jnp.ones((DIM,), jnp.float32), 'ln2_b': jnp.zeros((DIM,), jnp.float32), 'ffn1_w': s(ks[5], (DIM, FFN), DIM), 'ffn1_b': jnp.zeros((FFN,), jnp.float32), 'ffn2_w': s(ks[6], (FFN, DIM), FFN), 'ffn2_b': jnp.zeros((DIM,), jnp.float32)}
    _L3_gnn_all = _L3_gnn_setup()
    _L3_gnn_in = {k: v for k, v in _L3_gnn_all.items() if k in ('W_in_w', 'W_in_b', 'W_upd_w', 'W_upd_b', 'W_out_w', 'W_out_b', 'ln1_g', 'ln1_b', 'ln2_g', 'ln2_b', 'ffn1_w', 'ffn1_b', 'ffn2_w', 'ffn2_b')}
    del _L3_gnn_all
    return {'x': x, 'src': src, 'dst': dst, 'edge_attr_128': edge_attr_128, 'edge_attr_16': edge_attr_16, 'L0_gnn_W1': _L0_gnn_in['W1'], 'L0_gnn_b1': _L0_gnn_in['b1'], 'L0_gnn_W2': _L0_gnn_in['W2'], 'L0_gnn_b2': _L0_gnn_in['b2'], 'L1_gnn_W1': _L1_gnn_in['W1'], 'L1_gnn_b1': _L1_gnn_in['b1'], 'L1_gnn_W2': _L1_gnn_in['W2'], 'L1_gnn_b2': _L1_gnn_in['b2'], 'L2_gnn_W': _L2_gnn_in['W'], 'L2_gnn_att_src': _L2_gnn_in['att_src'], 'L2_gnn_att_dst': _L2_gnn_in['att_dst'], 'L2_gnn_bias': _L2_gnn_in['bias'], 'L2_gnn_gamma': _L2_gnn_in['gamma'], 'L2_gnn_beta': _L2_gnn_in['beta'], 'L3_gnn_W_in_w': _L3_gnn_in['W_in_w'], 'L3_gnn_W_in_b': _L3_gnn_in['W_in_b'], 'L3_gnn_W_upd_w': _L3_gnn_in['W_upd_w'], 'L3_gnn_W_upd_b': _L3_gnn_in['W_upd_b'], 'L3_gnn_W_out_w': _L3_gnn_in['W_out_w'], 'L3_gnn_W_out_b': _L3_gnn_in['W_out_b'], 'L3_gnn_ln1_g': _L3_gnn_in['ln1_g'], 'L3_gnn_ln1_b': _L3_gnn_in['ln1_b'], 'L3_gnn_ln2_g': _L3_gnn_in['ln2_g'], 'L3_gnn_ln2_b': _L3_gnn_in['ln2_b'], 'L3_gnn_ffn1_w': _L3_gnn_in['ffn1_w'], 'L3_gnn_ffn1_b': _L3_gnn_in['ffn1_b'], 'L3_gnn_ffn2_w': _L3_gnn_in['ffn2_w'], 'L3_gnn_ffn2_b': _L3_gnn_in['ffn2_b']}

def reference(x, src, dst, edge_attr_128, edge_attr_16, L0_gnn_W1, L0_gnn_b1, L0_gnn_W2, L0_gnn_b2, L1_gnn_W1, L1_gnn_b1, L1_gnn_W2, L1_gnn_b2, L2_gnn_W, L2_gnn_att_src, L2_gnn_att_dst, L2_gnn_bias, L2_gnn_gamma, L2_gnn_beta, L3_gnn_W_in_w, L3_gnn_W_in_b, L3_gnn_W_upd_w, L3_gnn_W_upd_b, L3_gnn_W_out_w, L3_gnn_W_out_b, L3_gnn_ln1_g, L3_gnn_ln1_b, L3_gnn_ln2_g, L3_gnn_ln2_b, L3_gnn_ffn1_w, L3_gnn_ffn1_b, L3_gnn_ffn2_w, L3_gnn_ffn2_b):
    import jax
    import jax.numpy as jnp

    def _L0_gnn_ref(x, edge_index, W1, b1, W2, b2):
        import jax, jax.numpy as jnp
        import numpy as np
        N_NODES = 50000
        N_EDGES = 12500
        IN_DIM = 128
        HIDDEN = 256
        OUT_DIM = HIDDEN // 2

        def gcn_conv(x, edge_index, W, b, num_nodes):
            src, dst = (edge_index[0], edge_index[1])
            loops = jnp.arange(num_nodes, dtype=src.dtype)
            src = jnp.concatenate([src, loops])
            dst = jnp.concatenate([dst, loops])
            deg = jax.ops.segment_sum(jnp.ones_like(dst, dtype=x.dtype), dst, num_segments=num_nodes)
            deg_inv_sqrt = jnp.where(deg > 0, jax.lax.rsqrt(jnp.maximum(deg, 1e-12)), 0.0)
            norm = deg_inv_sqrt[src] * deg_inv_sqrt[dst]
            h = x @ W.T
            msgs = norm[:, None] * h[src]
            out = jax.ops.segment_sum(msgs, dst, num_segments=num_nodes)
            return out + b
        h = gcn_conv(x, edge_index, W1, b1, N_NODES)
        h = jax.nn.relu(h)
        return gcn_conv(h, edge_index, W2, b2, N_NODES)

    def _L1_gnn_ref(x, edge_index, edge_attr, W1, b1, W2, b2):
        import jax, jax.numpy as jnp
        import numpy as np
        HIDDEN = 128
        N_NODES = 10000
        N_EDGES = 10000
        EPS = 0.0
        src = edge_index[0]
        dst = edge_index[1]
        msg = jax.nn.relu(x[src] + edge_attr)
        agg = jax.ops.segment_sum(msg, dst, num_segments=x.shape[0])
        h = (1.0 + EPS) * x + agg
        h = jax.nn.relu(h @ W1.T + b1)
        return h @ W2.T + b2

    def _L2_gnn_ref(x, edge_index, edge_attr, W, att_src, att_dst, bias, gamma, beta):
        import jax, jax.numpy as jnp
        import numpy as np
        N_NODES = 50000
        N_EDGES = 12500
        IN_C = 128
        OUT_C = 128
        EDGE_F = 16
        NEG_SLOPE = 0.2
        BN_EPS = 1e-05
        N = x.shape[0]
        h = x @ W
        loops = jnp.broadcast_to(jnp.arange(N, dtype=edge_index.dtype)[None, :], (2, N))
        ei = jnp.concatenate([edge_index, loops], axis=1)
        src, dst = (ei[0], ei[1])
        a_src = h @ att_src
        a_dst = h @ att_dst
        e = jax.nn.leaky_relu(a_src[src] + a_dst[dst], NEG_SLOPE)
        m = jax.ops.segment_max(e, dst, num_segments=N)
        ex = jnp.exp(e - m[dst])
        denom = jax.ops.segment_sum(ex, dst, num_segments=N)
        alpha = ex / denom[dst]
        out = jax.ops.segment_sum(alpha[:, None] * h[src], dst, num_segments=N) + bias
        mean = jnp.mean(out, axis=0)
        var = jnp.mean((out - mean) ** 2, axis=0)
        y = (out - mean) * jax.lax.rsqrt(var + BN_EPS) * gamma + beta
        return jax.nn.relu(y)

    def _L3_gnn_ref(x, edge_index, W_in_w, W_in_b, W_upd_w, W_upd_b, W_out_w, W_out_b, ln1_g, ln1_b, ln2_g, ln2_b, ffn1_w, ffn1_b, ffn2_w, ffn2_b):
        import jax, jax.numpy as jnp
        import numpy as np
        N, DIM, K = (50000, 128, 9)
        FFN = 4 * DIM
        EPS = 1e-05

        def layer_norm(x, g, b):
            mu = jnp.mean(x, axis=-1, keepdims=True)
            var = jnp.mean(jnp.square(x - mu), axis=-1, keepdims=True)
            return (x - mu) * jax.lax.rsqrt(var + EPS) * g + b
        src, dst = (edge_index[0], edge_index[1])
        n = x.shape[0]
        h = x @ W_in_w + W_in_b
        diff = h[src] - h[dst]
        seg_max = jax.ops.segment_max(diff, dst, num_segments=n)
        counts = jax.ops.segment_sum(jnp.ones_like(dst, jnp.int32), dst, num_segments=n)
        max_diff = jnp.where((counts > 0)[:, None], seg_max, 0.0)
        h = jnp.concatenate([h, max_diff], axis=-1) @ W_upd_w + W_upd_b
        h = h @ W_out_w + W_out_b
        x = layer_norm(x + h, ln1_g, ln1_b)
        f = jax.nn.gelu(x @ ffn1_w + ffn1_b, approximate=False) @ ffn2_w + ffn2_b
        return layer_norm(x + f, ln2_g, ln2_b)
    edge_index = jnp.stack([src, dst])
    x = _layernorm(x + _L0_gnn_ref(x, edge_index, L0_gnn_W1, L0_gnn_b1, L0_gnn_W2, L0_gnn_b2), axis=-1)
    x = _layernorm(x + _L1_gnn_ref(x, edge_index, edge_attr_128, L1_gnn_W1, L1_gnn_b1, L1_gnn_W2, L1_gnn_b2), axis=-1)
    x = _layernorm(x + _L2_gnn_ref(x, edge_index, edge_attr_16, L2_gnn_W, L2_gnn_att_src, L2_gnn_att_dst, L2_gnn_bias, L2_gnn_gamma, L2_gnn_beta), axis=-1)
    x = _layernorm(x + _L3_gnn_ref(x, edge_index, L3_gnn_W_in_w, L3_gnn_W_in_b, L3_gnn_W_upd_w, L3_gnn_W_upd_b, L3_gnn_W_out_w, L3_gnn_W_out_b, L3_gnn_ln1_g, L3_gnn_ln1_b, L3_gnn_ln2_g, L3_gnn_ln2_b, L3_gnn_ffn1_w, L3_gnn_ffn1_b, L3_gnn_ffn2_w, L3_gnn_ffn2_b), axis=-1)
    return x

_drawn_inputs = setup_inputs


def setup_inputs(seed=0):
    import zlib

    import numpy as np

    out = dict(_drawn_inputs(seed))
    spreads = {'L2_gnn_bias': (0.0, 0.8),
     'L2_gnn_gamma': (1.0, 0.2),
     'L2_gnn_beta': (0.0, 0.1),
     'L3_gnn_W_in_b': (0.0, 0.1),
     'L3_gnn_W_upd_b': (0.0, 0.1),
     'L3_gnn_W_out_b': (0.0, 0.1),
     'L3_gnn_ln1_g': (1.0, 0.2),
     'L3_gnn_ln1_b': (0.0, 0.1),
     'L3_gnn_ln2_g': (1.0, 0.2),
     'L3_gnn_ln2_b': (0.0, 0.1),
     'L3_gnn_ffn1_b': (0.0, 0.1),
     'L3_gnn_ffn2_b': (0.0, 0.1)}
    factors = {'L0_gnn_b1': 2.994, 'L1_gnn_b1': 3.015}
    for name, (base, spread) in spreads.items():
        noise = np.random.default_rng([zlib.crc32(name.encode()), seed]).standard_normal(out[name].shape)
        drawn = base * np.exp(spread * noise) if base else spread * noise
        out[name] = jnp.asarray(drawn.astype(out[name].dtype))
    for name, factor in factors.items():
        out[name] = (out[name] * factor).astype(out[name].dtype)
    return out
```

```python
from contextlib import ExitStack

import concourse.bass as bass
from concourse import mybir

F32 = mybir.dt.float32
BF16 = mybir.dt.bfloat16
I32 = mybir.dt.int32
ALU = mybir.AluOpType
ACT = mybir.ActivationFunctionType

P = 128
TILES = 4
GROUP = TILES * P
NODES = 50000
EDGES = 12500
GROUPS = -(-NODES // GROUP)
NPAD = GROUPS * GROUP
CHUNKS = -(-EDGES // GROUP)
EPAD = CHUNKS * GROUP
ECOLS = EPAD // P
ROWS = NPAD + EPAD
EPS = 1e-5
SKIP = 1 << 20
BIG = 1.5e38
RSQRT_MAGIC = 0x5F3759DF

MATS = ["L0_W1a", "L0_W1b", "L0_W2a", "L0_W2b", "L1_W1", "L1_W2", "L2_W", "W_in", "W_inT", "W_topT", "W_botT",
        "W_out", "F1a", "F1b", "F1c", "F1d", "F2a", "F2b", "F2c", "F2d"]
VECS = ["L0_b1a", "L0_b1b", "L0_b2", "L1_b1", "L1_b2", "att_src", "att_dst", "bias", "gamma", "beta",
        "b_in", "b_upd", "b_out", "ln1_g", "ln1_b", "ln2_g", "ln2_b", "f1_ba", "f1_bb", "f1_bc", "f1_bd", "f2_b"]


class Item:

    def __init__(self, turn, offset, ring):
        self.turn = turn + offset // ring
        self.slot = offset % ring
        self.n = self.turn * ring + self.slot
        self.ring = ring


class Step:
    def __init__(self, turn, offset, ring, count):
        self.turn, self.offset, self.ring, self.count = turn, offset, ring, count
        self.i = turn * ring + offset

    def item(self, lag):
        it = Item(self.turn, self.offset - lag, self.ring)
        if isinstance(it.n, int) and not 0 <= it.n < self.count:
            return None
        return it


def run_steps(engine, count, lags, ring, step):
    head = -(-(lags + ring) // ring)
    tail = count // ring
    for i in range(head * ring):
        step(Step(i // ring, i % ring, ring, count))
    with engine.Fori(head, tail) as turn:
        for u in range(ring):
            step(Step(turn, u, ring, count))
    for i in range(tail * ring, count + lags):
        step(Step(i // ring, i % ring, ring, count))


def need(engine, sem, item, back=0):
    value = item.n + 1 - back
    if not isinstance(value, int) or value > 0:
        engine.wait_ge(sem, value)


def need_dma(engine, sems, item, back=0, dmas=1):
    value = (item.turn + 1 - back) * (16 * dmas)
    if not isinstance(value, int) or value > 0:
        engine.wait_ge(sems[item.slot], value)


def need_apart(engine, started, sem, item):
    value = item.n + 1
    if not isinstance(value, int):
        value = engine.to_reg(value)
    engine.wait_ge(started, 1)
    engine.wait_ge(sem, value)


class Scope:

    def __init__(self, nc, stack, prefix):
        self.nc, self.stack, self.prefix, self.handles = nc, stack, prefix, []
        stack.callback(self.release)

    def release(self):
        if self.handles:
            self.nc.clear_and_free_semaphores(self.handles)
            self.nc.all_engine_barrier()

    def sb(self, name, shape, dt=F32):
        return self.stack.enter_context(self.nc.sbuf_tensor(f"{self.prefix}_{name}", shape, dt))

    def ring(self, name, depth, shape=(P, GROUP), dt=F32):
        return [self.sb(f"{name}{k}", list(shape), dt) for k in range(depth)]

    def pair(self, name, ring):
        return self.ring(name, 2) * (ring // 2)

    def bank(self, name):
        return self.stack.enter_context(self.nc.psum_tensor(f"{self.prefix}_{name}", [P, GROUP], F32))

    def sem(self, name):
        handle = self.nc.alloc_semaphore(name=f"{self.prefix}_{name}")
        self.handles.append(handle)
        return handle

    def sems(self, name, depth):
        return [self.sem(f"{name}{k}") for k in range(depth)]


def tile(buf, j):
    return buf[:, j * P:(j + 1) * P]


def transpose4(pe, out, in_, ident):
    for j in range(TILES):
        last = pe.transpose(tile(out, j), tile(in_, j), ident)
    return last


def product_nm(pe, out, pairs):
    for j in range(TILES):
        for n, (operand, matrix) in enumerate(pairs):
            last = pe.matmul(tile(out, j), tile(operand, j), matrix, start=(n == 0), stop=(n == len(pairs) - 1))
    return last


class Link:

    def __init__(self, ve, sem, base):
        self.ve, self.sem, self.base, self.n = ve, sem, base, 0

    def __call__(self, instruction):
        self.n += 1
        instruction.then_inc(self.sem, 1)
        self.ve.wait_ge(self.sem, self.base + self.n)


RSQRT_LINKS = 2 + 3 * 3


def rsqrt(ve, link, y, v, half, t):
    link(ve.tensor_scalar(y.bitcast(I32), v.bitcast(I32), 1, None, ALU.logical_shift_right))
    link(ve.tensor_scalar(y.bitcast(I32), y.bitcast(I32), -1.0, float(RSQRT_MAGIC), ALU.mult, ALU.add))
    for _ in range(3):
        link(ve.tensor_tensor(t, y, y, ALU.mult))
        link(ve.tensor_tensor(t, t, half, ALU.mult))
        link(ve.scalar_tensor_tensor(out=y, in0=t, scalar=1.5, in1=y, op0=ALU.add, op1=ALU.mult))


NORM_LINKS = 8 + RSQRT_LINKS + 1


class Norms:

    def __init__(self, scope, count, ring, last):
        cols = count * TILES
        self.last = last
        self.cols, self.ring_n = cols, ring
        self.stats = scope.sb("stats", [P, cols, 6])
        self.work = scope.sb("norm_work", [P, 4, cols])
        self.result = scope.ring("norm_result", ring, (P, 3, cols))
        self.sem = scope.sem("norm_link")
        self.init = scope.sem("norm_init")

    def prepare(self, ve):
        ve.memset(self.stats[:, :, :], 1.0).then_inc(self.init, 1)
        ve.wait_ge(self.init, 1)

    def take(self, ve, which, buf):
        for j in range(TILES):
            last = ve.bn_stats(self.stats[:, which * TILES + j, :], tile(buf, j))
        return last

    def finish(self, ve, step, measured):
        if isinstance(step.i, int) and step.i > self.last:
            return
        for sem, item in measured:
            need(ve, sem, item)
        link = Link(ve, self.sem, step.i * NORM_LINKS)
        s = self.stats
        t, v, half, d = (self.work[:, k, :] for k in range(4))
        mean, rstd, shift = (self.result[step.offset % self.ring_n][:, k, :] for k in range(3))
        link(ve.tensor_tensor(mean, s[:, :, 1], s[:, :, 4], ALU.add))
        link(ve.tensor_tensor(d, s[:, :, 1], s[:, :, 4], ALU.subtract))
        link(ve.tensor_tensor(v, s[:, :, 2], s[:, :, 5], ALU.add))
        link(ve.tensor_tensor(d, d, d, ALU.mult))
        link(ve.scalar_tensor_tensor(out=v, in0=d, scalar=P / 4.0, in1=v, op0=ALU.mult, op1=ALU.add))
        link(ve.tensor_scalar(v, v, 1.0 / P, EPS, ALU.mult, ALU.add))
        link(ve.tensor_scalar(half, v, -0.5, None, ALU.mult))
        link(ve.tensor_scalar(mean, mean, 0.5, None, ALU.mult))
        rsqrt(ve, link, rstd, v, half, t)
        link(ve.scalar_tensor_tensor(out=shift, in0=mean, scalar=-1.0, in1=rstd, op0=ALU.mult, op1=ALU.mult))

    def ready(self, engine, step):
        done = min(step.i, self.last + 1) if isinstance(step.i, int) else step.i
        engine.wait_ge(self.sem, done * NORM_LINKS)

    def columns(self, step, which, j):
        r = self.result[(step.offset - 1) % self.ring_n]
        c = which * TILES + j
        return [r[:, k, c:c + 1] for k in range(3)]

    def apply_vector(self, ve, step, which, out, in_):
        for j in range(TILES):
            mean, rstd, _ = self.columns(step, which, j)
            last = ve.tensor_scalar(tile(out, j), tile(in_, j), mean, rstd, ALU.subtract, ALU.mult)
        return last

    def apply_scalar(self, act, step, which, out, in_):
        for j in range(TILES):
            _, rstd, shift = self.columns(step, which, j)
            last = act.activation(tile(out, j), tile(in_, j), ACT.Identity, bias=shift, scale=rstd)
        return last


class Shared:
    pass


def node_rows(table, item):
    return table[bass.ds(item.n * GROUP, GROUP), :].rearrange("(p j) d -> p j d", j=TILES)


def edge_rows(table, item, first=NPAD):
    return table[bass.ds(item.n * GROUP + first, GROUP), :].rearrange("(j p) d -> p j d", p=P)


def as_tiles(buf):
    return buf[:, :].rearrange("p (j d) -> p j d", j=TILES)


def wide(buf, half):
    return buf[:, :, half * P:(half + 1) * P]


def setup_phase(nc, sh, dram):
    with ExitStack() as stack:
        s = Scope(nc, stack, "set")
        dst_bc = s.sb("dst_bc", [P, EPAD], I32)
        count_bc = s.sb("count_bc", [P, EPAD])
        next_cols = s.sb("next_cols", [P, ECOLS], I32)
        map_init = s.sb("map_init", [P, NPAD // P, 2])
        node_ids = s.sb("node_ids", [P, NPAD // P], I32)
        slot_ids = s.sb("slot_ids", [P, ECOLS], I32)
        counts = s.sb("counts", [P, ECOLS])
        skip = s.sb("skip", [P, ECOLS])
        ones_row = s.sb("ones_row", [P, 1])
        banks = [s.bank(f"fold{k}") for k in range(5)]
        top_out = s.sb("top_out", [P, P])
        loaded, ids, built, init_stored = s.sem("loaded"), s.sem("ids"), s.sem("built"), s.sem("init_stored")
        count_stored, counts_back = s.sem("count_stored"), s.sem("counts_back")
        ident_done, folded, fold_read = s.sem("ident_done"), s.sem("folded"), s.sem("fold_read")
        mat, vcol, vrow = sh.mat, sh.vcol, sh.vrow
        with nc.Block() as block:

            @block.sync
            def _(sp):
                sp.sem_inc(sh.started, 1)
                sp.dma_start(dst_bc[:, :], dram.dst_row.to_broadcast([P, EPAD])).then_inc(loaded, 16)
                sp.dma_start(next_cols[:, :], dram.next_cols).then_inc(loaded, 16)
                sp.dma_start(sh.src_cols[:, :], dram.src_cols).then_inc(loaded, 16)
                sp.dma_start(sh.dst_cols[:, :], dram.dst_cols).then_inc(loaded, 16)
                sp.dma_start(sh.mats[:, :], dram.mats).then_inc(loaded, 16)
                sp.dma_start(sh.vcols[:, :], dram.vcols).then_inc(loaded, 16)
                sp.dma_start(sh.vrows[:, :], dram.vrows.to_broadcast([P, len(VECS) * P])).then_inc(loaded, 16)
                sp.wait_ge(built, 1)
                sp.dma_start(dram.map[0:NPAD, :].rearrange("(p c) t -> p (c t)", p=P),
                             map_init[:, :, :].rearrange("p c t -> p (c t)")).then_inc(init_stored, 16)
                sp.wait_ge(built, 2)
                sp.dma_start(dram.count_row, count_bc[0:1, :]).then_inc(count_stored, 16)
                sp.wait_ge(count_stored, 16)
                with nc.allow_non_contiguous_dma(reason="12800 counts, once"):
                    sp.dma_start(counts[:, :], dram.count_row.rearrange("a (c p) -> p (a c)", p=P))\
                      .then_inc(counts_back, 16)
                sp.wait_ge(init_stored, 16)

            @block.gpsimd
            def _(pool):
                pool.iota(node_ids[:, :], pattern=[[1, NPAD // P]], base=0, channel_multiplier=NPAD // P)\
                    .then_inc(ids, 1)
                pool.iota(slot_ids[:, :], pattern=[[P, ECOLS]], base=NPAD, channel_multiplier=1).then_inc(ids, 1)
                pool.memset(sh.ident[:, :], 0.0).then_inc(ident_done, 1)
                pool.wait_ge(ident_done, 1)
                pool.affine_select(out=sh.ident[:, :], in_=sh.ident[:, :], compare_op=ALU.not_equal, fill=1.0,
                                   base=0, pattern=[[-1, P]], channel_multiplier=1).then_inc(ident_done, 1)

            @block.vector
            def _(ve):
                link = Link(ve, s.sem("link"), 0)
                ve.wait_ge(ids, 2)
                link(ve.memset(map_init[:, :, 1], 1.0))
                link(ve.tensor_copy(map_init[:, :, 0], node_ids[:, :]))
                ve.nop().then_inc(built, 1)
                link(ve.memset(ones_row[:, :], 1.0))
                link(ve.memset(sh.same[:, 0:1], 0.0))
                ve.wait_ge(loaded, 16 * 7)
                link(ve.tensor_tensor(sh.same[:, 1:EPAD], dst_bc[:, 1:EPAD], dst_bc[:, 0:EPAD - 1], ALU.is_equal))
                link(ve.tensor_tensor_scan(count_bc[:, :], sh.same[:, :], ones_row[:, 0:1].to_broadcast([P, EPAD]),
                                           0.0, ALU.mult, ALU.add))
                ve.nop().then_inc(built, 1)
                link(ve.tensor_tensor(sh.is_rep[:, :], sh.dst_cols[:, :], next_cols[:, :], ALU.not_equal))
                link(ve.tensor_scalar(skip[:, :], sh.is_rep[:, :], -float(SKIP), float(SKIP), ALU.mult, ALU.add))
                link(ve.tensor_tensor(sh.rep_rows[:, :], sh.dst_cols[:, :], skip[:, :], ALU.add))
                ve.wait_ge(counts_back, 16)
                link(ve.tensor_scalar(sh.map_rows[:, :, 1], counts[:, :], 1.0, None, ALU.add))
                link(ve.tensor_copy(sh.map_rows[:, :, 0], slot_ids[:, :]))
                link(ve.tensor_tensor(sh.ln1_b_f2[:, :], vrow["ln1_b"], vrow["f2_b"], ALU.add))
                link(ve.tensor_tensor(sh.att_both[:, 2, :], vcol["att_src"].to_broadcast([P, P]),
                                      vcol["att_dst"].to_broadcast([P, P]), ALU.add))
                link(ve.tensor_copy(sh.att_both[:, 0, :], vcol["att_src"].to_broadcast([P, P])))
                link(ve.tensor_copy(sh.att_both[:, 1, :], vcol["att_dst"].to_broadcast([P, P])))
                for k, (out, bank) in enumerate(zip([top_out, sh.fold_bot], banks)):
                    ve.wait_ge(folded, k + 1)
                    link(ve.tensor_copy(out[:, :], tile(bank, 0)))
                ve.nop().then_inc(fold_read, 1)
                link(ve.tensor_copy(sh.bc_cols[:, 0, :], vcol["b_in"].to_broadcast([P, P])))
                link(ve.tensor_copy(sh.bc_cols[:, 1, :], vcol["b_upd"].to_broadcast([P, P])))
                ve.nop().then_inc(fold_read, 1)
                ve.wait_ge(folded, 3)
                link(ve.tensor_tensor(sh.fold_self[:, :], tile(banks[2], 0), sh.ident[:, :], ALU.add))
                ve.wait_ge(folded, 4)
                link(ve.tensor_tensor(sh.fold_bias[:, :], tile(banks[3], 0), vrow["b_out"], ALU.add))

            @block.tensor
            def _(pe):
                pe.wait_ge(loaded, 16 * 7)
                pe.matmul(tile(banks[0], 0), mat["W_topT"], mat["W_out"], start=True, stop=True).then_inc(folded, 1)
                pe.matmul(tile(banks[1], 0), mat["W_botT"], mat["W_out"], start=True, stop=True).then_inc(folded, 1)
                pe.wait_ge(fold_read, 1)
                pe.wait_ge(ident_done, 2)
                pe.matmul(tile(banks[2], 0), mat["W_inT"], top_out[:, :], start=True, stop=True).then_inc(folded, 1)
                pe.wait_ge(fold_read, 2)
                pe.matmul(tile(banks[3], 0), sh.bc_cols[:, 0, :], top_out[:, :], start=True, stop=False)
                pe.matmul(tile(banks[3], 0), sh.bc_cols[:, 1, :], mat["W_out"], start=False, stop=True)\
                  .then_inc(folded, 1)


def map_phase(nc, sh, dram):
    with ExitStack() as stack:
        s = Scope(nc, stack, "map")
        R = 4
        idx = s.ring("idx", R, (P, TILES), I32)
        rows = s.ring("rows", R, (P, TILES, 2))
        copied, scattered = s.sem("copied"), s.sems("scattered", R)
        with nc.Block() as block:

            @block.gpsimd
            def _(pool):
                def scatter(step):
                    it = step.item(0)
                    need_dma(pool, scattered, it, 1, TILES)
                    cols = bass.ds(it.n * TILES, TILES)
                    pool.tensor_copy(idx[it.slot][:, :], sh.rep_rows[:, cols])
                    pool.tensor_copy(rows[it.slot][:, :, :], sh.map_rows[:, cols, :]).then_inc(copied, 1)
                    need_apart(pool, sh.started, copied, it)
                    for j in range(TILES):
                        pool.indirect_dma_start(dram.map, bass.IndirectOffsetOnAxis(ap=idx[it.slot][:, j:j + 1], axis=0),
                                                rows[it.slot][:, j, :], None, bounds_check=NPAD - 1,
                                                oob_is_err=False).then_inc(scattered[it.slot], 16)

                run_steps(pool, CHUNKS, 0, R, scatter)
                for k in range(R):
                    pool.wait_ge(scattered[k], 16 * TILES * len(range(k, CHUNKS, R)))

    with ExitStack() as stack:
        s = Scope(nc, stack, "look")
        R = 2
        ends = (("src", sh.src_cols, sh.src_map), ("dst", sh.dst_cols, sh.dst_map))
        idx = {e: s.ring(f"idx_{e}", R, (P, TILES), I32) for e, _, _ in ends}
        got = {e: s.ring(f"got_{e}", R, (P, TILES, 2)) for e, _, _ in ends}
        idx_copied, gathered, kept = s.sem("idx_copied"), s.sems("gathered", R), s.sem("kept")
        done = s.sem("done")
        with nc.Block() as block:

            @block.gpsimd
            def _(pool):
                def lookup(step):
                    it = step.item(0)
                    need(pool, kept, it, R)
                    cols = bass.ds(it.n * TILES, TILES)
                    for e, all_cols, _ in ends:
                        last = pool.tensor_copy(idx[e][it.slot][:, :], all_cols[:, cols])
                    last.then_inc(idx_copied, 1)
                    need_apart(pool, sh.started, idx_copied, it)
                    for e, _, _ in ends:
                        for j in range(TILES):
                            pool.indirect_dma_start(got[e][it.slot][:, j, :], None, dram.map,
                                                    bass.IndirectOffsetOnAxis(ap=idx[e][it.slot][:, j:j + 1], axis=0))\
                                .then_inc(gathered[it.slot], 16)

                run_steps(pool, CHUNKS, 0, R, lookup)
                pool.wait_ge(done, 17)
                last = sh.alone[:, (GROUPS - 1) * TILES:GROUPS * TILES]
                pool.affine_select(out=last, in_=last, compare_op=ALU.is_gt, fill=0.0,
                                   base=NODES - (GROUPS - 1) * GROUP, pattern=[[-1, TILES]],
                                   channel_multiplier=-TILES).then_inc(done, 1)
                pool.wait_ge(done, 18)

            @block.vector
            def _(ve):
                def keep(step):
                    it = step.item(0)
                    need_dma(ve, gathered, it, 0, 2 * TILES)
                    cols = bass.ds(it.n * TILES, TILES)
                    for e, _, out in ends:
                        last = ve.tensor_copy(out[:, cols, :], got[e][it.slot][:, :, :])
                    last.then_inc(kept, 1)

                run_steps(ve, CHUNKS, 0, R, keep)
                ve.wait_ge(kept, CHUNKS)
                link = Link(ve, s.sem("link"), 0)
                v, half, t = (s.sb(n, [P, ECOLS]) for n in ("v", "half", "t"))
                for (_, _, m), row, root in zip(ends, (sh.src_row, sh.dst_row), (sh.src_root, sh.dst_root)):
                    link(ve.tensor_copy(row[:, :], m[:, :, 0]))
                    link(ve.tensor_copy(v[:, :], m[:, :, 1]))
                    link(ve.tensor_scalar(half[:, :], v[:, :], -0.5, None, ALU.mult))
                    rsqrt(ve, link, root[:, :], v[:, :], half[:, :], t[:, :])

            @block.sync
            def _(sp):
                deg = s.sb("deg", [P, GROUPS, TILES, 2])
                sp.dma_start(deg[:, :, :, :], dram.map[0:NPAD, :].rearrange("(g p j) t -> p g (j t)", p=P, j=TILES)
                             .rearrange("p g (j t) -> p g j t", j=TILES)).then_inc(done, 16)
                sh.deg_loaded = deg
                sp.wait_ge(done, 16)

            @block.scalar
            def _(act):
                act.wait_ge(done, 16)
                act.activation(sh.alone[:, :].rearrange("p (g j) -> p g j", j=TILES), sh.deg_loaded[:, :, :, 1], ACT.Relu, bias=sh.two[:, :], scale=-1.0)\
                   .then_inc(done, 1)
                act.wait_ge(done, 17)



def dense_front_phase(nc, sh, dram):
    with ExitStack() as stack:
        s = Scope(nc, stack, "fr")
        R, LAGS = 4, 6
        mat, vcol, vrow = sh.mat, sh.vcol, sh.vrow
        b2_4, l1b2_4 = sh.b2_4, sh.l1b2_4
        xin, pre1, h2, x1, pre2 = (s.ring(n, R) for n in ("xin", "pre1", "h2", "x1", "pre2"))
        xb, xT, r1a, r1b, x1b, x1T, r3, x2T, sq = (s.pair(n, R) for n in ("xb", "xT", "r1a", "r1b", "x1b", "x1T", "r3",
                                                                          "x2T", "sq"))
        x2h = s.ring("x2h", R, (P, TILES, 2 * P))
        norms = Norms(s, 2, R, GROUPS - 1 + 4)
        bT, bMa, bMb, bC, bD, bE, bF, bH = (s.bank(n) for n in ("T", "Ma", "Mb", "C", "D", "E", "F", "H"))
        x_loaded, h2_stored, x1_stored, x2h_stored = (s.sems(n, R) for n in ("xld", "h2st", "x1st", "x2hst"))
        names = ["x_T", "xT_out", "xb_done", "mm1", "relu1", "mm2", "h2_out", "pre1_done", "meas1", "x1_done", "x1_T",
                 "x1T_out", "x1b_done", "mm3", "relu3", "mm4", "pre2_done", "meas2", "x2_done", "x2_T", "x2T_out",
                 "mmh", "h_out", "sq_out", "summed"]
        q = {n: s.sem(n) for n in names}
        with nc.Block() as block:

            @block.sync
            def _(sp):
                def step(st):
                    if it := st.item(0):
                        need(sp, q["x_T"], it, R)
                        need(sp, q["xb_done"], it, R)
                        sp.dma_start(as_tiles(xin[it.slot]), node_rows(dram.x, it)).then_inc(x_loaded[it.slot], 16)
                    if it := st.item(2):
                        need(sp, q["h2_out"], it)
                        sp.dma_start(node_rows(dram.h2, it), as_tiles(h2[it.slot])).then_inc(h2_stored[it.slot], 16)
                    if it := st.item(3):
                        need(sp, q["x1_done"], it)
                        sp.dma_start(node_rows(dram.x1, it), as_tiles(x1[it.slot])).then_inc(x1_stored[it.slot], 16)
                    if it := st.item(5):
                        need(sp, q["x2_done"], it)
                        need(sp, q["h_out"], it)
                        sp.dma_start(node_rows(dram.x2h, it), x2h[it.slot][:, :, :]).then_inc(x2h_stored[it.slot], 16)

                run_steps(sp, GROUPS, LAGS, R, step)
                for sems in (h2_stored, x1_stored, x2h_stored):
                    for k in range(R):
                        sp.wait_ge(sems[k], 16 * len(range(k, GROUPS, R)))

            @block.gpsimd
            def _(pool):
                def step(st):
                    if it := st.item(1):
                        need_dma(pool, x_loaded, it)
                        need(pool, q["pre1_done"], it, 2)
                        pool.tensor_tensor(xb[it.slot][:, :], xin[it.slot][:, :], b2_4[:, :], ALU.add)\
                            .then_inc(q["xb_done"], 1)
                    if it := st.item(3):
                        need(pool, q["x1_done"], it)
                        need(pool, q["pre2_done"], it, 2)
                        pool.tensor_tensor(x1b[it.slot][:, :], x1[it.slot][:, :], l1b2_4[:, :], ALU.add)\
                            .then_inc(q["x1b_done"], 1)

                run_steps(pool, GROUPS, LAGS, R, step)

            @block.tensor
            def _(pe):
                def step(st):
                    if it := st.item(1):
                        need_dma(pe, x_loaded, it)
                        if old := st.item(6):
                            need(pe, q["x2T_out"], old)
                        transpose4(pe, bT, xin[it.slot], sh.ident[:, :]).then_inc(q["x_T"], 1)
                    if it := st.item(2):
                        need(pe, q["relu1"], it)
                        need(pe, q["h2_out"], it, 1)
                        product_nm(pe, bC, [(r1a[it.slot], mat["L0_W2a"]), (r1b[it.slot], mat["L0_W2b"])])\
                            .then_inc(q["mm2"], 1)
                    if it := st.item(3):
                        need(pe, q["x1_done"], it)
                        need(pe, q["x1T_out"], it, 1)
                        transpose4(pe, bD, x1[it.slot], sh.ident[:, :]).then_inc(q["x1_T"], 1)
                    if it := st.item(1):
                        need(pe, q["xT_out"], it)
                        need(pe, q["relu1"], it, 1)
                        pe.matmul(bMa[:, :], mat["L0_W1a"], xT[it.slot][:, :], start=True, stop=True)
                        pe.matmul(bMb[:, :], mat["L0_W1b"], xT[it.slot][:, :], start=True, stop=True)\
                          .then_inc(q["mm1"], 1)
                    if it := st.item(4):
                        need(pe, q["relu3"], it)
                        need(pe, q["pre2_done"], it, 1)
                        product_nm(pe, bF, [(r3[it.slot], mat["L1_W2"])]).then_inc(q["mm4"], 1)
                    if it := st.item(3):
                        need(pe, q["x1T_out"], it)
                        need(pe, q["relu3"], it, 1)
                        pe.matmul(bE[:, :], mat["L1_W1"], x1T[it.slot][:, :], start=True, stop=True)\
                          .then_inc(q["mm3"], 1)
                    if it := st.item(5):
                        need(pe, q["x2_done"], it)
                        if new := st.item(1):
                            need(pe, q["xT_out"], new)
                        for j in range(TILES):
                            last = pe.transpose(tile(bT, j), wide(x2h[it.slot], 0)[:, j, :], sh.ident[:, :])
                        last.then_inc(q["x2_T"], 1)
                        need(pe, q["x2T_out"], it)
                        need(pe, q["sq_out"], it, 1)
                        product_nm(pe, bH, [(x2T[it.slot], mat["L2_W"])]).then_inc(q["mmh"], 1)

                run_steps(pe, GROUPS, LAGS, R, step)

            @block.scalar
            def _(act):
                def step(st):
                    if it := st.item(5):
                        norms.ready(act, st)
                        need_dma(act, x2h_stored, it, 1)
                        for j in range(TILES):
                            _, rstd, shift = norms.columns(st, 1, j)
                            last = act.activation(wide(x2h[it.slot], 0)[:, j, :], tile(pre2[it.slot], j), ACT.Identity,
                                                  bias=shift, scale=rstd)
                        last.then_inc(q["x2_done"], 1)
                    if it := st.item(2):
                        need(act, q["mm2"], it)
                        need_dma(act, h2_stored, it, 1)
                        need(act, q["pre1_done"], it, R)
                        act.activation(h2[it.slot][:, :], bC[:, :], ACT.Copy).then_inc(q["h2_out"], 1)
                    if it := st.item(3):
                        need(act, q["x1_T"], it)
                        need(act, q["mm3"], it, 2)
                        act.activation(x1T[it.slot][:, :], bD[:, :], ACT.Copy).then_inc(q["x1T_out"], 1)
                    if it := st.item(1):
                        need(act, q["mm1"], it)
                        need(act, q["mm2"], it, 2)
                        act.activation(r1a[it.slot][:, :], bMa[:, :], ACT.Relu, bias=vcol["L0_b1a"])
                        act.activation(r1b[it.slot][:, :], bMb[:, :], ACT.Relu, bias=vcol["L0_b1b"])\
                           .then_inc(q["relu1"], 1)
                    if it := st.item(3):
                        need(act, q["mm3"], it)
                        need(act, q["mm4"], it, 2)
                        act.activation(r3[it.slot][:, :], bE[:, :], ACT.Relu, bias=vcol["L1_b1"])\
                           .then_inc(q["relu3"], 1)
                    if it := st.item(5):
                        need(act, q["x2_T"], it)
                        need(act, q["mmh"], it, 2)
                        act.activation(x2T[it.slot][:, :], bT[:, :], ACT.Copy).then_inc(q["x2T_out"], 1)
                        need(act, q["mmh"], it)
                        need(act, q["summed"], it, 2)
                        act.activation(wide(x2h[it.slot], 1), as_tiles(bH), ACT.Copy).then_inc(q["h_out"], 1)
                        act.activation(sq[it.slot][:, :], bH[:, :], ACT.Square).then_inc(q["sq_out"], 1)

                run_steps(act, GROUPS, LAGS, R, step)

            @block.vector
            def _(ve):
                norms.prepare(ve)

                def step(st):
                    measured = []
                    norms.ready(ve, st) if not (isinstance(st.i, int) and st.i == 0) else None
                    if it := st.item(3):
                        need_dma(ve, x1_stored, it, 1)
                        need(ve, q["x1_T"], it, R)
                        need(ve, q["x1b_done"], it, R)
                        norms.apply_vector(ve, st, 0, x1[it.slot], pre1[it.slot]).then_inc(q["x1_done"], 1)
                    if it := st.item(1):
                        need(ve, q["x_T"], it)
                        need(ve, q["mm1"], it, 2)
                        ve.tensor_copy(xT[it.slot][:, :], bT[:, :]).then_inc(q["xT_out"], 1)
                    if it := st.item(2):
                        need(ve, q["h2_out"], it)
                        need(ve, q["xb_done"], it)
                        ve.tensor_tensor(pre1[it.slot][:, :], h2[it.slot][:, :], xb[it.slot][:, :], ALU.add)\
                          .then_inc(q["pre1_done"], 1)
                        need(ve, q["pre1_done"], it)
                        norms.take(ve, 0, pre1[it.slot]).then_inc(q["meas1"], 1)
                        measured.append((q["meas1"], it))
                    if it := st.item(4):
                        need(ve, q["mm4"], it)
                        need(ve, q["x1b_done"], it)
                        need(ve, q["x2_done"], it, R)
                        ve.tensor_tensor(pre2[it.slot][:, :], bF[:, :], x1b[it.slot][:, :], ALU.add)\
                          .then_inc(q["pre2_done"], 1)
                        need(ve, q["pre2_done"], it)
                        norms.take(ve, 1, pre2[it.slot]).then_inc(q["meas2"], 1)
                        measured.append((q["meas2"], it))
                    if it := st.item(6):
                        need(ve, q["h_out"], it)
                        need(ve, q["sq_out"], it)
                        need(ve, q["summed"], it, 1)
                        for j in range(TILES):
                            alone = sh.alone[:, bass.ds(it.n * TILES + j, 1)]
                            ve.scalar_tensor_tensor(out=sh.sum1[:, j, :], in0=wide(x2h[it.slot], 1)[:, j, :],
                                                    scalar=alone, in1=sh.sum1[:, j, :], op0=ALU.mult, op1=ALU.add)
                            last = ve.scalar_tensor_tensor(out=sh.sum2[:, j, :], in0=tile(sq[it.slot], j),
                                                           scalar=alone, in1=sh.sum2[:, j, :], op0=ALU.mult,
                                                           op1=ALU.add)
                        last.then_inc(q["summed"], 1)
                    norms.finish(ve, st, measured)

                run_steps(ve, GROUPS, LAGS, R, step)


class Gathers:

    def __init__(self, scope, started, name, table, columns, width, ring):
        self.table, self.columns, self.ring, self.started = table, columns, ring, started
        self.idx = scope.ring(f"{name}_idx", ring, (P, TILES), I32)
        self.rows = scope.ring(f"{name}_rows", ring, (P, TILES, width))
        self.copied = scope.sem(f"{name}_copied")
        self.landed = scope.sems(f"{name}_landed", ring)

    def issue(self, pool, it):
        pool.tensor_copy(self.idx[it.slot][:, :], self.columns[:, bass.ds(it.n * TILES, TILES)])\
            .then_inc(self.copied, 1)
        need_apart(pool, self.started, self.copied, it)
        for j in range(TILES):
            pool.indirect_dma_start(self.rows[it.slot][:, j, :], None, self.table,
                                    bass.IndirectOffsetOnAxis(ap=self.idx[it.slot][:, j:j + 1], axis=0))\
                .then_inc(self.landed[it.slot], 16)

    def wait(self, engine, it, back=0):
        need_dma(engine, self.landed, it, back, TILES)


def flat(rows):
    return rows[:, :, :].rearrange("p j d -> p (j d)")


def segment_sum(ve, it, sums, same, values):
    start = 0.0
    if not (isinstance(it.n, int) and it.n == 0):
        start = sums[(it.slot - 1) % len(sums)][:, GROUP - 1:GROUP]
    return ve.tensor_tensor_scan(sums[it.slot][:, :], same, values, start, ALU.mult, ALU.add)


def column(cols, it, j):
    return cols[:, bass.ds(it.n * TILES + j, 1)]


def edge_gcn1_phase(nc, sh, dram):
    with ExitStack() as stack:
        s = Scope(nc, stack, "e1")
        R, LAGS = 2, 2
        mat, vcol = sh.mat, sh.vcol
        src, dst = Gathers(s, sh.started, "src", dram.x, sh.src_cols, P, R), Gathers(s, sh.started, "dst", dram.x, sh.dst_cols, P, R)
        sums, v, u, uT, r1a, r1b, h2s, xob = (s.ring(n, R) for n in ("sums", "v", "u", "uT", "r1a", "r1b", "h2s", "xob"))
        bS, bA, bU, bMa, bMb, bH = (s.bank(n) for n in ("S", "A", "U", "Ma", "Mb", "H"))
        h2_stored, xob_stored = s.sems("h2st", R), s.sems("xobst", R)
        q = {n: s.sem(n) for n in ["scaled", "src_T", "summed", "sum_T", "v_done", "u_done", "u_T", "uT_out", "mm1",
                                   "relu1", "mm2", "h2_out", "xob_done"]}
        with nc.Block() as block:

            @block.gpsimd
            def _(pool):
                def step(st):
                    if it := st.item(0):
                        need(pool, q["src_T"], it, R)
                        src.issue(pool, it)
                        need(pool, q["v_done"], it, R)
                        need(pool, q["xob_done"], it, R)
                        dst.issue(pool, it)

                run_steps(pool, CHUNKS, LAGS, R, step)

            @block.vector
            def _(ve):
                def step(st):
                    if it := st.item(1):
                        src.wait(ve, it)
                        g = src.rows[it.slot]
                        for j in range(TILES):
                            last = ve.tensor_scalar(g[:, j, :], g[:, j, :], column(sh.src_root, it, j), None, ALU.mult)
                        last.then_inc(q["scaled"], 1)
                        dst.wait(ve, it)
                        need_dma(ve, xob_stored, it, 1)
                        ve.tensor_tensor(xob[it.slot][:, :], flat(dst.rows[it.slot]), sh.b2_4[:, :], ALU.add)\
                          .then_inc(q["xob_done"], 1)
                        need(ve, q["src_T"], it)
                        need(ve, q["sum_T"], it, R)
                        need(ve, q["summed"], it, 1)
                        segment_sum(ve, it, sums, sh.same[:, bass.ds(it.n * GROUP, GROUP)], bS[:, :])\
                            .then_inc(q["summed"], 1)
                        need(ve, q["sum_T"], it)
                        need(ve, q["u_done"], it, R)
                        for j in range(TILES):
                            last = ve.scalar_tensor_tensor(out=tile(v[it.slot], j), in0=dst.rows[it.slot][:, j, :],
                                                           scalar=column(sh.dst_root, it, j), in1=tile(bA, j),
                                                           op0=ALU.mult, op1=ALU.add)
                        last.then_inc(q["v_done"], 1)

                run_steps(ve, CHUNKS, LAGS, R, step)

            @block.scalar
            def _(act):
                def step(st):
                    if it := st.item(2):
                        need(act, q["u_T"], it)
                        need(act, q["mm1"], it, R)
                        act.activation(uT[it.slot][:, :], bU[:, :], ACT.Copy).then_inc(q["uT_out"], 1)
                        need(act, q["mm1"], it)
                        need(act, q["mm2"], it, R)
                        act.activation(r1a[it.slot][:, :], bMa[:, :], ACT.Relu, bias=vcol["L0_b1a"])
                        act.activation(r1b[it.slot][:, :], bMb[:, :], ACT.Relu, bias=vcol["L0_b1b"])\
                           .then_inc(q["relu1"], 1)
                        act.wait_ge(sh.started, 1)
                        need(act, q["mm2"], it)
                        need_dma(act, h2_stored, it, 1)
                        for j in range(TILES):
                            last = act.activation(tile(h2s[it.slot], j), tile(bH, j), ACT.Copy,
                                                  scale=column(sh.dst_root, it, j))
                        last.then_inc(q["h2_out"], 1)
                    if it := st.item(1):
                        act.wait_ge(sh.started, 1)
                        need(act, q["v_done"], it)
                        need(act, q["u_T"], it, R)
                        for j in range(TILES):
                            last = act.activation(tile(u[it.slot], j), tile(v[it.slot], j), ACT.Copy,
                                                  scale=column(sh.dst_root, it, j))
                        last.then_inc(q["u_done"], 1)

                run_steps(act, CHUNKS, LAGS, R, step)

            @block.tensor
            def _(pe):
                def step(st):
                    if it := st.item(1):
                        need(pe, q["scaled"], it)
                        need(pe, q["summed"], it, 1)
                        transpose4(pe, bS, flat(src.rows[it.slot]), sh.ident[:, :]).then_inc(q["src_T"], 1)
                    if it := st.item(2):
                        need(pe, q["u_done"], it)
                        need(pe, q["uT_out"], it, 1)
                        transpose4(pe, bU, u[it.slot], sh.ident[:, :]).then_inc(q["u_T"], 1)
                        need(pe, q["uT_out"], it)
                        need(pe, q["relu1"], it, 1)
                        pe.matmul(bMa[:, :], mat["L0_W1a"], uT[it.slot][:, :], start=True, stop=True)
                        pe.matmul(bMb[:, :], mat["L0_W1b"], uT[it.slot][:, :], start=True, stop=True)\
                          .then_inc(q["mm1"], 1)
                    if it := st.item(1):
                        need(pe, q["summed"], it)
                        need(pe, q["v_done"], it, 1)
                        transpose4(pe, bA, sums[it.slot], sh.ident[:, :]).then_inc(q["sum_T"], 1)
                    if it := st.item(2):
                        need(pe, q["relu1"], it)
                        need(pe, q["h2_out"], it, 1)
                        product_nm(pe, bH, [(r1a[it.slot], mat["L0_W2a"]), (r1b[it.slot], mat["L0_W2b"])])\
                            .then_inc(q["mm2"], 1)

                run_steps(pe, CHUNKS, LAGS, R, step)

            @block.sync
            def _(sp):
                def step(st):
                    if it := st.item(1):
                        need(sp, q["xob_done"], it)
                        sp.dma_start(edge_rows(dram.x_own, it, 0), as_tiles(xob[it.slot])).then_inc(xob_stored[it.slot], 16)
                    if it := st.item(2):
                        need(sp, q["h2_out"], it)
                        sp.dma_start(edge_rows(dram.h2, it), as_tiles(h2s[it.slot])).then_inc(h2_stored[it.slot], 16)

                run_steps(sp, CHUNKS, LAGS, R, step)
                for sems in (xob_stored, h2_stored):
                    for k in range(R):
                        sp.wait_ge(sems[k], 16 * len(range(k, CHUNKS, R)))


def edge_gcn2_phase(nc, sh, dram):
    with ExitStack() as stack:
        s = Scope(nc, stack, "e2")
        R, LAGS = 2, 3
        src = Gathers(s, sh.started, "src", dram.h2, sh.src_row, P, R)
        sums, xob, h2o, w, pre, x1 = (s.ring(n, R) for n in ("sums", "xob", "h2o", "w", "pre", "x1"))
        xob, h2o = s.ring("xob3", 4), s.ring("h2o3", 4)
        norms = Norms(s, 1, R, CHUNKS - 1 + 2)
        bS, bA = s.bank("S"), s.bank("A")
        own_loaded, x1_stored = s.sems("ownld", R), s.sems("x1st", R)
        q = {n: s.sem(n) for n in ["src_T", "summed", "sum_T", "w_done", "pre_done", "meas", "x1_done"]}
        xob, h2o = xob[:R], h2o[:R]
        with nc.Block() as block:

            @block.gpsimd
            def _(pool):
                def step(st):
                    if it := st.item(0):
                        need(pool, q["src_T"], it, R)
                        src.issue(pool, it)

                run_steps(pool, CHUNKS, LAGS, R, step)

            @block.sync
            def _(sp):
                def step(st):
                    if it := st.item(1):
                        need(sp, q["pre_done"], it, R)
                        sp.dma_start(as_tiles(xob[it.slot]), edge_rows(dram.x_own, it, 0)).then_inc(own_loaded[it.slot], 16)
                        sp.dma_start(as_tiles(h2o[it.slot]), edge_rows(dram.h2, it)).then_inc(own_loaded[it.slot], 16)
                    if it := st.item(3):
                        need(sp, q["x1_done"], it)
                        sp.dma_start(edge_rows(dram.x1, it), as_tiles(x1[it.slot])).then_inc(x1_stored[it.slot], 16)

                run_steps(sp, CHUNKS, LAGS, R, step)
                for k in range(R):
                    sp.wait_ge(x1_stored[k], 16 * len(range(k, CHUNKS, R)))

            @block.tensor
            def _(pe):
                def step(st):
                    if it := st.item(1):
                        src.wait(pe, it)
                        need(pe, q["summed"], it, 1)
                        transpose4(pe, bS, flat(src.rows[it.slot]), sh.ident[:, :]).then_inc(q["src_T"], 1)
                        need(pe, q["summed"], it)
                        need(pe, q["w_done"], it, 1)
                        transpose4(pe, bA, sums[it.slot], sh.ident[:, :]).then_inc(q["sum_T"], 1)

                run_steps(pe, CHUNKS, LAGS, R, step)

            @block.vector
            def _(ve):
                norms.prepare(ve)

                def step(st):
                    measured = []
                    if it := st.item(1):
                        need(ve, q["src_T"], it)
                        need(ve, q["sum_T"], it, R)
                        need(ve, q["summed"], it, 1)
                        segment_sum(ve, it, sums, sh.same[:, bass.ds(it.n * GROUP, GROUP)], bS[:, :])\
                            .then_inc(q["summed"], 1)
                    if it := st.item(2):
                        need(ve, q["sum_T"], it)
                        need_dma(ve, own_loaded, it, 0, 2)
                        ve.tensor_tensor(w[it.slot][:, :], bA[:, :], h2o[it.slot][:, :], ALU.add)\
                          .then_inc(q["w_done"], 1)
                        need(ve, q["w_done"], it)
                        need(ve, q["x1_done"], it, R)
                        for j in range(TILES):
                            last = ve.scalar_tensor_tensor(out=tile(pre[it.slot], j), in0=tile(w[it.slot], j),
                                                           scalar=column(sh.dst_root, it, j), in1=tile(xob[it.slot], j),
                                                           op0=ALU.mult, op1=ALU.add)
                        last.then_inc(q["pre_done"], 1)
                        need(ve, q["pre_done"], it)
                        norms.take(ve, 0, pre[it.slot]).then_inc(q["meas"], 1)
                        measured.append((q["meas"], it))
                    norms.finish(ve, st, measured)

                run_steps(ve, CHUNKS, LAGS, R, step)

            @block.scalar
            def _(act):
                def step(st):
                    if it := st.item(3):
                        norms.ready(act, st)
                        need_dma(act, x1_stored, it, 1)
                        norms.apply_scalar(act, st, 0, x1[it.slot], pre[it.slot]).then_inc(q["x1_done"], 1)

                run_steps(act, CHUNKS, LAGS, R, step)


def edge_gine_phase(nc, sh, dram):
    with ExitStack() as stack:
        s = Scope(nc, stack, "e3")
        R, LAGS = 2, 3
        mat, vcol = sh.mat, sh.vcol
        src = Gathers(s, sh.started, "src", dram.x1, sh.src_row, P, R)
        ea, x1o, x1b, sums, uT, r3, pre, x2T = (s.ring(n, R) for n in
                                                ("ea", "x1o", "x1b", "sums", "uT", "r3", "pre", "x2T"))
        x2h = s.ring("x2h", R, (P, TILES, 2 * P))
        norms = Norms(s, 1, R, CHUNKS - 1 + 2)
        bS, bO, bE, bF, bT, bH = (s.bank(n) for n in ("S", "O", "E", "F", "T", "H"))
        loaded, stored = s.sems("ld", R), s.sems("st", R)
        q = {n: s.sem(n) for n in ["msg", "msg_relu", "src_T", "own_T", "x1b_done", "summed", "u_done", "mm3", "relu3",
                                   "mm4", "pre_done", "meas", "x2_done", "x2_T", "x2T_out", "mmh", "h_out"]}
        with nc.Block() as block:

            @block.gpsimd
            def _(pool):
                def step(st):
                    if it := st.item(0):
                        need(pool, q["src_T"], it, R)
                        src.issue(pool, it)

                run_steps(pool, CHUNKS, LAGS, R, step)

            @block.sync
            def _(sp):
                def step(st):
                    if it := st.item(0):
                        need(sp, q["msg"], it, R)
                        need(sp, q["own_T"], it, R)
                        need(sp, q["x1b_done"], it, R)
                        sp.dma_start(as_tiles(ea[it.slot]), edge_rows(dram.edge_attr, it, 0)).then_inc(loaded[it.slot], 16)
                        sp.dma_start(as_tiles(x1o[it.slot]), edge_rows(dram.x1, it)).then_inc(loaded[it.slot], 16)
                    if it := st.item(3):
                        need(sp, q["x2_done"], it)
                        need(sp, q["h_out"], it)
                        sp.dma_start(edge_rows(dram.x2h, it), x2h[it.slot][:, :, :]).then_inc(stored[it.slot], 16)

                run_steps(sp, CHUNKS, LAGS, R, step)
                for k in range(R):
                    sp.wait_ge(stored[k], 16 * len(range(k, CHUNKS, R)))

            @block.tensor
            def _(pe):
                def step(st):
                    if it := st.item(1):
                        need_dma(pe, loaded, it, 0, 2)
                        need(pe, q["u_done"], it, 1)
                        transpose4(pe, bO, x1o[it.slot], sh.ident[:, :]).then_inc(q["own_T"], 1)
                    if it := st.item(3):
                        need(pe, q["x2_done"], it)
                        need(pe, q["x2T_out"], it, 1)
                        for j in range(TILES):
                            last = pe.transpose(tile(bT, j), wide(x2h[it.slot], 0)[:, j, :], sh.ident[:, :])
                        last.then_inc(q["x2_T"], 1)
                    if it := st.item(2):
                        need(pe, q["u_done"], it)
                        need(pe, q["relu3"], it, 1)
                        pe.matmul(bE[:, :], mat["L1_W1"], uT[it.slot][:, :], start=True, stop=True)\
                          .then_inc(q["mm3"], 1)
                    if it := st.item(3):
                        need(pe, q["x2T_out"], it)
                        need(pe, q["h_out"], it, 1)
                        product_nm(pe, bH, [(x2T[it.slot], mat["L2_W"])]).then_inc(q["mmh"], 1)
                    if it := st.item(2):
                        need(pe, q["relu3"], it)
                        need(pe, q["pre_done"], it, 1)
                        product_nm(pe, bF, [(r3[it.slot], mat["L1_W2"])]).then_inc(q["mm4"], 1)
                    if it := st.item(1):
                        need(pe, q["msg_relu"], it)
                        need(pe, q["summed"], it, 1)
                        transpose4(pe, bS, flat(src.rows[it.slot]), sh.ident[:, :]).then_inc(q["src_T"], 1)

                run_steps(pe, CHUNKS, LAGS, R, step)

            @block.vector
            def _(ve):
                norms.prepare(ve)

                def step(st):
                    measured = []
                    if it := st.item(1):
                        src.wait(ve, it)
                        need_dma(ve, loaded, it, 0, 2)
                        g = flat(src.rows[it.slot])
                        ve.tensor_tensor(g, g, ea[it.slot][:, :], ALU.add).then_inc(q["msg"], 1)
                        need(ve, q["pre_done"], it, R)
                        ve.tensor_tensor(x1b[it.slot][:, :], x1o[it.slot][:, :], sh.l1b2_4[:, :], ALU.add)\
                          .then_inc(q["x1b_done"], 1)
                    if it := st.item(2):
                        need(ve, q["mm4"], it)
                        need(ve, q["x1b_done"], it)
                        need(ve, q["x2_done"], it, R)
                        ve.tensor_tensor(pre[it.slot][:, :], bF[:, :], x1b[it.slot][:, :], ALU.add)\
                          .then_inc(q["pre_done"], 1)
                        need(ve, q["pre_done"], it)
                        norms.take(ve, 0, pre[it.slot]).then_inc(q["meas"], 1)
                        measured.append((q["meas"], it))
                    if it := st.item(1):
                        need(ve, q["src_T"], it)
                        need(ve, q["summed"], it, 1)
                        need(ve, q["u_done"], it, 1)
                        segment_sum(ve, it, sums, sh.same[:, bass.ds(it.n * GROUP, GROUP)], bS[:, :])\
                            .then_inc(q["summed"], 1)
                        need(ve, q["own_T"], it)
                        need(ve, q["summed"], it)
                        need(ve, q["mm3"], it, R)
                        ve.tensor_tensor(uT[it.slot][:, :], bO[:, :], sums[it.slot][:, :], ALU.add)\
                          .then_inc(q["u_done"], 1)
                    norms.finish(ve, st, measured)

                run_steps(ve, CHUNKS, LAGS, R, step)

            @block.scalar
            def _(act):
                def step(st):
                    if it := st.item(1):
                        need(act, q["msg"], it)
                        g = flat(src.rows[it.slot])
                        act.activation(g, g, ACT.Relu).then_inc(q["msg_relu"], 1)
                    if it := st.item(3):
                        norms.ready(act, st)
                        need_dma(act, stored, it, 1)
                        for j in range(TILES):
                            _, rstd, shift = norms.columns(st, 0, j)
                            last = act.activation(wide(x2h[it.slot], 0)[:, j, :], tile(pre[it.slot], j), ACT.Identity,
                                                  bias=shift, scale=rstd)
                        last.then_inc(q["x2_done"], 1)
                        need(act, q["x2_T"], it)
                        need(act, q["mmh"], it, R)
                        act.activation(x2T[it.slot][:, :], bT[:, :], ACT.Copy).then_inc(q["x2T_out"], 1)
                    if it := st.item(2):
                        need(act, q["mm3"], it)
                        need(act, q["mm4"], it, R)
                        act.activation(r3[it.slot][:, :], bE[:, :], ACT.Relu, bias=vcol["L1_b1"])\
                           .then_inc(q["relu3"], 1)
                    if it := st.item(3):
                        need(act, q["mmh"], it)
                        act.activation(wide(x2h[it.slot], 1), as_tiles(bH), ACT.Copy).then_inc(q["h_out"], 1)

                run_steps(act, CHUNKS, LAGS, R, step)


def edge_gat_phase(nc, sh, dram):
    with ExitStack() as stack:
        s = Scope(nc, stack, "e4")
        R, LAGS = 2, 3
        src = Gathers(s, sh.started, "src", dram.x2h, sh.src_row, 2 * P, R)
        dst = Gathers(s, sh.started, "dst", dram.x2h, sh.dst_row, 2 * P, R)
        hsT, hdT, e, es, w, S, L, num, den = (s.ring(n, R) for n in (
            "hsT", "hdT", "e", "es", "w", "S", "L", "num", "den"))
        z, c, ws, wh, sq, big = (s.ring(n, 1) * R for n in ("z", "c", "ws", "wh", "sq", "big"))
        m = s.ring("m", R, (P, GROUP + 1))
        rden = s.ring("rden", R, (P, TILES))
        bS, bD, bZ, bZs, bN, bL = (s.bank(n) for n in ("S", "D", "Z", "Zs", "N", "L"))
        q = {n: s.sem(n) for n in ["src_T", "dst_T", "hsT_out", "hdT_out", "logits", "z_out", "zs_out", "e_done",
                                   "es_done", "e_max", "big_done", "m_done", "carry", "c1", "c2", "w1", "ws1", "c_exp",
                                   "w_exp", "ws_exp", "c_done", "wh_done", "S_done", "L_done", "num1", "num_done",
                                   "den_done", "num_T", "den_T", "rden_done", "o_out", "sq_out", "summed"]}
        with nc.Block() as block:

            @block.gpsimd
            def _(pool):
                def step(st):
                    if it := st.item(0):
                        need(pool, q["src_T"], it, R)
                        src.issue(pool, it)
                        need(pool, q["dst_T"], it, R)
                        dst.issue(pool, it)

                run_steps(pool, CHUNKS, LAGS, R, step)

            @block.tensor
            def _(pe):
                def step(st):
                    if it := st.item(1):
                        src.wait(pe, it)
                        need(pe, q["hsT_out"], it, 1)
                        for j in range(TILES):
                            last = pe.transpose(tile(bS, j), wide(src.rows[it.slot], 1)[:, j, :], sh.ident[:, :])
                        last.then_inc(q["src_T"], 1)
                        dst.wait(pe, it)
                        need(pe, q["hdT_out"], it, 1)
                        for j in range(TILES):
                            last = pe.transpose(tile(bD, j), wide(dst.rows[it.slot], 1)[:, j, :], sh.ident[:, :])
                        last.then_inc(q["dst_T"], 1)
                        need(pe, q["hsT_out"], it)
                        need(pe, q["hdT_out"], it)
                        need(pe, q["e_done"], it, 1)
                        need(pe, q["es_done"], it, 1)
                        pe.matmul(bZ[:, :], sh.att_both[:, 0, :], hsT[it.slot][:, :], start=True, stop=False)
                        pe.matmul(bZ[:, :], sh.att_both[:, 1, :], hdT[it.slot][:, :], start=False, stop=True)
                        pe.matmul(bZs[:, :], sh.att_both[:, 2, :], hdT[it.slot][:, :], start=True, stop=True)\
                          .then_inc(q["logits"], 1)
                    if it := st.item(3):
                        need(pe, q["num_done"], it)
                        need(pe, q["o_out"], it, 1)
                        transpose4(pe, bN, num[it.slot], sh.ident[:, :]).then_inc(q["num_T"], 1)
                        need(pe, q["den_done"], it)
                        need(pe, q["rden_done"], it, 1)
                        transpose4(pe, bL, den[it.slot], sh.ident[:, :]).then_inc(q["den_T"], 1)

                run_steps(pe, CHUNKS, LAGS, R, step)

            @block.scalar
            def _(act):
                def step(st):
                    if it := st.item(1):
                        need(act, q["src_T"], it)
                        need(act, q["wh_done"], it, R)
                        act.activation(hsT[it.slot][:, :], bS[:, :], ACT.Copy).then_inc(q["hsT_out"], 1)
                        need(act, q["dst_T"], it)
                        need(act, q["num1"], it, R)
                        act.activation(hdT[it.slot][:, :], bD[:, :], ACT.Copy).then_inc(q["hdT_out"], 1)
                        need(act, q["logits"], it)
                        need(act, q["m_done"], it, 1)
                        act.activation(z[it.slot][:, :], bZ[:, :], ACT.Copy, scale=0.2).then_inc(q["z_out"], 1)
                        need(act, q["es_done"], it, 1)
                        act.activation(ws[it.slot][:, :], bZs[:, :], ACT.Copy, scale=0.2).then_inc(q["zs_out"], 1)
                    if it := st.item(2):
                        need(act, q["c2"], it)
                        act.activation(c[it.slot][:, :], c[it.slot][:, :], ACT.Exp).then_inc(q["c_exp"], 1)
                        need(act, q["w1"], it)
                        act.activation(w[it.slot][:, :], w[it.slot][:, :], ACT.Exp).then_inc(q["w_exp"], 1)
                        need(act, q["ws1"], it)
                        act.activation(es[it.slot][:, :], es[it.slot][:, :], ACT.Exp).then_inc(q["ws_exp"], 1)
                    if it := st.item(3):
                        act.wait_ge(sh.started, 1)
                        need(act, q["num_T"], it)
                        need(act, q["rden_done"], it)
                        out = sh.gat_own[:, bass.ds(it.n * GROUP, GROUP)]
                        for j in range(TILES):
                            last = act.activation(sh.gat_own[:, bass.ds(it.n * GROUP + j * P, P)], tile(bN, j), ACT.Copy,
                                                  scale=rden[it.slot][:, j:j + 1])
                        last.then_inc(q["o_out"], 1)
                        act.wait_ge(sh.started, 1)
                        need(act, q["o_out"], it)
                        need(act, q["summed"], it, 1)
                        act.activation(sq[it.slot][:, :], out, ACT.Square).then_inc(q["sq_out"], 1)

                run_steps(act, CHUNKS, LAGS, R, step)

            @block.vector
            def _(ve):
                def step(st):
                    if it := st.item(1):
                        same = sh.same[:, bass.ds(it.n * GROUP, GROUP)]
                        need(ve, q["m_done"], it, 1)
                        ve.tensor_scalar(big[it.slot][:, :], same, 0.5, 2.0 * BIG, ALU.subtract, ALU.mult)\
                          .then_inc(q["big_done"], 1)
                        need(ve, q["z_out"], it)
                        need(ve, q["w1"], it, R)
                        ve.tensor_tensor(e[it.slot][:, :], z[it.slot][:, :], bZ[:, :], ALU.max).then_inc(q["e_done"], 1)
                        need(ve, q["zs_out"], it)
                        need(ve, q["den_done"], it, R)
                        need(ve, q["num1"], it, R)
                        ve.tensor_tensor(es[it.slot][:, :], ws[it.slot][:, :], bZs[:, :], ALU.max)\
                          .then_inc(q["es_done"], 1)
                        need(ve, q["e_done"], it)
                        need(ve, q["es_done"], it)
                        ve.tensor_tensor(z[it.slot][:, :], e[it.slot][:, :], es[it.slot][:, :], ALU.max)\
                          .then_inc(q["e_max"], 1)
                        mm, prev = m[it.slot], m[(it.slot - 1) % R]
                        first = isinstance(it.n, int) and it.n == 0
                        if not first:
                            need(ve, q["m_done"], it, 1)
                        (ve.memset(mm[:, 0:1], 0.0) if first else ve.tensor_copy(mm[:, 0:1], prev[:, GROUP:GROUP + 1]))\
                            .then_inc(q["carry"], 1)
                        need(ve, q["carry"], it)
                        need(ve, q["e_max"], it)
                        need(ve, q["big_done"], it)
                        ve.tensor_tensor_scan(mm[:, 1:GROUP + 1], big[it.slot][:, :], z[it.slot][:, :], mm[:, 0:1],
                                              ALU.min, ALU.max).then_inc(q["m_done"], 1)
                    if it := st.item(2):
                        same = sh.same[:, bass.ds(it.n * GROUP, GROUP)]
                        before, now = m[it.slot][:, 0:GROUP], m[it.slot][:, 1:GROUP + 1]
                        need(ve, q["m_done"], it)
                        need(ve, q["S_done"], it, 1)
                        ve.tensor_tensor(c[it.slot][:, :], before, now, ALU.min).then_inc(q["c1"], 1)
                        ve.tensor_tensor(w[it.slot][:, :], e[it.slot][:, :], now, ALU.subtract).then_inc(q["w1"], 1)
                        need(ve, q["c1"], it)
                        ve.tensor_tensor(c[it.slot][:, :], c[it.slot][:, :], now, ALU.subtract).then_inc(q["c2"], 1)
                        ve.tensor_tensor(es[it.slot][:, :], es[it.slot][:, :], now, ALU.subtract).then_inc(q["ws1"], 1)
                        need(ve, q["c_exp"], it)
                        ve.tensor_tensor(c[it.slot][:, :], c[it.slot][:, :], same, ALU.mult).then_inc(q["c_done"], 1)
                        need(ve, q["w_exp"], it)
                        ve.tensor_tensor(wh[it.slot][:, :], w[it.slot][:, :], hsT[it.slot][:, :], ALU.mult)\
                          .then_inc(q["wh_done"], 1)
                        need(ve, q["c_done"], it)
                        if not (isinstance(it.n, int) and it.n == 0):
                            need(ve, q["S_done"], it, 1)
                            need(ve, q["L_done"], it, 1)
                        segment_sum(ve, it, L, c[it.slot][:, :], w[it.slot][:, :]).then_inc(q["L_done"], 1)
                        need(ve, q["wh_done"], it)
                        segment_sum(ve, it, S, c[it.slot][:, :], wh[it.slot][:, :]).then_inc(q["S_done"], 1)
                        need(ve, q["ws_exp"], it)
                        need(ve, q["num_T"], it, R)
                        need(ve, q["den_T"], it, R)
                        ve.tensor_tensor(num[it.slot][:, :], es[it.slot][:, :], hdT[it.slot][:, :], ALU.mult)\
                          .then_inc(q["num1"], 1)
                        need(ve, q["L_done"], it)
                        ve.tensor_tensor(den[it.slot][:, :], es[it.slot][:, :], L[it.slot][:, :], ALU.add)\
                          .then_inc(q["den_done"], 1)
                        need(ve, q["num1"], it)
                        need(ve, q["S_done"], it)
                        ve.tensor_tensor(num[it.slot][:, :], num[it.slot][:, :], S[it.slot][:, :], ALU.add)\
                          .then_inc(q["num_done"], 1)
                    if it := st.item(3):
                        need(ve, q["den_T"], it)
                        need(ve, q["o_out"], it, R)
                        ve.reciprocal(rden[it.slot][:, :], as_tiles(bL)[:, :, 0]).then_inc(q["rden_done"], 1)
                        need(ve, q["o_out"], it)
                        need(ve, q["sq_out"], it)
                        need(ve, q["summed"], it, 1)
                        for j in range(TILES):
                            rep = column(sh.is_rep, it, j)
                            ve.scalar_tensor_tensor(out=sh.sum1[:, j, :],
                                                    in0=sh.gat_own[:, bass.ds(it.n * GROUP + j * P, P)],
                                                    scalar=rep, in1=sh.sum1[:, j, :], op0=ALU.mult, op1=ALU.add)
                            last = ve.scalar_tensor_tensor(out=sh.sum2[:, j, :], in0=tile(sq[it.slot], j),
                                                           scalar=rep, in1=sh.sum2[:, j, :], op0=ALU.mult, op1=ALU.add)
                        last.then_inc(q["summed"], 1)

                run_steps(ve, CHUNKS, LAGS, R, step)


def batch_norm_phase(nc, sh, dram):
    with ExitStack() as stack:
        s = Scope(nc, stack, "bn")
        b1, b2 = s.bank("one"), s.bank("two")
        ones = s.sb("ones", [P, P])
        mean, var, half, t, y, row = (s.sb(n, [P, P]) for n in ("mean", "var", "half", "t", "y", "row"))
        stored, summed, cleared = s.sem("stored"), s.sem("summed"), s.sem("cleared")
        with nc.Block() as block:

            @block.sync
            def _(sp):
                sp.dma_start(dram.x2h[NPAD:ROWS, P:2 * P].rearrange("(c p) d -> p c d", p=P),
                             sh.gat_own[:, :].rearrange("p (c d) -> p c d", d=P)).then_inc(stored, 16)
                sp.wait_ge(stored, 16)

            @block.tensor
            def _(pe):
                pe.wait_ge(cleared, 1)
                for j in range(TILES):
                    pe.matmul(tile(b1, 0), ones[:, :], sh.sum1[:, j, :], start=(j == 0), stop=(j == TILES - 1))
                for j in range(TILES):
                    last = pe.matmul(tile(b2, 0), ones[:, :], sh.sum2[:, j, :], start=(j == 0), stop=(j == TILES - 1))
                last.then_inc(summed, 1)

            @block.vector
            def _(ve):
                ve.memset(ones[:, :], 1.0).then_inc(cleared, 1)
                ve.wait_ge(cleared, 1)
                ve.wait_ge(summed, 1)
                link = Link(ve, s.sem("link"), 0)
                link(ve.tensor_scalar(mean[:, :], tile(b1, 0), 1.0 / NODES, None, ALU.mult))
                link(ve.tensor_scalar(var[:, :], tile(b2, 0), 1.0 / NODES, None, ALU.mult))
                link(ve.tensor_tensor(t[:, :], mean[:, :], mean[:, :], ALU.mult))
                link(ve.tensor_tensor(var[:, :], var[:, :], t[:, :], ALU.subtract))
                link(ve.tensor_scalar(var[:, :], var[:, :], 0.0, EPS, ALU.max, ALU.add))
                link(ve.tensor_scalar(half[:, :], var[:, :], -0.5, None, ALU.mult))
                rsqrt(ve, link, y[:, :], var[:, :], half[:, :], t[:, :])
                link(ve.tensor_tensor(y[:, :], y[:, :], sh.vrow["gamma"], ALU.mult))
                link(ve.tensor_tensor(mean[:, :], mean[:, :], sh.vrow["bias"], ALU.add))
                link(ve.tensor_tensor(t[:, :], sh.vrow["bias"], mean[:, :], ALU.subtract))
                link(ve.tensor_tensor(t[:, :], t[:, :], y[:, :], ALU.mult))
                link(ve.tensor_tensor(row[:, :], t[:, :], sh.vrow["beta"], ALU.add))
                for j in range(TILES):
                    link(ve.tensor_copy(tile(sh.bn_scale_4, j), y[:, :]))
                    link(ve.tensor_copy(tile(sh.bn_shift_4, j), row[:, :]))


def back_phase(nc, sh, dram, edges):
    with ExitStack() as stack:
        s = Scope(nc, stack, "be" if edges else "bk")
        R = 4
        count = CHUNKS if edges else GROUPS
        B = 1 if edges else 0
        Y = B + 2
        LAGS = Y + 4
        mat, vcol = sh.mat, sh.vcol
        xh_depth = 2 if edges else R
        xh = s.ring("xh", xh_depth, (P, TILES, 2 * P)) * (R // xh_depth)
        x3, x4 = s.ring("x3", R), s.ring("x4", R)
        z, x3p, x3T, t1p, n1, tT, tb, t2p, n2, u, x4p = (s.pair(n, R) for n in (
            "z", "x3p", "x3T", "t1p", "n1", "tT", "tb", "t2p", "n2", "u", "x4p"))
        g = [s.ring(f"g{k}", 2) for k in range(4)]
        norms = Norms(s, 5 if edges else 4, R, count - 1 + Y + 3)
        bT, bY, bN, bGa, bGb, bO = (s.bank(n) for n in ("T", "Y", "N", "Ga", "Gb", "O"))
        bG = [bGa, bGb]
        xh_loaded, out_stored = s.sems("xhld", R), s.sems("outst", R)
        names = ["z1", "z2", "x3p_done", "meas0", "x3_done", "x3_T", "x3T_out", "mmy", "t1p_done", "meas1", "n1_done",
                 "n1_T", "tT_out", "tb1", "tb2", "mmg", "gelu", "mmo", "t2p_done", "meas2", "n2_done", "u1", "u2",
                 "x4p_done", "meas3", "x4_done"]
        if edges:
            names += ["sz1", "sz2", "s3p_done", "meas4", "s3_done", "s3_T", "s3T_out", "mms", "mmh", "hmax", "hmax_b",
                      "h_out", "md_done", "big_done", "rep_copied"]
            src = Gathers(s, sh.started, "src", dram.x2h, sh.src_row, 2 * P, 2)
            rep_idx = s.ring("rep_idx", R, (P, TILES), I32)
            scattered = s.sems("scattered", R)
            s3p, s3, s3T, hmax, md = (s.ring(n, 2) for n in ("s3p", "s3", "s3T", "hmax", "md"))
            sz, hT, big = (s.ring(n, 1) * 2 for n in ("sz", "hT", "big"))
            bS, bH = s.bank("S"), s.bank("H")
        q = {n: s.sem(n) for n in names}
        half = lambda it: it.slot % 2

        def src_item(it):
            return Item(it.turn * 2, it.slot, 2)

        with nc.Block() as block:

            @block.sync
            def _(sp):
                def step(st):
                    if it := st.item(B):
                        need(sp, q["x3p_done"], it, xh_depth)
                        rows = edge_rows(dram.x2h, it) if edges else node_rows(dram.x2h, it)
                        sp.dma_start(xh[it.slot][:, :, :], rows).then_inc(xh_loaded[it.slot], 16)
                    if not edges and (it := st.item(LAGS)):
                        need(sp, q["x4_done"], it)
                        sp.dma_start(node_rows(dram.out, it), as_tiles(x4[it.slot])).then_inc(out_stored[it.slot], 16)

                run_steps(sp, count, LAGS, R, step)
                for k in range(R):
                    if not edges:
                        sp.wait_ge(out_stored[k], 16 * len(range(k, count, R)))

            @block.gpsimd
            def _(pool):
                def step(st):
                    if edges and (it := st.item(0)):
                        need(pool, q["s3p_done"], it, 2)
                        src.issue(pool, src_item(it))
                    if it := st.item(B + 1):
                        need_dma(pool, xh_loaded, it)
                        need(pool, q["x3p_done"], it, 2)
                        zz = z[half(it)]
                        pool.tensor_tensor(as_tiles(zz), wide(xh[it.slot], 1), as_tiles(sh.bn_scale_4), ALU.mult)\
                            .then_inc(q["z1"], 1)
                        need(pool, q["z1"], it)
                        pool.tensor_tensor(zz[:, :], zz[:, :], sh.bn_shift_4[:, :], ALU.add).then_inc(q["z2"], 1)
                    if it := st.item(Y + 1):
                        need(pool, q["n1_done"], it)
                        need(pool, q["t2p_done"], it, 2)
                        pool.tensor_tensor(tb[it.slot][:, :], n1[it.slot][:, :], sh.ln1_g_4[:, :], ALU.mult)\
                            .then_inc(q["tb1"], 1)
                        need(pool, q["tb1"], it)
                        pool.tensor_tensor(tb[it.slot][:, :], tb[it.slot][:, :], sh.ln1_b_f2_4[:, :], ALU.add)\
                            .then_inc(q["tb2"], 1)
                    if it := st.item(Y + 3):
                        need(pool, q["n2_done"], it)
                        need(pool, q["x4p_done"], it, 2)
                        pool.tensor_tensor(u[it.slot][:, :], n2[it.slot][:, :], sh.ln2_g_4[:, :], ALU.mult)\
                            .then_inc(q["u1"], 1)
                        need(pool, q["u1"], it)
                        pool.tensor_tensor(u[it.slot][:, :], u[it.slot][:, :], sh.ln2_b_4[:, :], ALU.add)\
                            .then_inc(q["u2"], 1)
                    if edges and (it := st.item(LAGS)):
                        need_dma(pool, scattered, it, 1, TILES)
                        pool.tensor_copy(rep_idx[it.slot][:, :], sh.rep_rows[:, bass.ds(it.n * TILES, TILES)])\
                            .then_inc(q["rep_copied"], 1)
                        need_apart(pool, sh.started, q["rep_copied"], it)
                        need(pool, q["x4_done"], it)
                        for j in range(TILES):
                            pool.indirect_dma_start(dram.out, bass.IndirectOffsetOnAxis(ap=rep_idx[it.slot][:, j:j + 1], axis=0),
                                                    tile(x4[it.slot], j), None, bounds_check=NPAD - 1,
                                                    oob_is_err=False).then_inc(scattered[it.slot], 16)

                run_steps(pool, count, LAGS, R, step)
                if edges:
                    for k in range(R):
                        pool.wait_ge(scattered[k], 16 * TILES * len(range(k, count, R)))

            @block.tensor
            def _(pe):
                def step(st):
                    if it := st.item(Y):
                        need(pe, q["x3_done"], it)
                        need(pe, q["x3T_out"], it, 1)
                        transpose4(pe, bT, x3[it.slot], sh.ident[:, :]).then_inc(q["x3_T"], 1)
                    if edges and (it := st.item(2)):
                        need(pe, q["s3_done"], it)
                        need(pe, q["hmax"], it, 1)
                        transpose4(pe, bS, s3[half(it)], sh.ident[:, :]).then_inc(q["s3_T"], 1)
                    if it := st.item(Y + 2):
                        value = it.n * 4 + 4
                        pe.wait_ge(q["gelu"], value)
                        need(pe, q["t2p_done"], it, 1)
                        product_nm(pe, bO, [(g[k][half(it)], mat["F2" + "abcd"[k]]) for k in range(4)])\
                            .then_inc(q["mmo"], 1)
                    if it := st.item(Y + 1):
                        need(pe, q["n1_done"], it)
                        need(pe, q["tT_out"], it, 1)
                        transpose4(pe, bN, n1[it.slot], sh.ident[:, :]).then_inc(q["n1_T"], 1)
                    if edges and (it := st.item(2)):
                        need(pe, q["s3T_out"], it)
                        pe.matmul(bS[:, :], mat["W_in"], s3T[half(it)][:, :], start=True, stop=True)\
                          .then_inc(q["mms"], 1)
                    if edges and (it := st.item(Y)):
                        need(pe, q["x3T_out"], it)
                        need(pe, q["h_out"], it, 1)
                        pe.matmul(bH[:, :], mat["W_in"], x3T[it.slot][:, :], start=True, stop=True)\
                          .then_inc(q["mmh"], 1)
                    if it := st.item(Y):
                        need(pe, q["x3T_out"], it)
                        need(pe, q["t1p_done"], it, 1)
                        pairs = [(x3T[it.slot], sh.fold_self[:, :])]
                        if edges:
                            need(pe, q["md_done"], it)
                            pairs.append((md[half(it)], sh.fold_bot[:, :]))
                        product_nm(pe, bY, pairs).then_inc(q["mmy"], 1)
                    if it := st.item(Y + 1):
                        need(pe, q["tT_out"], it)
                        for k in range(4):
                            value = it.n * 4 + k - 1
                            if not isinstance(value, int) or value > 0:
                                pe.wait_ge(q["gelu"], value)
                            pe.matmul(bG[k % 2][:, :], mat["F1" + "abcd"[k]], tT[half(it)][:, :], start=True,
                                      stop=True).then_inc(q["mmg"], 1)

                run_steps(pe, count, LAGS, R, step)

            @block.scalar
            def _(act):
                def step(st):
                    if it := st.item(Y + 1):
                        norms.ready(act, st)
                        need(act, q["n1_T"], it, 2)
                        need(act, q["tb1"], it, 2)
                        norms.apply_scalar(act, st, 1, n1[it.slot], t1p[it.slot]).then_inc(q["n1_done"], 1)
                    if it := st.item(Y + 3):
                        norms.ready(act, st)
                        need(act, q["u1"], it, 2)
                        norms.apply_scalar(act, st, 2, n2[it.slot], t2p[it.slot]).then_inc(q["n2_done"], 1)
                    if it := st.item(Y):
                        need(act, q["x3_T"], it)
                        need(act, q["mmy"], it, 2)
                        act.activation(x3T[it.slot][:, :], bT[:, :], ACT.Copy).then_inc(q["x3T_out"], 1)
                    if edges and (it := st.item(2)):
                        need(act, q["s3_T"], it)
                        need(act, q["mms"], it, 2)
                        act.activation(s3T[half(it)][:, :], bS[:, :], ACT.Copy).then_inc(q["s3T_out"], 1)
                    if it := st.item(Y + 1):
                        need(act, q["n1_T"], it)
                        value = (it.n - 1) * 4
                        if not isinstance(value, int) or value > 0:
                            act.wait_ge(q["mmg"], value)
                        act.activation(tT[half(it)][:, :], bN[:, :], ACT.Identity, bias=vcol["ln1_b"],
                                       scale=vcol["ln1_g"]).then_inc(q["tT_out"], 1)
                    if edges and (it := st.item(Y)):
                        need(act, q["mmh"], it)
                        need(act, q["md_done"], it, 1)
                        act.activation(hT[half(it)][:, :], bH[:, :], ACT.Identity, bias=vcol["b_in"])\
                           .then_inc(q["h_out"], 1)
                        need(act, q["hmax"], it)
                        act.activation(md[half(it)][:, :], hmax[half(it)][:, :], ACT.Identity, bias=vcol["b_in"])\
                           .then_inc(q["hmax_b"], 1)
                    if it := st.item(LAGS):
                        norms.ready(act, st)
                        if edges:
                            need_dma(act, scattered, it, 1, TILES)
                        else:
                            need_dma(act, out_stored, it, 1)
                        norms.apply_scalar(act, st, 3, x4[it.slot], x4p[it.slot]).then_inc(q["x4_done"], 1)
                    if it := st.item(Y + 1):
                        need(act, q["mmo"], it, 2)
                        for k in range(4):
                            act.wait_ge(q["mmg"], it.n * 4 + k + 1)
                            act.activation(g[k][half(it)][:, :], bG[k % 2][:, :], ACT.Gelu,
                                           bias=vcol["f1_b" + "abcd"[k]]).then_inc(q["gelu"], 1)

                run_steps(act, count, LAGS, R, step)

            @block.vector
            def _(ve):
                norms.prepare(ve)

                def step(st):
                    measured = []
                    if not (isinstance(st.i, int) and st.i == 0):
                        norms.ready(ve, st)
                    if it := st.item(Y):
                        need(ve, q["x3_T"], it, R)
                        norms.apply_vector(ve, st, 0, x3[it.slot], x3p[it.slot]).then_inc(q["x3_done"], 1)
                    if edges and (it := st.item(2)):
                        need(ve, q["s3_T"], it, 2)
                        norms.apply_vector(ve, st, 4, s3[half(it)], s3p[half(it)]).then_inc(q["s3_done"], 1)
                    if it := st.item(B + 1):
                        need(ve, q["z2"], it)
                        need_dma(ve, xh_loaded, it)
                        ve.scalar_tensor_tensor(out=as_tiles(x3p[it.slot]), in0=as_tiles(z[half(it)]), scalar=0.0,
                                                in1=wide(xh[it.slot], 0), op0=ALU.max, op1=ALU.add)\
                          .then_inc(q["x3p_done"], 1)
                        need(ve, q["x3p_done"], it)
                        norms.take(ve, 0, x3p[it.slot]).then_inc(q["meas0"], 1)
                        measured.append((q["meas0"], it))
                    if edges and (it := st.item(1)):
                        src.wait(ve, src_item(it))
                        rows = src.rows[half(it)]
                        ve.tensor_tensor(as_tiles(sz[half(it)]), wide(rows, 1), as_tiles(sh.bn_scale_4), ALU.mult)\
                          .then_inc(q["sz1"], 1)
                        need(ve, q["sz1"], it)
                        ve.tensor_tensor(sz[half(it)][:, :], sz[half(it)][:, :], sh.bn_shift_4[:, :], ALU.add)\
                          .then_inc(q["sz2"], 1)
                        need(ve, q["sz2"], it)
                        ve.scalar_tensor_tensor(out=as_tiles(s3p[half(it)]), in0=as_tiles(sz[half(it)]), scalar=0.0,
                                                in1=wide(rows, 0), op0=ALU.max, op1=ALU.add)\
                          .then_inc(q["s3p_done"], 1)
                        need(ve, q["s3p_done"], it)
                        norms.take(ve, 4, s3p[half(it)]).then_inc(q["meas4"], 1)
                        measured.append((q["meas4"], it))
                    if edges and (it := st.item(2)):
                        same = sh.same[:, bass.ds(it.n * GROUP, GROUP)]
                        if not (isinstance(it.n, int) and it.n == 0):
                            need(ve, q["hmax"], it, 1)
                        ve.tensor_scalar(big[half(it)][:, :], same, 0.5, 2.0 * BIG, ALU.subtract, ALU.mult)\
                          .then_inc(q["big_done"], 1)
                        need(ve, q["big_done"], it)
                        need(ve, q["mms"], it)
                        need(ve, q["hmax_b"], it, 2)
                        start = -BIG
                        if not (isinstance(it.n, int) and it.n == 0):
                            start = hmax[1 - half(it)][:, GROUP - 1:GROUP]
                        ve.tensor_tensor_scan(hmax[half(it)][:, :], big[half(it)][:, :], bS[:, :], start, ALU.min,
                                              ALU.max).then_inc(q["hmax"], 1)
                    if edges and (it := st.item(Y)):
                        need(ve, q["hmax_b"], it)
                        need(ve, q["h_out"], it)
                        ve.tensor_tensor(md[half(it)][:, :], md[half(it)][:, :], hT[half(it)][:, :], ALU.subtract)\
                          .then_inc(q["md_done"], 1)
                    if it := st.item(Y + 3):
                        need(ve, q["u2"], it)
                        need(ve, q["x4_done"], it, 2)
                        ve.tensor_tensor(x4p[it.slot][:, :], u[it.slot][:, :], x3[it.slot][:, :], ALU.add)\
                          .then_inc(q["x4p_done"], 1)
                        need(ve, q["x4p_done"], it)
                        norms.take(ve, 3, x4p[it.slot]).then_inc(q["meas3"], 1)
                        measured.append((q["meas3"], it))
                    if it := st.item(Y + 2):
                        need(ve, q["mmo"], it)
                        need(ve, q["tb2"], it)
                        need(ve, q["n2_done"], it, 2)
                        ve.tensor_tensor(t2p[it.slot][:, :], bO[:, :], tb[it.slot][:, :], ALU.add)\
                          .then_inc(q["t2p_done"], 1)
                        need(ve, q["t2p_done"], it)
                        norms.take(ve, 2, t2p[it.slot]).then_inc(q["meas2"], 1)
                        measured.append((q["meas2"], it))
                    if it := st.item(Y):
                        need(ve, q["mmy"], it)
                        need(ve, q["n1_done"], it, 2)
                        ve.tensor_tensor(t1p[it.slot][:, :], bY[:, :], sh.fold_bias_4[:, :], ALU.add)\
                          .then_inc(q["t1p_done"], 1)
                        need(ve, q["t1p_done"], it)
                        norms.take(ve, 1, t1p[it.slot]).then_inc(q["meas1"], 1)
                        measured.append((q["meas1"], it))
                    norms.finish(ve, st, measured)

                run_steps(ve, count, LAGS, R, step)


def repeat_rows_phase(nc, sh):
    with ExitStack() as stack:
        s = Scope(nc, stack, "rep")
        copied = s.sem("copied")
        with nc.Block() as block:

            @block.vector
            def _(ve):
                link = Link(ve, copied, 0)
                for out, row in ((sh.b2_4, sh.vrow["L0_b2"]), (sh.l1b2_4, sh.vrow["L1_b2"]),
                                 (sh.ln1_g_4, sh.vrow["ln1_g"]), (sh.ln1_b_f2_4, sh.ln1_b_f2[:, :]),
                                 (sh.ln2_g_4, sh.vrow["ln2_g"]), (sh.ln2_b_4, sh.vrow["ln2_b"]),
                                 (sh.fold_bias_4, sh.fold_bias[:, :])):
                    for j in range(TILES):
                        link(ve.tensor_copy(tile(out, j), row))
                link(ve.memset(sh.sum1[:, :, :], 0.0))
                link(ve.memset(sh.sum2[:, :, :], 0.0))
                link(ve.memset(sh.two[:, :], 2.0))


class Tables:
    pass


def graph_layers(nc, x, src_cols, dst_cols, next_cols, dst_row, edge_attr, mats, vcols, vrows, out):
    dram, sh = Tables(), Shared()
    dram.x, dram.src_cols, dram.dst_cols, dram.next_cols, dram.dst_row = x, src_cols, dst_cols, next_cols, dst_row
    dram.edge_attr, dram.mats, dram.vcols, dram.vrows, dram.out = edge_attr, mats, vcols, vrows, out
    scratch = lambda name, shape: nc.dram_tensor(name, shape, F32, kind="Internal").ap()
    dram.map = scratch("node_map", (NPAD, 2))
    dram.h2 = scratch("h2", (ROWS, P))
    dram.x1 = scratch("x1", (ROWS, P))
    dram.x2h = scratch("x2h", (ROWS, 2 * P))
    dram.x_own = scratch("x_own", (EPAD, P))
    dram.count_row = scratch("count_row", (1, EPAD))
    with ExitStack() as stack:
        s = Scope(nc, stack, "sh")
        sh.mats = s.sb("mats", [P, len(MATS) * P])
        sh.vcols = s.sb("vcols", [P, len(VECS)])
        sh.vrows = s.sb("vrows", [P, len(VECS) * P])
        sh.mat = {n: sh.mats[:, k * P:(k + 1) * P] for k, n in enumerate(MATS)}
        sh.vcol = {n: sh.vcols[:, k:k + 1] for k, n in enumerate(VECS)}
        sh.vrow = {n: sh.vrows[:, k * P:(k + 1) * P] for k, n in enumerate(VECS)}
        sh.ident = s.sb("ident", [P, P])
        sh.started = s.sem("started")
        sh.same = s.sb("same", [P, EPAD], BF16)
        sh.src_cols, sh.dst_cols, sh.rep_rows, sh.src_row, sh.dst_row = (
            s.sb(n, [P, ECOLS], I32) for n in ("src_cols", "dst_cols", "rep_rows", "src_row", "dst_row"))
        sh.is_rep, sh.src_root, sh.dst_root = (s.sb(n, [P, ECOLS]) for n in ("is_rep", "src_root", "dst_root"))
        sh.map_rows, sh.src_map, sh.dst_map = (s.sb(n, [P, ECOLS, 2]) for n in ("map_rows", "src_map", "dst_map"))
        sh.alone3 = s.sb("alone", [P, GROUPS * TILES])
        sh.alone = sh.alone3
        sh.two = s.sb("two", [P, 1])
        sh.sum1, sh.sum2 = s.sb("sum1", [P, TILES, P]), s.sb("sum2", [P, TILES, P])
        sh.att_both = s.sb("att_both", [P, 3, P])
        sh.bc_cols = s.sb("bc_cols", [P, 2, P])
        sh.fold_self, sh.fold_bot, sh.fold_bias, sh.ln1_b_f2 = (
            s.sb(n, [P, P]) for n in ("fold_self", "fold_bot", "fold_bias", "ln1_b_f2"))
        (sh.b2_4, sh.l1b2_4, sh.ln1_g_4, sh.ln1_b_f2_4, sh.ln2_g_4, sh.ln2_b_4, sh.fold_bias_4, sh.bn_scale_4,
         sh.bn_shift_4) = (s.sb(n, [P, GROUP]) for n in (
            "b2_4", "l1b2_4", "ln1_g_4", "ln1_b_f2_4", "ln2_g_4", "ln2_b_4", "fold_bias_4", "bn_scale_4", "bn_shift_4"))
        setup_phase(nc, sh, dram)
        repeat_rows_phase(nc, sh)
        map_phase(nc, sh, dram)
        dense_front_phase(nc, sh, dram)
        edge_gcn1_phase(nc, sh, dram)
        edge_gcn2_phase(nc, sh, dram)
        edge_gine_phase(nc, sh, dram)
        with ExitStack() as gat_stack:
            sh.gat_own = Scope(nc, gat_stack, "g").sb("gat_own", [P, EPAD])
            edge_gat_phase(nc, sh, dram)
            batch_norm_phase(nc, sh, dram)
        back_phase(nc, sh, dram, False)
        back_phase(nc, sh, dram, True)


def kernel(x, src, dst, edge_attr_128, edge_attr_16, **w):
    import numpy as np
    import concourse.bacc as bacc
    from concourse.bass_utils import run_bass_kernel_spmd

    def columns(a):
        return np.ascontiguousarray(a.reshape(ECOLS, P).T)

    def padded(a, fill):
        return np.concatenate([a, np.full((EPAD - EDGES,), fill, a.dtype)])

    W = {k: np.asarray(v) for k, v in w.items()}
    src, dst, x = np.asarray(src), padded(np.asarray(dst), NODES), np.asarray(x)
    x_pad = np.concatenate([x, np.zeros((NPAD - NODES, P), x.dtype)])
    edge_attr = np.asarray(edge_attr_128)
    edge_attr = np.concatenate([edge_attr, np.zeros((EPAD - EDGES, P), edge_attr.dtype)])
    w1t, w2t, upd = W["L0_gnn_W1"].T, W["L0_gnn_W2"].T, W["L3_gnn_W_upd_w"]
    f1, f2 = W["L3_gnn_ffn1_w"], W["L3_gnn_ffn2_w"]
    mats = [w1t[:, :P], w1t[:, P:], w2t[:P], w2t[P:], W["L1_gnn_W1"].T, W["L1_gnn_W2"].T, W["L2_gnn_W"],
            W["L3_gnn_W_in_w"], W["L3_gnn_W_in_w"].T, upd[:P].T, upd[P:].T, W["L3_gnn_W_out_w"]]
    mats += [f1[:, k * P:(k + 1) * P] for k in range(4)] + [f2[k * P:(k + 1) * P] for k in range(4)]
    f1b = W["L3_gnn_ffn1_b"]
    vecs = [W["L0_gnn_b1"][:P], W["L0_gnn_b1"][P:], W["L0_gnn_b2"], W["L1_gnn_b1"], W["L1_gnn_b2"],
            W["L2_gnn_att_src"], W["L2_gnn_att_dst"], W["L2_gnn_bias"], W["L2_gnn_gamma"], W["L2_gnn_beta"],
            W["L3_gnn_W_in_b"], W["L3_gnn_W_upd_b"], W["L3_gnn_W_out_b"], W["L3_gnn_ln1_g"], W["L3_gnn_ln1_b"],
            W["L3_gnn_ln2_g"], W["L3_gnn_ln2_b"]] + [f1b[k * P:(k + 1) * P] for k in range(4)] + [W["L3_gnn_ffn2_b"]]
    arrays = {
        "x": x_pad, "src_cols": columns(padded(src, 0)), "dst_cols": columns(dst),
        "next_cols": columns(np.concatenate([dst[1:], np.full((1,), NODES, dst.dtype)])),
        "dst_row": dst[None, :], "edge_attr": edge_attr,
        "mats": np.ascontiguousarray(np.concatenate(mats, axis=1)),
        "vcols": np.ascontiguousarray(np.stack(vecs, axis=1)), "vrows": np.concatenate(vecs)[None, :],
    }
    nc = bacc.Bacc("TRN2", target_bir_lowering=False, num_devices=1)
    args = [nc.dram_tensor(f"in_{n}", a.shape, mybir.dt.from_np(a.dtype), kind="ExternalInput").ap()
            for n, a in arrays.items()]
    out = nc.dram_tensor("out", (NPAD, P), F32, kind="ExternalOutput").ap()
    graph_layers(nc, *args, out)
    result = run_bass_kernel_spmd(nc, [{f"in_{n}": a for n, a in arrays.items()}], core_ids=[0])
    return result.results[0]["out"][:NODES]
```

```python
from contextlib import ExitStack

import concourse.bass as bass
from concourse import mybir

F32 = mybir.dt.float32
BF16 = mybir.dt.bfloat16
I32 = mybir.dt.int32
ALU = mybir.AluOpType
ACT = mybir.ActivationFunctionType

P = 128
TILES = 4
GROUP = TILES * P
NODES = 50000
EDGES = 12500
GROUPS = -(-NODES // GROUP)
NPAD = GROUPS * GROUP
CHUNKS = -(-EDGES // GROUP)
EPAD = CHUNKS * GROUP
ECOLS = EPAD // P
ROWS = NPAD + EPAD
EPS = 1e-5
SKIP = 1 << 20
BIG = 1.5e38
RSQRT_MAGIC = 0x5F3759DF

MATS = ["L0_W1a", "L0_W1b", "L0_W2a", "L0_W2b", "L1_W1", "L1_W2", "L2_W", "W_in", "W_inT", "W_topT", "W_botT",
        "W_out", "F1a", "F1b", "F1c", "F1d", "F2a", "F2b", "F2c", "F2d"]
VECS = ["L0_b1a", "L0_b1b", "L0_b2", "L1_b1", "L1_b2", "att_src", "att_dst", "bias", "gamma", "beta",
        "b_in", "b_upd", "b_out", "ln1_g", "ln1_b", "ln2_g", "ln2_b", "f1_ba", "f1_bb", "f1_bc", "f1_bd", "f2_b"]


class Item:

    def __init__(self, turn, offset, ring):
        self.turn = turn + offset // ring
        self.slot = offset % ring
        self.n = self.turn * ring + self.slot
        self.ring = ring


class Step:
    def __init__(self, turn, offset, ring, count):
        self.turn, self.offset, self.ring, self.count = turn, offset, ring, count
        self.i = turn * ring + offset

    def item(self, lag):
        it = Item(self.turn, self.offset - lag, self.ring)
        if isinstance(it.n, int) and not 0 <= it.n < self.count:
            return None
        return it


def run_steps(engine, count, lags, ring, step):
    head = -(-(lags + ring) // ring)
    tail = count // ring
    for i in range(head * ring):
        step(Step(i // ring, i % ring, ring, count))
    with engine.Fori(head, tail) as turn:
        for u in range(ring):
            step(Step(turn, u, ring, count))
    for i in range(tail * ring, count + lags):
        step(Step(i // ring, i % ring, ring, count))


def need(engine, sem, item, back=0):
    value = item.n + 1 - back
    if not isinstance(value, int) or value > 0:
        engine.wait_ge(sem, value)


def need_dma(engine, sems, item, back=0, dmas=1):
    value = (item.turn + 1 - back) * (16 * dmas)
    if not isinstance(value, int) or value > 0:
        engine.wait_ge(sems[item.slot], value)


def need_apart(engine, started, sem, item):
    value = item.n + 1
    if not isinstance(value, int):
        value = engine.to_reg(value)
    engine.wait_ge(started, 1)
    engine.wait_ge(sem, value)


class Scope:

    def __init__(self, nc, stack, prefix):
        self.nc, self.stack, self.prefix, self.handles = nc, stack, prefix, []
        stack.callback(self.release)

    def release(self):
        if self.handles:
            self.nc.clear_and_free_semaphores(self.handles)
            self.nc.all_engine_barrier()

    def sb(self, name, shape, dt=F32):
        return self.stack.enter_context(self.nc.sbuf_tensor(f"{self.prefix}_{name}", shape, dt))

    def ring(self, name, depth, shape=(P, GROUP), dt=F32):
        return [self.sb(f"{name}{k}", list(shape), dt) for k in range(depth)]

    def pair(self, name, ring):
        return self.ring(name, 2) * (ring // 2)

    def bank(self, name):
        return self.stack.enter_context(self.nc.psum_tensor(f"{self.prefix}_{name}", [P, GROUP], F32))

    def sem(self, name):
        handle = self.nc.alloc_semaphore(name=f"{self.prefix}_{name}")
        self.handles.append(handle)
        return handle

    def sems(self, name, depth):
        return [self.sem(f"{name}{k}") for k in range(depth)]


def tile(buf, j):
    return buf[:, j * P:(j + 1) * P]


def transpose4(pe, out, in_, ident):
    for j in range(TILES):
        last = pe.transpose(tile(out, j), tile(in_, j), ident)
    return last


def product_nm(pe, out, pairs):
    for j in range(TILES):
        for n, (operand, matrix) in enumerate(pairs):
            last = pe.matmul(tile(out, j), tile(operand, j), matrix, start=(n == 0), stop=(n == len(pairs) - 1))
    return last


class Link:

    def __init__(self, ve, sem, base):
        self.ve, self.sem, self.base, self.n = ve, sem, base, 0

    def __call__(self, instruction):
        self.n += 1
        instruction.then_inc(self.sem, 1)
        self.ve.wait_ge(self.sem, self.base + self.n)


RSQRT_LINKS = 2 + 3 * 3


def rsqrt(ve, link, y, v, half, t):
    link(ve.tensor_scalar(y.bitcast(I32), v.bitcast(I32), 1, None, ALU.logical_shift_right))
    link(ve.tensor_scalar(y.bitcast(I32), y.bitcast(I32), -1.0, float(RSQRT_MAGIC), ALU.mult, ALU.add))
    for _ in range(3):
        link(ve.tensor_tensor(t, y, y, ALU.mult))
        link(ve.tensor_tensor(t, t, half, ALU.mult))
        link(ve.scalar_tensor_tensor(out=y, in0=t, scalar=1.5, in1=y, op0=ALU.add, op1=ALU.mult))


NORM_LINKS = 8 + RSQRT_LINKS + 1


class Norms:

    def __init__(self, scope, count, last):
        cols = count * TILES
        self.last = last
        self.stats = scope.ring("stats", 2, (P, cols, 6))
        self.work = scope.sb("norm_work", [P, 4, cols])
        self.result = scope.ring("norm_result", 2, (P, 3, cols))
        self.sem = scope.sem("norm_link")
        self.init = scope.sem("norm_init")

    def prepare(self, ve):
        for k in range(2):
            ve.memset(self.stats[k][:, :, :], 1.0).then_inc(self.init, 1)
        ve.wait_ge(self.init, 2)

    def take(self, ve, step, which, buf, chain):
        for j in range(TILES):
            last = ve.bn_stats(self.stats[step.offset % 2][:, which * TILES + j, :], tile(buf, j))
            if j < TILES - 1:
                next(chain, None)
        return last

    def chain(self, ve, step, measured):
        if isinstance(step.i, int) and step.i > self.last:
            return
        for sem, item in measured:
            if item:
                need(ve, sem, item)
        base = step.i * NORM_LINKS
        s = self.stats[(step.offset - 1) % 2]
        t, v, half, d = (self.work[:, k, :] for k in range(4))
        mean, rstd, shift = (self.result[step.offset % 2][:, k, :] for k in range(3))
        if not isinstance(base, int) or base > 0:
            ve.wait_ge(self.sem, base)
        ve.tensor_tensor(mean, s[:, :, 1], s[:, :, 4], ALU.add).then_inc(self.sem, 1)
        yield
        ve.wait_ge(self.sem, base + 1)
        ve.tensor_tensor(d, s[:, :, 1], s[:, :, 4], ALU.subtract).then_inc(self.sem, 1)
        yield
        ve.tensor_tensor(v, s[:, :, 2], s[:, :, 5], ALU.add).then_inc(self.sem, 1)
        ve.wait_ge(self.sem, base + 2)
        ve.tensor_tensor(d, d, d, ALU.mult).then_inc(self.sem, 1)
        yield
        ve.wait_ge(self.sem, base + 4)
        ve.scalar_tensor_tensor(out=v, in0=d, scalar=P / 4.0, in1=v, op0=ALU.mult, op1=ALU.add).then_inc(self.sem, 1)
        yield
        ve.wait_ge(self.sem, base + 5)
        ve.tensor_scalar(v, v, 1.0 / P, EPS, ALU.mult, ALU.add).then_inc(self.sem, 1)
        ve.tensor_scalar(mean, mean, 0.5, None, ALU.mult).then_inc(self.sem, 1)
        yield
        ve.wait_ge(self.sem, base + 7)
        ve.tensor_scalar(half, v, -0.5, None, ALU.mult).then_inc(self.sem, 1)
        ve.tensor_scalar(rstd.bitcast(I32), v.bitcast(I32), 1, None, ALU.logical_shift_right).then_inc(self.sem, 1)
        yield
        ve.wait_ge(self.sem, base + 9)
        ve.tensor_scalar(rstd.bitcast(I32), rstd.bitcast(I32), -1.0, float(RSQRT_MAGIC), ALU.mult, ALU.add)\
          .then_inc(self.sem, 1)
        yield
        for k in range(3):
            ve.wait_ge(self.sem, base + 10 + 3 * k)
            ve.tensor_tensor(t, rstd, rstd, ALU.mult).then_inc(self.sem, 1)
            yield
            ve.wait_ge(self.sem, base + 11 + 3 * k)
            ve.tensor_tensor(t, t, half, ALU.mult).then_inc(self.sem, 1)
            yield
            ve.wait_ge(self.sem, base + 12 + 3 * k)
            ve.scalar_tensor_tensor(out=rstd, in0=t, scalar=1.5, in1=rstd, op0=ALU.add, op1=ALU.mult)\
              .then_inc(self.sem, 1)
            yield
        ve.wait_ge(self.sem, base + 19)
        ve.scalar_tensor_tensor(out=shift, in0=mean, scalar=-1.0, in1=rstd, op0=ALU.mult, op1=ALU.mult)\
          .then_inc(self.sem, 1)
        yield

    def ready(self, engine, step):
        done = min(step.i, self.last) + 1 if isinstance(step.i, int) else step.i + 1
        engine.wait_ge(self.sem, done * NORM_LINKS)

    def columns(self, step, which, j):
        c = which * TILES + j
        return [self.result[step.offset % 2][:, k, c:c + 1] for k in range(3)]

    def apply_vector(self, ve, step, which, out, in_):
        for j in range(TILES):
            mean, rstd, _ = self.columns(step, which, j)
            last = ve.tensor_scalar(tile(out, j), tile(in_, j), mean, rstd, ALU.subtract, ALU.mult)
        return last

    def apply_scalar(self, act, step, which, out, in_):
        for j in range(TILES):
            _, rstd, shift = self.columns(step, which, j)
            last = act.activation(tile(out, j), tile(in_, j), ACT.Identity, bias=shift, scale=rstd)
        return last


class OldNorms:

    def __init__(self, scope, count, ring, last):
        cols = count * TILES
        self.last = last
        self.cols, self.ring_n = cols, ring
        self.stats = scope.sb("stats", [P, cols, 6])
        self.work = scope.sb("norm_work", [P, 4, cols])
        self.result = scope.ring("norm_result", ring, (P, 3, cols))
        self.sem = scope.sem("norm_link")
        self.init = scope.sem("norm_init")

    def prepare(self, ve):
        ve.memset(self.stats[:, :, :], 1.0).then_inc(self.init, 1)
        ve.wait_ge(self.init, 1)

    def take(self, ve, which, buf):
        for j in range(TILES):
            last = ve.bn_stats(self.stats[:, which * TILES + j, :], tile(buf, j))
        return last

    def finish(self, ve, step, measured):
        if isinstance(step.i, int) and step.i > self.last:
            return
        for sem, item in measured:
            need(ve, sem, item)
        link = Link(ve, self.sem, step.i * NORM_LINKS)
        s = self.stats
        t, v, half, d = (self.work[:, k, :] for k in range(4))
        mean, rstd, shift = (self.result[step.offset % self.ring_n][:, k, :] for k in range(3))
        link(ve.tensor_tensor(mean, s[:, :, 1], s[:, :, 4], ALU.add))
        link(ve.tensor_tensor(d, s[:, :, 1], s[:, :, 4], ALU.subtract))
        link(ve.tensor_tensor(v, s[:, :, 2], s[:, :, 5], ALU.add))
        link(ve.tensor_tensor(d, d, d, ALU.mult))
        link(ve.scalar_tensor_tensor(out=v, in0=d, scalar=P / 4.0, in1=v, op0=ALU.mult, op1=ALU.add))
        link(ve.tensor_scalar(v, v, 1.0 / P, EPS, ALU.mult, ALU.add))
        link(ve.tensor_scalar(half, v, -0.5, None, ALU.mult))
        link(ve.tensor_scalar(mean, mean, 0.5, None, ALU.mult))
        rsqrt(ve, link, rstd, v, half, t)
        link(ve.scalar_tensor_tensor(out=shift, in0=mean, scalar=-1.0, in1=rstd, op0=ALU.mult, op1=ALU.mult))

    def ready(self, engine, step):
        done = min(step.i, self.last + 1) if isinstance(step.i, int) else step.i
        engine.wait_ge(self.sem, done * NORM_LINKS)

    def columns(self, step, which, j):
        r = self.result[(step.offset - 1) % self.ring_n]
        c = which * TILES + j
        return [r[:, k, c:c + 1] for k in range(3)]

    def apply_vector(self, ve, step, which, out, in_):
        for j in range(TILES):
            mean, rstd, _ = self.columns(step, which, j)
            last = ve.tensor_scalar(tile(out, j), tile(in_, j), mean, rstd, ALU.subtract, ALU.mult)
        return last

    def apply_scalar(self, act, step, which, out, in_):
        for j in range(TILES):
            _, rstd, shift = self.columns(step, which, j)
            last = act.activation(tile(out, j), tile(in_, j), ACT.Identity, bias=shift, scale=rstd)
        return last


class Shared:
    pass


def node_rows(table, item):
    return table[bass.ds(item.n * GROUP, GROUP), :].rearrange("(p j) d -> p j d", j=TILES)


def edge_rows(table, item, first=NPAD):
    return table[bass.ds(item.n * GROUP + first, GROUP), :].rearrange("(j p) d -> p j d", p=P)


def as_tiles(buf):
    return buf[:, :].rearrange("p (j d) -> p j d", j=TILES)


def wide(buf, half):
    return buf[:, :, half * P:(half + 1) * P]


def setup_phase(nc, sh, dram):
    with ExitStack() as stack:
        s = Scope(nc, stack, "set")
        dst_bc = s.sb("dst_bc", [P, EPAD], I32)
        count_bc = s.sb("count_bc", [P, EPAD])
        next_cols = s.sb("next_cols", [P, ECOLS], I32)
        map_init = s.sb("map_init", [P, NPAD // P, 2])
        node_ids = s.sb("node_ids", [P, NPAD // P], I32)
        slot_ids = s.sb("slot_ids", [P, ECOLS], I32)
        counts = s.sb("counts", [P, ECOLS])
        skip = s.sb("skip", [P, ECOLS])
        ones_row = s.sb("ones_row", [P, 1])
        banks = [s.bank(f"fold{k}") for k in range(5)]
        top_out = s.sb("top_out", [P, P])
        loaded, ids, built, init_stored = s.sem("loaded"), s.sem("ids"), s.sem("built"), s.sem("init_stored")
        count_stored, counts_back = s.sem("count_stored"), s.sem("counts_back")
        ident_done, folded, fold_read = s.sem("ident_done"), s.sem("folded"), s.sem("fold_read")
        mat, vcol, vrow = sh.mat, sh.vcol, sh.vrow
        with nc.Block() as block:

            @block.sync
            def _(sp):
                sp.sem_inc(sh.started, 1)
                sp.dma_start(dst_bc[:, :], dram.dst_row.to_broadcast([P, EPAD])).then_inc(loaded, 16)
                sp.dma_start(next_cols[:, :], dram.next_cols).then_inc(loaded, 16)
                sp.dma_start(sh.src_cols[:, :], dram.src_cols).then_inc(loaded, 16)
                sp.dma_start(sh.dst_cols[:, :], dram.dst_cols).then_inc(loaded, 16)
                sp.dma_start(sh.mats[:, :], dram.mats).then_inc(loaded, 16)
                sp.dma_start(sh.vcols[:, :], dram.vcols).then_inc(loaded, 16)
                sp.dma_start(sh.vrows[:, :], dram.vrows.to_broadcast([P, len(VECS) * P])).then_inc(loaded, 16)
                sp.wait_ge(built, 1)
                sp.dma_start(dram.map[0:NPAD, :].rearrange("(p c) t -> p (c t)", p=P),
                             map_init[:, :, :].rearrange("p c t -> p (c t)")).then_inc(init_stored, 16)
                sp.wait_ge(built, 2)
                sp.dma_start(dram.count_row, count_bc[0:1, :]).then_inc(count_stored, 16)
                sp.wait_ge(count_stored, 16)
                with nc.allow_non_contiguous_dma(reason="12800 counts, once"):
                    sp.dma_start(counts[:, :], dram.count_row.rearrange("a (c p) -> p (a c)", p=P))\
                      .then_inc(counts_back, 16)
                sp.wait_ge(init_stored, 16)

            @block.gpsimd
            def _(pool):
                pool.iota(node_ids[:, :], pattern=[[1, NPAD // P]], base=0, channel_multiplier=NPAD // P)\
                    .then_inc(ids, 1)
                pool.iota(slot_ids[:, :], pattern=[[P, ECOLS]], base=NPAD, channel_multiplier=1).then_inc(ids, 1)
                pool.memset(sh.ident[:, :], 0.0).then_inc(ident_done, 1)
                pool.wait_ge(ident_done, 1)
                pool.affine_select(out=sh.ident[:, :], in_=sh.ident[:, :], compare_op=ALU.not_equal, fill=1.0,
                                   base=0, pattern=[[-1, P]], channel_multiplier=1).then_inc(ident_done, 1)

            @block.vector
            def _(ve):
                link = Link(ve, s.sem("link"), 0)
                ve.wait_ge(ids, 2)
                link(ve.memset(map_init[:, :, 1], 1.0))
                link(ve.tensor_copy(map_init[:, :, 0], node_ids[:, :]))
                ve.nop().then_inc(built, 1)
                link(ve.memset(ones_row[:, :], 1.0))
                link(ve.memset(sh.same[:, 0:1], 0.0))
                ve.wait_ge(loaded, 16 * 7)
                link(ve.tensor_tensor(sh.same[:, 1:EPAD], dst_bc[:, 1:EPAD], dst_bc[:, 0:EPAD - 1], ALU.is_equal))
                link(ve.tensor_tensor_scan(count_bc[:, :], sh.same[:, :], ones_row[:, 0:1].to_broadcast([P, EPAD]),
                                           0.0, ALU.mult, ALU.add))
                ve.nop().then_inc(built, 1)
                link(ve.tensor_tensor(sh.is_rep[:, :], sh.dst_cols[:, :], next_cols[:, :], ALU.not_equal))
                link(ve.tensor_scalar(skip[:, :], sh.is_rep[:, :], -float(SKIP), float(SKIP), ALU.mult, ALU.add))
                link(ve.tensor_tensor(sh.rep_rows[:, :], sh.dst_cols[:, :], skip[:, :], ALU.add))
                ve.wait_ge(counts_back, 16)
                link(ve.tensor_scalar(sh.map_rows[:, :, 1], counts[:, :], 1.0, None, ALU.add))
                link(ve.tensor_copy(sh.map_rows[:, :, 0], slot_ids[:, :]))
                link(ve.tensor_tensor(sh.ln1_b_f2[:, :], vrow["ln1_b"], vrow["f2_b"], ALU.add))
                link(ve.tensor_tensor(sh.att_both[:, 2, :], vcol["att_src"].to_broadcast([P, P]),
                                      vcol["att_dst"].to_broadcast([P, P]), ALU.add))
                link(ve.tensor_copy(sh.att_both[:, 0, :], vcol["att_src"].to_broadcast([P, P])))
                link(ve.tensor_copy(sh.att_both[:, 1, :], vcol["att_dst"].to_broadcast([P, P])))
                for k, (out, bank) in enumerate(zip([top_out, sh.fold_bot], banks)):
                    ve.wait_ge(folded, k + 1)
                    link(ve.tensor_copy(out[:, :], tile(bank, 0)))
                ve.nop().then_inc(fold_read, 1)
                link(ve.tensor_copy(sh.bc_cols[:, 0, :], vcol["b_in"].to_broadcast([P, P])))
                link(ve.tensor_copy(sh.bc_cols[:, 1, :], vcol["b_upd"].to_broadcast([P, P])))
                ve.nop().then_inc(fold_read, 1)
                ve.wait_ge(folded, 3)
                link(ve.tensor_tensor(sh.fold_self[:, :], tile(banks[2], 0), sh.ident[:, :], ALU.add))
                ve.wait_ge(folded, 4)
                link(ve.tensor_tensor(sh.fold_bias[:, :], tile(banks[3], 0), vrow["b_out"], ALU.add))

            @block.tensor
            def _(pe):
                pe.wait_ge(loaded, 16 * 7)
                pe.matmul(tile(banks[0], 0), mat["W_topT"], mat["W_out"], start=True, stop=True).then_inc(folded, 1)
                pe.matmul(tile(banks[1], 0), mat["W_botT"], mat["W_out"], start=True, stop=True).then_inc(folded, 1)
                pe.wait_ge(fold_read, 1)
                pe.wait_ge(ident_done, 2)
                pe.matmul(tile(banks[2], 0), mat["W_inT"], top_out[:, :], start=True, stop=True).then_inc(folded, 1)
                pe.wait_ge(fold_read, 2)
                pe.matmul(tile(banks[3], 0), sh.bc_cols[:, 0, :], top_out[:, :], start=True, stop=False)
                pe.matmul(tile(banks[3], 0), sh.bc_cols[:, 1, :], mat["W_out"], start=False, stop=True)\
                  .then_inc(folded, 1)


def map_phase(nc, sh, dram):
    with ExitStack() as stack:
        s = Scope(nc, stack, "map")
        R = 4
        idx = s.ring("idx", R, (P, TILES), I32)
        rows = s.ring("rows", R, (P, TILES, 2))
        copied, scattered = s.sem("copied"), s.sems("scattered", R)
        with nc.Block() as block:

            @block.gpsimd
            def _(pool):
                def scatter(step):
                    it = step.item(0)
                    need_dma(pool, scattered, it, 1, TILES)
                    cols = bass.ds(it.n * TILES, TILES)
                    pool.tensor_copy(idx[it.slot][:, :], sh.rep_rows[:, cols])
                    pool.tensor_copy(rows[it.slot][:, :, :], sh.map_rows[:, cols, :]).then_inc(copied, 1)
                    need_apart(pool, sh.started, copied, it)
                    for j in range(TILES):
                        pool.indirect_dma_start(dram.map, bass.IndirectOffsetOnAxis(ap=idx[it.slot][:, j:j + 1], axis=0),
                                                rows[it.slot][:, j, :], None, bounds_check=NPAD - 1,
                                                oob_is_err=False).then_inc(scattered[it.slot], 16)

                run_steps(pool, CHUNKS, 0, R, scatter)
                for k in range(R):
                    pool.wait_ge(scattered[k], 16 * TILES * len(range(k, CHUNKS, R)))

    with ExitStack() as stack:
        s = Scope(nc, stack, "look")
        R = 2
        ends = (("src", sh.src_cols, sh.src_map), ("dst", sh.dst_cols, sh.dst_map))
        idx = {e: s.ring(f"idx_{e}", R, (P, TILES), I32) for e, _, _ in ends}
        got = {e: s.ring(f"got_{e}", R, (P, TILES, 2)) for e, _, _ in ends}
        idx_copied, gathered, kept = s.sem("idx_copied"), s.sems("gathered", R), s.sem("kept")
        done = s.sem("done")
        with nc.Block() as block:

            @block.gpsimd
            def _(pool):
                def lookup(step):
                    it = step.item(0)
                    need(pool, kept, it, R)
                    cols = bass.ds(it.n * TILES, TILES)
                    for e, all_cols, _ in ends:
                        last = pool.tensor_copy(idx[e][it.slot][:, :], all_cols[:, cols])
                    last.then_inc(idx_copied, 1)
                    need_apart(pool, sh.started, idx_copied, it)
                    for e, _, _ in ends:
                        for j in range(TILES):
                            pool.indirect_dma_start(got[e][it.slot][:, j, :], None, dram.map,
                                                    bass.IndirectOffsetOnAxis(ap=idx[e][it.slot][:, j:j + 1], axis=0))\
                                .then_inc(gathered[it.slot], 16)

                run_steps(pool, CHUNKS, 0, R, lookup)
                pool.wait_ge(done, 17)
                last = sh.alone[:, (GROUPS - 1) * TILES:GROUPS * TILES]
                pool.affine_select(out=last, in_=last, compare_op=ALU.is_gt, fill=0.0,
                                   base=NODES - (GROUPS - 1) * GROUP, pattern=[[-1, TILES]],
                                   channel_multiplier=-TILES).then_inc(done, 1)
                pool.wait_ge(done, 18)

            @block.vector
            def _(ve):
                def keep(step):
                    it = step.item(0)
                    need_dma(ve, gathered, it, 0, 2 * TILES)
                    cols = bass.ds(it.n * TILES, TILES)
                    for e, _, out in ends:
                        last = ve.tensor_copy(out[:, cols, :], got[e][it.slot][:, :, :])
                    last.then_inc(kept, 1)

                run_steps(ve, CHUNKS, 0, R, keep)
                ve.wait_ge(kept, CHUNKS)
                link = Link(ve, s.sem("link"), 0)
                v, half, t = (s.sb(n, [P, ECOLS]) for n in ("v", "half", "t"))
                for (_, _, m), row, root in zip(ends, (sh.src_row, sh.dst_row), (sh.src_root, sh.dst_root)):
                    link(ve.tensor_copy(row[:, :], m[:, :, 0]))
                    link(ve.tensor_copy(v[:, :], m[:, :, 1]))
                    link(ve.tensor_scalar(half[:, :], v[:, :], -0.5, None, ALU.mult))
                    rsqrt(ve, link, root[:, :], v[:, :], half[:, :], t[:, :])

            @block.sync
            def _(sp):
                deg = s.sb("deg", [P, GROUPS, TILES, 2])
                sp.dma_start(deg[:, :, :, :], dram.map[0:NPAD, :].rearrange("(g p j) t -> p g (j t)", p=P, j=TILES)
                             .rearrange("p g (j t) -> p g j t", j=TILES)).then_inc(done, 16)
                sh.deg_loaded = deg
                sp.wait_ge(done, 16)

            @block.scalar
            def _(act):
                act.wait_ge(done, 16)
                act.activation(sh.alone[:, :].rearrange("p (g j) -> p g j", j=TILES), sh.deg_loaded[:, :, :, 1], ACT.Relu, bias=sh.two[:, :], scale=-1.0)\
                   .then_inc(done, 1)
                act.wait_ge(done, 17)



def dense_front_phase(nc, sh, dram):
    with ExitStack() as stack:
        s = Scope(nc, stack, "fr")
        R = 4
        T_X, MM1, MM2, NORM1, T_X1, MM3, MM4, NORM2, T_X2, MMH, SUM = 1, 2, 3, 4, 5, 6, 7, 8, 9, 10, 11
        LAGS = SUM
        mat, vcol = sh.mat, sh.vcol
        xin, x1, x1b, h2 = (s.ring(n, R) for n in ("xin", "x1", "x1b", "h2"))
        xb, xT, r1a, r1b, pre1, x1T, r3, pre2, x2T, sq = (s.pair(n, R) for n in (
            "xb", "xT", "r1a", "r1b", "pre1", "x1T", "r3", "pre2", "x2T", "sq"))
        x2h = s.ring("x2h", R, (P, TILES, 2 * P))
        norms = Norms(s, 2, GROUPS - 1 + NORM2)
        bT, bMa, bMb, bC, bD, bE, bF, bH = (s.bank(n) for n in ("T", "Ma", "Mb", "C", "D", "E", "F", "H"))
        x_loaded, h2_stored, x1_stored, x2h_stored = (s.sems(n, R) for n in ("xld", "h2st", "x1st", "x2hst"))
        names = ["x_T", "xT_out", "xb_done", "mm1", "relu1", "mm2", "h2_out", "pre1_done", "meas1", "x1_done", "x1_T",
                 "x1T_out", "x1b_done", "mm3", "relu3", "mm4", "pre2_done", "meas2", "x2_done", "x2_T", "x2T_out",
                 "mmh", "h_out", "sq_out", "summed"]
        q = {n: s.sem(n) for n in names}
        with nc.Block() as block:

            @block.sync
            def _(sp):
                def step(st):
                    if it := st.item(0):
                        need(sp, q["x_T"], it, R)
                        need(sp, q["xb_done"], it, R)
                        sp.dma_start(as_tiles(xin[it.slot]), node_rows(dram.x, it)).then_inc(x_loaded[it.slot], 16)
                    if it := st.item(MM2):
                        need(sp, q["h2_out"], it)
                        sp.dma_start(node_rows(dram.h2, it), as_tiles(h2[it.slot])).then_inc(h2_stored[it.slot], 16)
                    if it := st.item(NORM1):
                        need(sp, q["x1_done"], it)
                        sp.dma_start(node_rows(dram.x1, it), as_tiles(x1[it.slot])).then_inc(x1_stored[it.slot], 16)
                    if it := st.item(MMH):
                        need(sp, q["x2_done"], it)
                        need(sp, q["h_out"], it)
                        sp.dma_start(node_rows(dram.x2h, it), x2h[it.slot][:, :, :]).then_inc(x2h_stored[it.slot], 16)

                run_steps(sp, GROUPS, LAGS, R, step)
                for sems in (h2_stored, x1_stored, x2h_stored):
                    for k in range(R):
                        sp.wait_ge(sems[k], 16 * len(range(k, GROUPS, R)))

            @block.gpsimd
            def _(pool):
                def step(st):
                    if it := st.item(MM1):
                        need_dma(pool, x_loaded, it)
                        need(pool, q["pre1_done"], it, 2)
                        pool.tensor_tensor(xb[it.slot][:, :], xin[it.slot][:, :], sh.b2_4[:, :], ALU.add)\
                            .then_inc(q["xb_done"], 1)
                    if it := st.item(T_X1):
                        need(pool, q["x1_done"], it)
                        need(pool, q["pre2_done"], it, R)
                        pool.tensor_tensor(x1b[it.slot][:, :], x1[it.slot][:, :], sh.l1b2_4[:, :], ALU.add)\
                            .then_inc(q["x1b_done"], 1)

                run_steps(pool, GROUPS, LAGS, R, step)

            @block.tensor
            def _(pe):
                def step(st):
                    if it := st.item(T_X):
                        need_dma(pe, x_loaded, it)
                        need(pe, q["xT_out"], it, 1)
                        if other := st.item(T_X2 + 1):
                            need(pe, q["x2T_out"], other)
                        transpose4(pe, bT, xin[it.slot], sh.ident[:, :]).then_inc(q["x_T"], 1)
                    if it := st.item(MM1):
                        need(pe, q["xT_out"], it)
                        need(pe, q["relu1"], it, 1)
                        pe.matmul(bMa[:, :], mat["L0_W1a"], xT[it.slot][:, :], start=True, stop=True)
                        pe.matmul(bMb[:, :], mat["L0_W1b"], xT[it.slot][:, :], start=True, stop=True)\
                          .then_inc(q["mm1"], 1)
                    if it := st.item(MM2):
                        need(pe, q["relu1"], it)
                        need(pe, q["h2_out"], it, 1)
                        product_nm(pe, bC, [(r1a[it.slot], mat["L0_W2a"]), (r1b[it.slot], mat["L0_W2b"])])\
                            .then_inc(q["mm2"], 1)
                    if it := st.item(T_X1):
                        need(pe, q["x1_done"], it)
                        need(pe, q["x1T_out"], it, 1)
                        transpose4(pe, bD, x1[it.slot], sh.ident[:, :]).then_inc(q["x1_T"], 1)
                    if it := st.item(MM4):
                        need(pe, q["relu3"], it)
                        need(pe, q["pre2_done"], it, 1)
                        product_nm(pe, bF, [(r3[it.slot], mat["L1_W2"])]).then_inc(q["mm4"], 1)
                    if it := st.item(MM3):
                        need(pe, q["x1T_out"], it)
                        need(pe, q["relu3"], it, 1)
                        pe.matmul(bE[:, :], mat["L1_W1"], x1T[it.slot][:, :], start=True, stop=True)\
                          .then_inc(q["mm3"], 1)
                    if it := st.item(MMH):
                        need(pe, q["x2T_out"], it)
                        need(pe, q["sq_out"], it, 1)
                        product_nm(pe, bH, [(x2T[it.slot], mat["L2_W"])]).then_inc(q["mmh"], 1)
                    if it := st.item(T_X2):
                        need(pe, q["x2_done"], it)
                        need(pe, q["x2T_out"], it, 1)
                        if other := st.item(T_X):
                            need(pe, q["xT_out"], other)
                        for j in range(TILES):
                            last = pe.transpose(tile(bT, j), wide(x2h[it.slot], 0)[:, j, :], sh.ident[:, :])
                        last.then_inc(q["x2_T"], 1)

                run_steps(pe, GROUPS, LAGS, R, step)

            @block.scalar
            def _(act):
                def step(st):
                    if it := st.item(T_X):
                        need(act, q["x_T"], it)
                        need(act, q["mm1"], it, 2)
                        act.activation(xT[it.slot][:, :], bT[:, :], ACT.Copy).then_inc(q["xT_out"], 1)
                    if it := st.item(MM1):
                        need(act, q["mm1"], it)
                        need(act, q["mm2"], it, 2)
                        act.activation(r1a[it.slot][:, :], bMa[:, :], ACT.Relu, bias=vcol["L0_b1a"])
                        act.activation(r1b[it.slot][:, :], bMb[:, :], ACT.Relu, bias=vcol["L0_b1b"])\
                           .then_inc(q["relu1"], 1)
                    if it := st.item(MM2):
                        need(act, q["mm2"], it)
                        need_dma(act, h2_stored, it, 1)
                        need(act, q["pre1_done"], it, R)
                        act.activation(h2[it.slot][:, :], bC[:, :], ACT.Copy).then_inc(q["h2_out"], 1)
                    if it := st.item(T_X1):
                        need(act, q["x1_T"], it)
                        need(act, q["mm3"], it, 2)
                        act.activation(x1T[it.slot][:, :], bD[:, :], ACT.Copy).then_inc(q["x1T_out"], 1)
                    if it := st.item(MM3):
                        need(act, q["mm3"], it)
                        need(act, q["mm4"], it, 2)
                        act.activation(r3[it.slot][:, :], bE[:, :], ACT.Relu, bias=vcol["L1_b1"])\
                           .then_inc(q["relu3"], 1)
                    if it := st.item(MMH):
                        need(act, q["mmh"], it)
                        need(act, q["summed"], it, 2)
                        act.activation(wide(x2h[it.slot], 1), as_tiles(bH), ACT.Copy).then_inc(q["h_out"], 1)
                        act.activation(sq[it.slot][:, :], bH[:, :], ACT.Square).then_inc(q["sq_out"], 1)
                    if it := st.item(T_X2):
                        need(act, q["x2_T"], it)
                        need(act, q["mmh"], it, 2)
                        act.activation(x2T[it.slot][:, :], bT[:, :], ACT.Copy).then_inc(q["x2T_out"], 1)
                    if it := st.item(NORM2):
                        norms.ready(act, st)
                        need_dma(act, x2h_stored, it, 1)
                        need(act, q["summed"], it, R)
                        for j in range(TILES):
                            _, rstd, shift = norms.columns(st, 1, j)
                            last = act.activation(wide(x2h[it.slot], 0)[:, j, :], tile(pre2[it.slot], j), ACT.Identity,
                                                  bias=shift, scale=rstd)
                        last.then_inc(q["x2_done"], 1)

                run_steps(act, GROUPS, LAGS, R, step)

            @block.vector
            def _(ve):
                norms.prepare(ve)

                def step(st):
                    chain = norms.chain(ve, st, [(q["meas1"], st.item(MM2 + 1)), (q["meas2"], st.item(MM4 + 1))])
                    if it := st.item(SUM):
                        need(ve, q["h_out"], it)
                        need(ve, q["sq_out"], it)
                        need(ve, q["summed"], it, 1)
                        for j in range(TILES):
                            alone = sh.alone[:, bass.ds(it.n * TILES + j, 1)]
                            ve.scalar_tensor_tensor(out=sh.sum1[:, j, :], in0=wide(x2h[it.slot], 1)[:, j, :],
                                                    scalar=alone, in1=sh.sum1[:, j, :], op0=ALU.mult, op1=ALU.add)
                            next(chain, None)
                            last = ve.scalar_tensor_tensor(out=sh.sum2[:, j, :], in0=tile(sq[it.slot], j),
                                                           scalar=alone, in1=sh.sum2[:, j, :], op0=ALU.mult,
                                                           op1=ALU.add)
                            if j < TILES - 1:
                                next(chain, None)
                        last.then_inc(q["summed"], 1)
                        next(chain, None)
                    if it := st.item(MM2):
                        need(ve, q["h2_out"], it)
                        need(ve, q["xb_done"], it)
                        need(ve, q["x1_done"], it, 2)
                        ve.tensor_tensor(pre1[it.slot][:, :], h2[it.slot][:, :], xb[it.slot][:, :], ALU.add)\
                          .then_inc(q["pre1_done"], 1)
                        next(chain, None)
                        need(ve, q["pre1_done"], it)
                        norms.take(ve, st, 0, pre1[it.slot], chain).then_inc(q["meas1"], 1)
                    if it := st.item(MM4):
                        need(ve, q["mm4"], it)
                        need(ve, q["x1b_done"], it)
                        need(ve, q["x2_done"], it, 2)
                        ve.tensor_tensor(pre2[it.slot][:, :], bF[:, :], x1b[it.slot][:, :], ALU.add)\
                          .then_inc(q["pre2_done"], 1)
                        next(chain, None)
                        need(ve, q["pre2_done"], it)
                        norms.take(ve, st, 1, pre2[it.slot], chain).then_inc(q["meas2"], 1)
                    for _ in chain:
                        pass
                    if it := st.item(NORM1):
                        norms.ready(ve, st)
                        need_dma(ve, x1_stored, it, 1)
                        need(ve, q["x1_T"], it, R)
                        need(ve, q["x1b_done"], it, R)
                        norms.apply_vector(ve, st, 0, x1[it.slot], pre1[it.slot]).then_inc(q["x1_done"], 1)

                run_steps(ve, GROUPS, LAGS, R, step)


class Gathers:

    def __init__(self, scope, started, name, table, columns, width, ring):
        self.table, self.columns, self.ring, self.started = table, columns, ring, started
        self.idx = scope.ring(f"{name}_idx", ring, (P, TILES), I32)
        self.rows = scope.ring(f"{name}_rows", ring, (P, TILES, width))
        self.copied = scope.sem(f"{name}_copied")
        self.landed = scope.sems(f"{name}_landed", ring)

    def issue(self, pool, it):
        pool.tensor_copy(self.idx[it.slot][:, :], self.columns[:, bass.ds(it.n * TILES, TILES)])\
            .then_inc(self.copied, 1)
        need_apart(pool, self.started, self.copied, it)
        for j in range(TILES):
            pool.indirect_dma_start(self.rows[it.slot][:, j, :], None, self.table,
                                    bass.IndirectOffsetOnAxis(ap=self.idx[it.slot][:, j:j + 1], axis=0))\
                .then_inc(self.landed[it.slot], 16)

    def wait(self, engine, it, back=0):
        need_dma(engine, self.landed, it, back, TILES)


def flat(rows):
    return rows[:, :, :].rearrange("p j d -> p (j d)")


def segment_sum(ve, it, sums, same, values):
    start = 0.0
    if not (isinstance(it.n, int) and it.n == 0):
        start = sums[(it.slot - 1) % len(sums)][:, GROUP - 1:GROUP]
    return ve.tensor_tensor_scan(sums[it.slot][:, :], same, values, start, ALU.mult, ALU.add)


def column(cols, it, j):
    return cols[:, bass.ds(it.n * TILES + j, 1)]


def edge_gcn1_phase(nc, sh, dram):
    with ExitStack() as stack:
        s = Scope(nc, stack, "e1")
        R, LAGS = 2, 2
        mat, vcol = sh.mat, sh.vcol
        src, dst = Gathers(s, sh.started, "src", dram.x, sh.src_cols, P, R), Gathers(s, sh.started, "dst", dram.x, sh.dst_cols, P, R)
        sums, v, u, uT, r1a, r1b, h2s, xob = (s.ring(n, R) for n in ("sums", "v", "u", "uT", "r1a", "r1b", "h2s", "xob"))
        bS, bA, bU, bMa, bMb, bH = (s.bank(n) for n in ("S", "A", "U", "Ma", "Mb", "H"))
        h2_stored, xob_stored = s.sems("h2st", R), s.sems("xobst", R)
        q = {n: s.sem(n) for n in ["scaled", "src_T", "summed", "sum_T", "v_done", "u_done", "u_T", "uT_out", "mm1",
                                   "relu1", "mm2", "h2_out", "xob_done"]}
        with nc.Block() as block:

            @block.gpsimd
            def _(pool):
                def step(st):
                    if it := st.item(0):
                        need(pool, q["src_T"], it, R)
                        src.issue(pool, it)
                        need(pool, q["v_done"], it, R)
                        need(pool, q["xob_done"], it, R)
                        dst.issue(pool, it)

                run_steps(pool, CHUNKS, LAGS, R, step)

            @block.vector
            def _(ve):
                def step(st):
                    if it := st.item(1):
                        src.wait(ve, it)
                        g = src.rows[it.slot]
                        for j in range(TILES):
                            last = ve.tensor_scalar(g[:, j, :], g[:, j, :], column(sh.src_root, it, j), None, ALU.mult)
                        last.then_inc(q["scaled"], 1)
                        dst.wait(ve, it)
                        need_dma(ve, xob_stored, it, 1)
                        ve.tensor_tensor(xob[it.slot][:, :], flat(dst.rows[it.slot]), sh.b2_4[:, :], ALU.add)\
                          .then_inc(q["xob_done"], 1)
                        need(ve, q["src_T"], it)
                        need(ve, q["sum_T"], it, R)
                        need(ve, q["summed"], it, 1)
                        segment_sum(ve, it, sums, sh.same[:, bass.ds(it.n * GROUP, GROUP)], bS[:, :])\
                            .then_inc(q["summed"], 1)
                        need(ve, q["sum_T"], it)
                        need(ve, q["u_done"], it, R)
                        for j in range(TILES):
                            last = ve.scalar_tensor_tensor(out=tile(v[it.slot], j), in0=dst.rows[it.slot][:, j, :],
                                                           scalar=column(sh.dst_root, it, j), in1=tile(bA, j),
                                                           op0=ALU.mult, op1=ALU.add)
                        last.then_inc(q["v_done"], 1)

                run_steps(ve, CHUNKS, LAGS, R, step)

            @block.scalar
            def _(act):
                def step(st):
                    if it := st.item(2):
                        need(act, q["u_T"], it)
                        need(act, q["mm1"], it, R)
                        act.activation(uT[it.slot][:, :], bU[:, :], ACT.Copy).then_inc(q["uT_out"], 1)
                        need(act, q["mm1"], it)
                        need(act, q["mm2"], it, R)
                        act.activation(r1a[it.slot][:, :], bMa[:, :], ACT.Relu, bias=vcol["L0_b1a"])
                        act.activation(r1b[it.slot][:, :], bMb[:, :], ACT.Relu, bias=vcol["L0_b1b"])\
                           .then_inc(q["relu1"], 1)
                        act.wait_ge(sh.started, 1)
                        need(act, q["mm2"], it)
                        need_dma(act, h2_stored, it, 1)
                        for j in range(TILES):
                            last = act.activation(tile(h2s[it.slot], j), tile(bH, j), ACT.Copy,
                                                  scale=column(sh.dst_root, it, j))
                        last.then_inc(q["h2_out"], 1)
                    if it := st.item(1):
                        act.wait_ge(sh.started, 1)
                        need(act, q["v_done"], it)
                        need(act, q["u_T"], it, R)
                        for j in range(TILES):
                            last = act.activation(tile(u[it.slot], j), tile(v[it.slot], j), ACT.Copy,
                                                  scale=column(sh.dst_root, it, j))
                        last.then_inc(q["u_done"], 1)

                run_steps(act, CHUNKS, LAGS, R, step)

            @block.tensor
            def _(pe):
                def step(st):
                    if it := st.item(1):
                        need(pe, q["scaled"], it)
                        need(pe, q["summed"], it, 1)
                        transpose4(pe, bS, flat(src.rows[it.slot]), sh.ident[:, :]).then_inc(q["src_T"], 1)
                    if it := st.item(2):
                        need(pe, q["u_done"], it)
                        need(pe, q["uT_out"], it, 1)
                        transpose4(pe, bU, u[it.slot], sh.ident[:, :]).then_inc(q["u_T"], 1)
                        need(pe, q["uT_out"], it)
                        need(pe, q["relu1"], it, 1)
                        pe.matmul(bMa[:, :], mat["L0_W1a"], uT[it.slot][:, :], start=True, stop=True)
                        pe.matmul(bMb[:, :], mat["L0_W1b"], uT[it.slot][:, :], start=True, stop=True)\
                          .then_inc(q["mm1"], 1)
                    if it := st.item(1):
                        need(pe, q["summed"], it)
                        need(pe, q["v_done"], it, 1)
                        transpose4(pe, bA, sums[it.slot], sh.ident[:, :]).then_inc(q["sum_T"], 1)
                    if it := st.item(2):
                        need(pe, q["relu1"], it)
                        need(pe, q["h2_out"], it, 1)
                        product_nm(pe, bH, [(r1a[it.slot], mat["L0_W2a"]), (r1b[it.slot], mat["L0_W2b"])])\
                            .then_inc(q["mm2"], 1)

                run_steps(pe, CHUNKS, LAGS, R, step)

            @block.sync
            def _(sp):
                def step(st):
                    if it := st.item(1):
                        need(sp, q["xob_done"], it)
                        sp.dma_start(edge_rows(dram.x_own, it, 0), as_tiles(xob[it.slot])).then_inc(xob_stored[it.slot], 16)
                    if it := st.item(2):
                        need(sp, q["h2_out"], it)
                        sp.dma_start(edge_rows(dram.h2, it), as_tiles(h2s[it.slot])).then_inc(h2_stored[it.slot], 16)

                run_steps(sp, CHUNKS, LAGS, R, step)
                for sems in (xob_stored, h2_stored):
                    for k in range(R):
                        sp.wait_ge(sems[k], 16 * len(range(k, CHUNKS, R)))


def edge_gcn2_phase(nc, sh, dram):
    with ExitStack() as stack:
        s = Scope(nc, stack, "e2")
        R, LAGS = 2, 3
        src = Gathers(s, sh.started, "src", dram.h2, sh.src_row, P, R)
        sums, xob, h2o, w, pre, x1 = (s.ring(n, R) for n in ("sums", "xob", "h2o", "w", "pre", "x1"))
        xob, h2o = s.ring("xob3", 4), s.ring("h2o3", 4)
        norms = OldNorms(s, 1, R, CHUNKS - 1 + 2)
        bS, bA = s.bank("S"), s.bank("A")
        own_loaded, x1_stored = s.sems("ownld", R), s.sems("x1st", R)
        q = {n: s.sem(n) for n in ["src_T", "summed", "sum_T", "w_done", "pre_done", "meas", "x1_done"]}
        xob, h2o = xob[:R], h2o[:R]
        with nc.Block() as block:

            @block.gpsimd
            def _(pool):
                def step(st):
                    if it := st.item(0):
                        need(pool, q["src_T"], it, R)
                        src.issue(pool, it)

                run_steps(pool, CHUNKS, LAGS, R, step)

            @block.sync
            def _(sp):
                def step(st):
                    if it := st.item(1):
                        need(sp, q["pre_done"], it, R)
                        sp.dma_start(as_tiles(xob[it.slot]), edge_rows(dram.x_own, it, 0)).then_inc(own_loaded[it.slot], 16)
                        sp.dma_start(as_tiles(h2o[it.slot]), edge_rows(dram.h2, it)).then_inc(own_loaded[it.slot], 16)
                    if it := st.item(3):
                        need(sp, q["x1_done"], it)
                        sp.dma_start(edge_rows(dram.x1, it), as_tiles(x1[it.slot])).then_inc(x1_stored[it.slot], 16)

                run_steps(sp, CHUNKS, LAGS, R, step)
                for k in range(R):
                    sp.wait_ge(x1_stored[k], 16 * len(range(k, CHUNKS, R)))

            @block.tensor
            def _(pe):
                def step(st):
                    if it := st.item(1):
                        src.wait(pe, it)
                        need(pe, q["summed"], it, 1)
                        transpose4(pe, bS, flat(src.rows[it.slot]), sh.ident[:, :]).then_inc(q["src_T"], 1)
                        need(pe, q["summed"], it)
                        need(pe, q["w_done"], it, 1)
                        transpose4(pe, bA, sums[it.slot], sh.ident[:, :]).then_inc(q["sum_T"], 1)

                run_steps(pe, CHUNKS, LAGS, R, step)

            @block.vector
            def _(ve):
                norms.prepare(ve)

                def step(st):
                    measured = []
                    if it := st.item(1):
                        need(ve, q["src_T"], it)
                        need(ve, q["sum_T"], it, R)
                        need(ve, q["summed"], it, 1)
                        segment_sum(ve, it, sums, sh.same[:, bass.ds(it.n * GROUP, GROUP)], bS[:, :])\
                            .then_inc(q["summed"], 1)
                    if it := st.item(2):
                        need(ve, q["sum_T"], it)
                        need_dma(ve, own_loaded, it, 0, 2)
                        ve.tensor_tensor(w[it.slot][:, :], bA[:, :], h2o[it.slot][:, :], ALU.add)\
                          .then_inc(q["w_done"], 1)
                        need(ve, q["w_done"], it)
                        need(ve, q["x1_done"], it, R)
                        for j in range(TILES):
                            last = ve.scalar_tensor_tensor(out=tile(pre[it.slot], j), in0=tile(w[it.slot], j),
                                                           scalar=column(sh.dst_root, it, j), in1=tile(xob[it.slot], j),
                                                           op0=ALU.mult, op1=ALU.add)
                        last.then_inc(q["pre_done"], 1)
                        need(ve, q["pre_done"], it)
                        norms.take(ve, 0, pre[it.slot]).then_inc(q["meas"], 1)
                        measured.append((q["meas"], it))
                    norms.finish(ve, st, measured)

                run_steps(ve, CHUNKS, LAGS, R, step)

            @block.scalar
            def _(act):
                def step(st):
                    if it := st.item(3):
                        norms.ready(act, st)
                        need_dma(act, x1_stored, it, 1)
                        norms.apply_scalar(act, st, 0, x1[it.slot], pre[it.slot]).then_inc(q["x1_done"], 1)

                run_steps(act, CHUNKS, LAGS, R, step)


def edge_gine_phase(nc, sh, dram):
    with ExitStack() as stack:
        s = Scope(nc, stack, "e3")
        R, LAGS = 2, 3
        mat, vcol = sh.mat, sh.vcol
        src = Gathers(s, sh.started, "src", dram.x1, sh.src_row, P, R)
        ea, x1o, x1b, sums, uT, r3, pre, x2T = (s.ring(n, R) for n in
                                                ("ea", "x1o", "x1b", "sums", "uT", "r3", "pre", "x2T"))
        x2h = s.ring("x2h", R, (P, TILES, 2 * P))
        norms = OldNorms(s, 1, R, CHUNKS - 1 + 2)
        bS, bO, bE, bF, bT, bH = (s.bank(n) for n in ("S", "O", "E", "F", "T", "H"))
        loaded, stored = s.sems("ld", R), s.sems("st", R)
        q = {n: s.sem(n) for n in ["msg", "msg_relu", "src_T", "own_T", "x1b_done", "summed", "u_done", "mm3", "relu3",
                                   "mm4", "pre_done", "meas", "x2_done", "x2_T", "x2T_out", "mmh", "h_out"]}
        with nc.Block() as block:

            @block.gpsimd
            def _(pool):
                def step(st):
                    if it := st.item(0):
                        need(pool, q["src_T"], it, R)
                        src.issue(pool, it)

                run_steps(pool, CHUNKS, LAGS, R, step)

            @block.sync
            def _(sp):
                def step(st):
                    if it := st.item(0):
                        need(sp, q["msg"], it, R)
                        need(sp, q["own_T"], it, R)
                        need(sp, q["x1b_done"], it, R)
                        sp.dma_start(as_tiles(ea[it.slot]), edge_rows(dram.edge_attr, it, 0)).then_inc(loaded[it.slot], 16)
                        sp.dma_start(as_tiles(x1o[it.slot]), edge_rows(dram.x1, it)).then_inc(loaded[it.slot], 16)
                    if it := st.item(3):
                        need(sp, q["x2_done"], it)
                        need(sp, q["h_out"], it)
                        sp.dma_start(edge_rows(dram.x2h, it), x2h[it.slot][:, :, :]).then_inc(stored[it.slot], 16)

                run_steps(sp, CHUNKS, LAGS, R, step)
                for k in range(R):
                    sp.wait_ge(stored[k], 16 * len(range(k, CHUNKS, R)))

            @block.tensor
            def _(pe):
                def step(st):
                    if it := st.item(1):
                        need_dma(pe, loaded, it, 0, 2)
                        need(pe, q["u_done"], it, 1)
                        transpose4(pe, bO, x1o[it.slot], sh.ident[:, :]).then_inc(q["own_T"], 1)
                    if it := st.item(3):
                        need(pe, q["x2_done"], it)
                        need(pe, q["x2T_out"], it, 1)
                        for j in range(TILES):
                            last = pe.transpose(tile(bT, j), wide(x2h[it.slot], 0)[:, j, :], sh.ident[:, :])
                        last.then_inc(q["x2_T"], 1)
                    if it := st.item(2):
                        need(pe, q["u_done"], it)
                        need(pe, q["relu3"], it, 1)
                        pe.matmul(bE[:, :], mat["L1_W1"], uT[it.slot][:, :], start=True, stop=True)\
                          .then_inc(q["mm3"], 1)
                    if it := st.item(3):
                        need(pe, q["x2T_out"], it)
                        need(pe, q["h_out"], it, 1)
                        product_nm(pe, bH, [(x2T[it.slot], mat["L2_W"])]).then_inc(q["mmh"], 1)
                    if it := st.item(2):
                        need(pe, q["relu3"], it)
                        need(pe, q["pre_done"], it, 1)
                        product_nm(pe, bF, [(r3[it.slot], mat["L1_W2"])]).then_inc(q["mm4"], 1)
                    if it := st.item(1):
                        need(pe, q["msg_relu"], it)
                        need(pe, q["summed"], it, 1)
                        transpose4(pe, bS, flat(src.rows[it.slot]), sh.ident[:, :]).then_inc(q["src_T"], 1)

                run_steps(pe, CHUNKS, LAGS, R, step)

            @block.vector
            def _(ve):
                norms.prepare(ve)

                def step(st):
                    measured = []
                    if it := st.item(1):
                        src.wait(ve, it)
                        need_dma(ve, loaded, it, 0, 2)
                        g = flat(src.rows[it.slot])
                        ve.tensor_tensor(g, g, ea[it.slot][:, :], ALU.add).then_inc(q["msg"], 1)
                        need(ve, q["pre_done"], it, R)
                        ve.tensor_tensor(x1b[it.slot][:, :], x1o[it.slot][:, :], sh.l1b2_4[:, :], ALU.add)\
                          .then_inc(q["x1b_done"], 1)
                    if it := st.item(2):
                        need(ve, q["mm4"], it)
                        need(ve, q["x1b_done"], it)
                        need(ve, q["x2_done"], it, R)
                        ve.tensor_tensor(pre[it.slot][:, :], bF[:, :], x1b[it.slot][:, :], ALU.add)\
                          .then_inc(q["pre_done"], 1)
                        need(ve, q["pre_done"], it)
                        norms.take(ve, 0, pre[it.slot]).then_inc(q["meas"], 1)
                        measured.append((q["meas"], it))
                    if it := st.item(1):
                        need(ve, q["src_T"], it)
                        need(ve, q["summed"], it, 1)
                        need(ve, q["u_done"], it, 1)
                        segment_sum(ve, it, sums, sh.same[:, bass.ds(it.n * GROUP, GROUP)], bS[:, :])\
                            .then_inc(q["summed"], 1)
                        need(ve, q["own_T"], it)
                        need(ve, q["summed"], it)
                        need(ve, q["mm3"], it, R)
                        ve.tensor_tensor(uT[it.slot][:, :], bO[:, :], sums[it.slot][:, :], ALU.add)\
                          .then_inc(q["u_done"], 1)
                    norms.finish(ve, st, measured)

                run_steps(ve, CHUNKS, LAGS, R, step)

            @block.scalar
            def _(act):
                def step(st):
                    if it := st.item(1):
                        need(act, q["msg"], it)
                        g = flat(src.rows[it.slot])
                        act.activation(g, g, ACT.Relu).then_inc(q["msg_relu"], 1)
                    if it := st.item(3):
                        norms.ready(act, st)
                        need_dma(act, stored, it, 1)
                        for j in range(TILES):
                            _, rstd, shift = norms.columns(st, 0, j)
                            last = act.activation(wide(x2h[it.slot], 0)[:, j, :], tile(pre[it.slot], j), ACT.Identity,
                                                  bias=shift, scale=rstd)
                        last.then_inc(q["x2_done"], 1)
                        need(act, q["x2_T"], it)
                        need(act, q["mmh"], it, R)
                        act.activation(x2T[it.slot][:, :], bT[:, :], ACT.Copy).then_inc(q["x2T_out"], 1)
                    if it := st.item(2):
                        need(act, q["mm3"], it)
                        need(act, q["mm4"], it, R)
                        act.activation(r3[it.slot][:, :], bE[:, :], ACT.Relu, bias=vcol["L1_b1"])\
                           .then_inc(q["relu3"], 1)
                    if it := st.item(3):
                        need(act, q["mmh"], it)
                        act.activation(wide(x2h[it.slot], 1), as_tiles(bH), ACT.Copy).then_inc(q["h_out"], 1)

                run_steps(act, CHUNKS, LAGS, R, step)


def edge_gat_phase(nc, sh, dram):
    with ExitStack() as stack:
        s = Scope(nc, stack, "e4")
        R, LAGS = 2, 3
        src = Gathers(s, sh.started, "src", dram.x2h, sh.src_row, 2 * P, R)
        dst = Gathers(s, sh.started, "dst", dram.x2h, sh.dst_row, 2 * P, R)
        hsT, hdT, e, es, w, S, L, num, den = (s.ring(n, R) for n in (
            "hsT", "hdT", "e", "es", "w", "S", "L", "num", "den"))
        z, c, ws, wh, sq, big = (s.ring(n, 1) * R for n in ("z", "c", "ws", "wh", "sq", "big"))
        m = s.ring("m", R, (P, GROUP + 1))
        rden = s.ring("rden", R, (P, TILES))
        bS, bD, bZ, bZs, bN, bL = (s.bank(n) for n in ("S", "D", "Z", "Zs", "N", "L"))
        q = {n: s.sem(n) for n in ["src_T", "dst_T", "hsT_out", "hdT_out", "logits", "z_out", "zs_out", "e_done",
                                   "es_done", "e_max", "big_done", "m_done", "carry", "c1", "c2", "w1", "ws1", "c_exp",
                                   "w_exp", "ws_exp", "c_done", "wh_done", "S_done", "L_done", "num1", "num_done",
                                   "den_done", "num_T", "den_T", "rden_done", "o_out", "sq_out", "summed"]}
        with nc.Block() as block:

            @block.gpsimd
            def _(pool):
                def step(st):
                    if it := st.item(0):
                        need(pool, q["src_T"], it, R)
                        src.issue(pool, it)
                        need(pool, q["dst_T"], it, R)
                        dst.issue(pool, it)

                run_steps(pool, CHUNKS, LAGS, R, step)

            @block.tensor
            def _(pe):
                def step(st):
                    if it := st.item(1):
                        src.wait(pe, it)
                        need(pe, q["hsT_out"], it, 1)
                        for j in range(TILES):
                            last = pe.transpose(tile(bS, j), wide(src.rows[it.slot], 1)[:, j, :], sh.ident[:, :])
                        last.then_inc(q["src_T"], 1)
                        dst.wait(pe, it)
                        need(pe, q["hdT_out"], it, 1)
                        for j in range(TILES):
                            last = pe.transpose(tile(bD, j), wide(dst.rows[it.slot], 1)[:, j, :], sh.ident[:, :])
                        last.then_inc(q["dst_T"], 1)
                        need(pe, q["hsT_out"], it)
                        need(pe, q["hdT_out"], it)
                        need(pe, q["e_done"], it, 1)
                        need(pe, q["es_done"], it, 1)
                        pe.matmul(bZ[:, :], sh.att_both[:, 0, :], hsT[it.slot][:, :], start=True, stop=False)
                        pe.matmul(bZ[:, :], sh.att_both[:, 1, :], hdT[it.slot][:, :], start=False, stop=True)
                        pe.matmul(bZs[:, :], sh.att_both[:, 2, :], hdT[it.slot][:, :], start=True, stop=True)\
                          .then_inc(q["logits"], 1)
                    if it := st.item(3):
                        need(pe, q["num_done"], it)
                        need(pe, q["o_out"], it, 1)
                        transpose4(pe, bN, num[it.slot], sh.ident[:, :]).then_inc(q["num_T"], 1)
                        need(pe, q["den_done"], it)
                        need(pe, q["rden_done"], it, 1)
                        transpose4(pe, bL, den[it.slot], sh.ident[:, :]).then_inc(q["den_T"], 1)

                run_steps(pe, CHUNKS, LAGS, R, step)

            @block.scalar
            def _(act):
                def step(st):
                    if it := st.item(1):
                        need(act, q["src_T"], it)
                        need(act, q["wh_done"], it, R)
                        act.activation(hsT[it.slot][:, :], bS[:, :], ACT.Copy).then_inc(q["hsT_out"], 1)
                        need(act, q["dst_T"], it)
                        need(act, q["num1"], it, R)
                        act.activation(hdT[it.slot][:, :], bD[:, :], ACT.Copy).then_inc(q["hdT_out"], 1)
                        need(act, q["logits"], it)
                        need(act, q["m_done"], it, 1)
                        act.activation(z[it.slot][:, :], bZ[:, :], ACT.Copy, scale=0.2).then_inc(q["z_out"], 1)
                        need(act, q["es_done"], it, 1)
                        act.activation(ws[it.slot][:, :], bZs[:, :], ACT.Copy, scale=0.2).then_inc(q["zs_out"], 1)
                    if it := st.item(2):
                        need(act, q["c2"], it)
                        act.activation(c[it.slot][:, :], c[it.slot][:, :], ACT.Exp).then_inc(q["c_exp"], 1)
                        need(act, q["w1"], it)
                        act.activation(w[it.slot][:, :], w[it.slot][:, :], ACT.Exp).then_inc(q["w_exp"], 1)
                        need(act, q["ws1"], it)
                        act.activation(es[it.slot][:, :], es[it.slot][:, :], ACT.Exp).then_inc(q["ws_exp"], 1)
                    if it := st.item(3):
                        act.wait_ge(sh.started, 1)
                        need(act, q["num_T"], it)
                        need(act, q["rden_done"], it)
                        out = sh.gat_own[:, bass.ds(it.n * GROUP, GROUP)]
                        for j in range(TILES):
                            last = act.activation(sh.gat_own[:, bass.ds(it.n * GROUP + j * P, P)], tile(bN, j), ACT.Copy,
                                                  scale=rden[it.slot][:, j:j + 1])
                        last.then_inc(q["o_out"], 1)
                        act.wait_ge(sh.started, 1)
                        need(act, q["o_out"], it)
                        need(act, q["summed"], it, 1)
                        act.activation(sq[it.slot][:, :], out, ACT.Square).then_inc(q["sq_out"], 1)

                run_steps(act, CHUNKS, LAGS, R, step)

            @block.vector
            def _(ve):
                def step(st):
                    if it := st.item(1):
                        same = sh.same[:, bass.ds(it.n * GROUP, GROUP)]
                        need(ve, q["m_done"], it, 1)
                        ve.tensor_scalar(big[it.slot][:, :], same, 0.5, 2.0 * BIG, ALU.subtract, ALU.mult)\
                          .then_inc(q["big_done"], 1)
                        need(ve, q["z_out"], it)
                        need(ve, q["w1"], it, R)
                        ve.tensor_tensor(e[it.slot][:, :], z[it.slot][:, :], bZ[:, :], ALU.max).then_inc(q["e_done"], 1)
                        need(ve, q["zs_out"], it)
                        need(ve, q["den_done"], it, R)
                        need(ve, q["num1"], it, R)
                        ve.tensor_tensor(es[it.slot][:, :], ws[it.slot][:, :], bZs[:, :], ALU.max)\
                          .then_inc(q["es_done"], 1)
                        need(ve, q["e_done"], it)
                        need(ve, q["es_done"], it)
                        ve.tensor_tensor(z[it.slot][:, :], e[it.slot][:, :], es[it.slot][:, :], ALU.max)\
                          .then_inc(q["e_max"], 1)
                        mm, prev = m[it.slot], m[(it.slot - 1) % R]
                        first = isinstance(it.n, int) and it.n == 0
                        if not first:
                            need(ve, q["m_done"], it, 1)
                        (ve.memset(mm[:, 0:1], 0.0) if first else ve.tensor_copy(mm[:, 0:1], prev[:, GROUP:GROUP + 1]))\
                            .then_inc(q["carry"], 1)
                        need(ve, q["carry"], it)
                        need(ve, q["e_max"], it)
                        need(ve, q["big_done"], it)
                        ve.tensor_tensor_scan(mm[:, 1:GROUP + 1], big[it.slot][:, :], z[it.slot][:, :], mm[:, 0:1],
                                              ALU.min, ALU.max).then_inc(q["m_done"], 1)
                    if it := st.item(2):
                        same = sh.same[:, bass.ds(it.n * GROUP, GROUP)]
                        before, now = m[it.slot][:, 0:GROUP], m[it.slot][:, 1:GROUP + 1]
                        need(ve, q["m_done"], it)
                        need(ve, q["S_done"], it, 1)
                        ve.tensor_tensor(c[it.slot][:, :], before, now, ALU.min).then_inc(q["c1"], 1)
                        ve.tensor_tensor(w[it.slot][:, :], e[it.slot][:, :], now, ALU.subtract).then_inc(q["w1"], 1)
                        need(ve, q["c1"], it)
                        ve.tensor_tensor(c[it.slot][:, :], c[it.slot][:, :], now, ALU.subtract).then_inc(q["c2"], 1)
                        ve.tensor_tensor(es[it.slot][:, :], es[it.slot][:, :], now, ALU.subtract).then_inc(q["ws1"], 1)
                        need(ve, q["c_exp"], it)
                        ve.tensor_tensor(c[it.slot][:, :], c[it.slot][:, :], same, ALU.mult).then_inc(q["c_done"], 1)
                        need(ve, q["w_exp"], it)
                        ve.tensor_tensor(wh[it.slot][:, :], w[it.slot][:, :], hsT[it.slot][:, :], ALU.mult)\
                          .then_inc(q["wh_done"], 1)
                        need(ve, q["c_done"], it)
                        if not (isinstance(it.n, int) and it.n == 0):
                            need(ve, q["S_done"], it, 1)
                            need(ve, q["L_done"], it, 1)
                        segment_sum(ve, it, L, c[it.slot][:, :], w[it.slot][:, :]).then_inc(q["L_done"], 1)
                        need(ve, q["wh_done"], it)
                        segment_sum(ve, it, S, c[it.slot][:, :], wh[it.slot][:, :]).then_inc(q["S_done"], 1)
                        need(ve, q["ws_exp"], it)
                        need(ve, q["num_T"], it, R)
                        need(ve, q["den_T"], it, R)
                        ve.tensor_tensor(num[it.slot][:, :], es[it.slot][:, :], hdT[it.slot][:, :], ALU.mult)\
                          .then_inc(q["num1"], 1)
                        need(ve, q["L_done"], it)
                        ve.tensor_tensor(den[it.slot][:, :], es[it.slot][:, :], L[it.slot][:, :], ALU.add)\
                          .then_inc(q["den_done"], 1)
                        need(ve, q["num1"], it)
                        need(ve, q["S_done"], it)
                        ve.tensor_tensor(num[it.slot][:, :], num[it.slot][:, :], S[it.slot][:, :], ALU.add)\
                          .then_inc(q["num_done"], 1)
                    if it := st.item(3):
                        need(ve, q["den_T"], it)
                        need(ve, q["o_out"], it, R)
                        ve.reciprocal(rden[it.slot][:, :], as_tiles(bL)[:, :, 0]).then_inc(q["rden_done"], 1)
                        need(ve, q["o_out"], it)
                        need(ve, q["sq_out"], it)
                        need(ve, q["summed"], it, 1)
                        for j in range(TILES):
                            rep = column(sh.is_rep, it, j)
                            ve.scalar_tensor_tensor(out=sh.sum1[:, j, :],
                                                    in0=sh.gat_own[:, bass.ds(it.n * GROUP + j * P, P)],
                                                    scalar=rep, in1=sh.sum1[:, j, :], op0=ALU.mult, op1=ALU.add)
                            last = ve.scalar_tensor_tensor(out=sh.sum2[:, j, :], in0=tile(sq[it.slot], j),
                                                           scalar=rep, in1=sh.sum2[:, j, :], op0=ALU.mult, op1=ALU.add)
                        last.then_inc(q["summed"], 1)

                run_steps(ve, CHUNKS, LAGS, R, step)


def batch_norm_phase(nc, sh, dram):
    with ExitStack() as stack:
        s = Scope(nc, stack, "bn")
        b1, b2 = s.bank("one"), s.bank("two")
        ones = s.sb("ones", [P, P])
        mean, var, half, t, y, row = (s.sb(n, [P, P]) for n in ("mean", "var", "half", "t", "y", "row"))
        stored, summed, cleared = s.sem("stored"), s.sem("summed"), s.sem("cleared")
        with nc.Block() as block:

            @block.sync
            def _(sp):
                sp.dma_start(dram.x2h[NPAD:ROWS, P:2 * P].rearrange("(c p) d -> p c d", p=P),
                             sh.gat_own[:, :].rearrange("p (c d) -> p c d", d=P)).then_inc(stored, 16)
                sp.wait_ge(stored, 16)

            @block.tensor
            def _(pe):
                pe.wait_ge(cleared, 1)
                for j in range(TILES):
                    pe.matmul(tile(b1, 0), ones[:, :], sh.sum1[:, j, :], start=(j == 0), stop=(j == TILES - 1))
                for j in range(TILES):
                    last = pe.matmul(tile(b2, 0), ones[:, :], sh.sum2[:, j, :], start=(j == 0), stop=(j == TILES - 1))
                last.then_inc(summed, 1)

            @block.vector
            def _(ve):
                ve.memset(ones[:, :], 1.0).then_inc(cleared, 1)
                ve.wait_ge(cleared, 1)
                ve.wait_ge(summed, 1)
                link = Link(ve, s.sem("link"), 0)
                link(ve.tensor_scalar(mean[:, :], tile(b1, 0), 1.0 / NODES, None, ALU.mult))
                link(ve.tensor_scalar(var[:, :], tile(b2, 0), 1.0 / NODES, None, ALU.mult))
                link(ve.tensor_tensor(t[:, :], mean[:, :], mean[:, :], ALU.mult))
                link(ve.tensor_tensor(var[:, :], var[:, :], t[:, :], ALU.subtract))
                link(ve.tensor_scalar(var[:, :], var[:, :], 0.0, EPS, ALU.max, ALU.add))
                link(ve.tensor_scalar(half[:, :], var[:, :], -0.5, None, ALU.mult))
                rsqrt(ve, link, y[:, :], var[:, :], half[:, :], t[:, :])
                link(ve.tensor_tensor(y[:, :], y[:, :], sh.vrow["gamma"], ALU.mult))
                link(ve.tensor_tensor(mean[:, :], mean[:, :], sh.vrow["bias"], ALU.add))
                link(ve.tensor_tensor(t[:, :], sh.vrow["bias"], mean[:, :], ALU.subtract))
                link(ve.tensor_tensor(t[:, :], t[:, :], y[:, :], ALU.mult))
                link(ve.tensor_tensor(row[:, :], t[:, :], sh.vrow["beta"], ALU.add))
                for j in range(TILES):
                    link(ve.tensor_copy(tile(sh.bn_scale_4, j), y[:, :]))
                    link(ve.tensor_copy(tile(sh.bn_shift_4, j), row[:, :]))


def back_phase(nc, sh, dram, edges):
    with ExitStack() as stack:
        s = Scope(nc, stack, "be" if edges else "bk")
        R = 4
        count = CHUNKS if edges else GROUPS
        LOAD = 1 if edges else 0
        Z, X3P, NORM0, T_X3 = LOAD + 1, LOAD + 2, LOAD + 3, LOAD + 4
        S3P, NORM_S, T_S3, MMS, MD = 2, 3, 4, 5, 6
        Y = MD + 1 if edges else T_X3 + 1
        NORM1, T_N1, FFN1, FFN2, NORM2, X4P, NORM3 = (Y + k for k in range(1, 8))
        KEEP = X4P - R
        LAGS = NORM3 + 1 if edges else NORM3
        mat, vcol = sh.mat, sh.vcol
        xh = s.ring("xh", R, (P, TILES, 2 * P))
        x3k, x3l, tb = (s.ring(n, R) for n in ("x3k", "x3l", "tb"))
        x3T_depth = R if edges else 2
        x3T = s.ring("x3T", x3T_depth) * (R // x3T_depth)
        x3, x4, z, x3p, t1p, n1, tT, t2p, n2, x4p = (s.pair(n, R) for n in (
            "x3", "x4", "z", "x3p", "t1p", "n1", "tT", "t2p", "n2", "x4p"))
        g = [s.pair(f"g{k}", R) for k in range(4)]
        norms = Norms(s, 5 if edges else 4, count - 1 + NORM3)
        bT, bY, bN, bGa, bGb, bO = (s.bank(n) for n in ("T", "Y", "N", "Ga", "Gb", "O"))
        bG = [bGa, bGb]
        xh_loaded, out_stored = s.sems("xhld", R), s.sems("outst", R)
        names = ["z1", "z2", "x3p_done", "meas0", "x3_done", "x3_T", "x3T_out", "x3k_done", "kept", "mmy",
                 "t1p_done", "meas1", "n1_done", "n1_T", "tT_out", "tb1", "tb2", "mmg", "gelu", "mmo", "t2p_done",
                 "meas2", "n2_done", "u_done", "x4p_done", "meas3", "x4_done"]
        if edges:
            names += ["sz1", "sz2", "s3p_done", "meas4", "s3_done", "s3_T", "s3T_out", "mms", "mmh", "hmax",
                      "hmax_b", "h_out", "md_done", "big_done", "rep_copied"]
            src = Gathers(s, sh.started, "src", dram.x2h, sh.src_row, 2 * P, R)
            rep_idx = s.ring("rep_idx", R, (P, TILES), I32)
            scattered = s.sems("scattered", R)
            s3p, s3, s3T, hmax, md = (s.pair(n, R) for n in ("s3p", "s3", "s3T", "hmax", "md"))
            sz, hT, big = s.sb("sz", [P, GROUP]), s.sb("hT", [P, GROUP]), s.sb("big", [P, GROUP])
            bS, bH = s.bank("S"), s.bank("H")
        q = {n: s.sem(n) for n in names}

        with nc.Block() as block:

            @block.sync
            def _(sp):
                def step(st):
                    if it := st.item(LOAD):
                        need(sp, q["x3p_done"], it, R)
                        rows = edge_rows(dram.x2h, it) if edges else node_rows(dram.x2h, it)
                        sp.dma_start(xh[it.slot][:, :, :], rows).then_inc(xh_loaded[it.slot], 16)
                    if not edges and (it := st.item(NORM3)):
                        need(sp, q["x4_done"], it)
                        sp.dma_start(node_rows(dram.out, it), as_tiles(x4[it.slot])).then_inc(out_stored[it.slot], 16)

                run_steps(sp, count, LAGS, R, step)
                for k in range(R):
                    if not edges:
                        sp.wait_ge(out_stored[k], 16 * len(range(k, count, R)))

            @block.gpsimd
            def _(pool):
                def step(st):
                    if it := st.item(X4P):
                        need(pool, q["n2_done"], it)
                        pool.tensor_tensor(n2[it.slot][:, :], n2[it.slot][:, :], sh.ln2_g_4[:, :], ALU.mult)\
                            .then_inc(q["u_done"], 1)
                    if edges and (it := st.item(LAGS)):
                        need_dma(pool, scattered, it, 1, TILES)
                        pool.tensor_copy(rep_idx[it.slot][:, :], sh.rep_rows[:, bass.ds(it.n * TILES, TILES)])\
                            .then_inc(q["rep_copied"], 1)
                        need_apart(pool, sh.started, q["rep_copied"], it)
                        need(pool, q["x4_done"], it)
                        for j in range(TILES):
                            pool.indirect_dma_start(dram.out, bass.IndirectOffsetOnAxis(ap=rep_idx[it.slot][:, j:j + 1], axis=0),
                                                    tile(x4[it.slot], j), None, bounds_check=NPAD - 1,
                                                    oob_is_err=False).then_inc(scattered[it.slot], 16)
                    if edges and (it := st.item(0)):
                        need(pool, q["s3p_done"], it, R)
                        src.issue(pool, it)
                    if it := st.item(T_X3):
                        need(pool, q["x3_done"], it)
                        need(pool, q["kept"], it, R)
                        pool.tensor_tensor(x3k[it.slot][:, :], x3[it.slot][:, :], sh.ln2_b_4[:, :], ALU.add)\
                            .then_inc(q["x3k_done"], 1)
                    if it := st.item(Z):
                        need_dma(pool, xh_loaded, it)
                        need(pool, q["x3p_done"], it, 2)
                        pool.tensor_tensor(as_tiles(z[it.slot]), wide(xh[it.slot], 1), as_tiles(sh.bn_scale_4), ALU.mult)\
                            .then_inc(q["z1"], 1)
                        need(pool, q["z1"], it)
                        pool.tensor_tensor(z[it.slot][:, :], z[it.slot][:, :], sh.bn_shift_4[:, :], ALU.add)\
                            .then_inc(q["z2"], 1)
                    if it := st.item(T_N1):
                        need(pool, q["n1_done"], it)
                        need(pool, q["t2p_done"], it, R)
                        pool.tensor_tensor(tb[it.slot][:, :], n1[it.slot][:, :], sh.ln1_g_4[:, :], ALU.mult)\
                            .then_inc(q["tb1"], 1)
                        need(pool, q["tb1"], it)
                        pool.tensor_tensor(tb[it.slot][:, :], tb[it.slot][:, :], sh.ln1_b_f2_4[:, :], ALU.add)\
                            .then_inc(q["tb2"], 1)

                run_steps(pool, count, LAGS, R, step)
                if edges:
                    for k in range(R):
                        pool.wait_ge(scattered[k], 16 * TILES * len(range(k, count, R)))

            @block.tensor
            def _(pe):
                def step(st):
                    if it := st.item(FFN2):
                        gelus = it.n * 4 + 4
                        pe.wait_ge(q["gelu"], gelus)
                        need(pe, q["t2p_done"], it, 1)
                        product_nm(pe, bO, [(g[k][it.slot], mat["F2" + "abcd"[k]]) for k in range(4)])\
                            .then_inc(q["mmo"], 1)
                    if edges and (it := st.item(MMS)):
                        need(pe, q["s3T_out"], it)
                        need(pe, q["hmax"], it, 1)
                        pe.matmul(bS[:, :], mat["W_in"], s3T[it.slot][:, :], start=True, stop=True)\
                          .then_inc(q["mms"], 1)
                    if edges and (it := st.item(MD)):
                        need(pe, q["x3T_out"], it)
                        need(pe, q["h_out"], it, 1)
                        pe.matmul(bH[:, :], mat["W_in"], x3T[it.slot][:, :], start=True, stop=True)\
                          .then_inc(q["mmh"], 1)
                    if it := st.item(FFN1):
                        need(pe, q["tT_out"], it)
                        for k in range(4):
                            gelus = it.n * 4 + k - 1
                            if not isinstance(gelus, int) or gelus > 0:
                                pe.wait_ge(q["gelu"], gelus)
                            pe.matmul(bG[k % 2][:, :], mat["F1" + "abcd"[k]], tT[it.slot][:, :], start=True,
                                      stop=True).then_inc(q["mmg"], 1)
                    if it := st.item(Y):
                        need(pe, q["x3T_out"], it)
                        need(pe, q["t1p_done"], it, 1)
                        pairs = [(x3T[it.slot], sh.fold_self[:, :])]
                        if edges:
                            need(pe, q["md_done"], it)
                            pairs.append((md[it.slot], sh.fold_bot[:, :]))
                        product_nm(pe, bY, pairs).then_inc(q["mmy"], 1)
                    if it := st.item(T_X3):
                        need(pe, q["x3_done"], it)
                        need(pe, q["x3T_out"], it, 1)
                        if edges and (other := st.item(T_S3 + 1)):
                            need(pe, q["s3T_out"], other)
                        transpose4(pe, bT, x3[it.slot], sh.ident[:, :]).then_inc(q["x3_T"], 1)
                    if it := st.item(T_N1):
                        need(pe, q["n1_done"], it)
                        need(pe, q["tT_out"], it, 1)
                        transpose4(pe, bN, n1[it.slot], sh.ident[:, :]).then_inc(q["n1_T"], 1)
                    if edges and (it := st.item(T_S3)):
                        need(pe, q["s3_done"], it)
                        need(pe, q["s3T_out"], it, 1)
                        if other := st.item(T_X3):
                            need(pe, q["x3T_out"], other)
                        transpose4(pe, bT, s3[it.slot], sh.ident[:, :]).then_inc(q["s3_T"], 1)

                run_steps(pe, count, LAGS, R, step)

            @block.scalar
            def _(act):
                def step(st):
                    if edges and (it := st.item(MD)):
                        need(act, q["mmh"], it)
                        need(act, q["md_done"], it, 1)
                        act.activation(hT[:, :], bH[:, :], ACT.Identity, bias=vcol["b_in"]).then_inc(q["h_out"], 1)
                        need(act, q["hmax"], it)
                        need(act, q["mmy"], it, 2)
                        act.activation(md[it.slot][:, :], hmax[it.slot][:, :], ACT.Identity, bias=vcol["b_in"])\
                           .then_inc(q["hmax_b"], 1)
                    if it := st.item(FFN1):
                        need(act, q["mmo"], it, 2)
                        for k in range(4):
                            act.wait_ge(q["mmg"], it.n * 4 + k + 1)
                            act.activation(g[k][it.slot][:, :], bG[k % 2][:, :], ACT.Gelu,
                                           bias=vcol["f1_b" + "abcd"[k]]).then_inc(q["gelu"], 1)
                    if it := st.item(NORM1):
                        norms.ready(act, st)
                        need(act, q["n1_T"], it, 2)
                        need(act, q["tb1"], it, 2)
                        norms.apply_scalar(act, st, 1, n1[it.slot], t1p[it.slot]).then_inc(q["n1_done"], 1)
                    if it := st.item(NORM2):
                        norms.ready(act, st)
                        need(act, q["x4p_done"], it, 2)
                        norms.apply_scalar(act, st, 2, n2[it.slot], t2p[it.slot]).then_inc(q["n2_done"], 1)
                    if it := st.item(NORM3):
                        norms.ready(act, st)
                        if before := st.item(NORM3 + 2):
                            if edges:
                                need_dma(act, scattered, before, 0, TILES)
                            else:
                                need_dma(act, out_stored, before)
                        norms.apply_scalar(act, st, 3, x4[it.slot], x4p[it.slot]).then_inc(q["x4_done"], 1)
                    if it := st.item(T_X3):
                        need(act, q["x3_T"], it)
                        need(act, q["mmy"], it, x3T_depth)
                        act.activation(x3T[it.slot][:, :], bT[:, :], ACT.Copy).then_inc(q["x3T_out"], 1)
                    if it := st.item(T_N1):
                        need(act, q["n1_T"], it)
                        products = (it.n - 1) * 4
                        if not isinstance(products, int) or products > 0:
                            act.wait_ge(q["mmg"], products)
                        act.activation(tT[it.slot][:, :], bN[:, :], ACT.Identity, bias=vcol["ln1_b"],
                                       scale=vcol["ln1_g"]).then_inc(q["tT_out"], 1)
                    if edges and (it := st.item(T_S3)):
                        need(act, q["s3_T"], it)
                        need(act, q["mms"], it, 2)
                        act.activation(s3T[it.slot][:, :], bT[:, :], ACT.Copy).then_inc(q["s3T_out"], 1)

                run_steps(act, count, LAGS, R, step)

            @block.vector
            def _(ve):
                norms.prepare(ve)

                def step(st):
                    measured = [(q["meas0"], st.item(X3P + 1)), (q["meas1"], st.item(Y + 1)),
                                (q["meas2"], st.item(FFN2 + 1)), (q["meas3"], st.item(X4P + 1))]
                    if edges:
                        measured.append((q["meas4"], st.item(S3P + 1)))
                    chain = norms.chain(ve, st, measured)
                    for name, lag in (("n1_done", NORM1), ("n2_done", NORM2), ("x4_done", NORM3)):
                        if before := st.item(lag + 2):
                            need(ve, q[name], before)
                    next(chain, None)
                    if it := st.item(X3P):
                        need(ve, q["z2"], it)
                        need_dma(ve, xh_loaded, it)
                        need(ve, q["x3_done"], it, 2)
                        ve.scalar_tensor_tensor(out=as_tiles(x3p[it.slot]), in0=as_tiles(z[it.slot]), scalar=0.0,
                                                in1=wide(xh[it.slot], 0), op0=ALU.max, op1=ALU.add)\
                          .then_inc(q["x3p_done"], 1)
                        next(chain, None)
                        need(ve, q["x3p_done"], it)
                        norms.take(ve, st, 0, x3p[it.slot], chain).then_inc(q["meas0"], 1)
                        next(chain, None)
                    if it := st.item(X4P):
                        need(ve, q["u_done"], it)
                        need(ve, q["kept"], it)
                        need(ve, q["x4_done"], it, 2)
                        ve.tensor_tensor(x4p[it.slot][:, :], n2[it.slot][:, :], x3l[it.slot][:, :], ALU.add)\
                          .then_inc(q["x4p_done"], 1)
                        next(chain, None)
                        need(ve, q["x4p_done"], it)
                        norms.take(ve, st, 3, x4p[it.slot], chain).then_inc(q["meas3"], 1)
                        next(chain, None)
                    if it := st.item(KEEP):
                        need(ve, q["x3k_done"], it)
                        need(ve, q["x4p_done"], it, R)
                        ve.tensor_copy(x3l[it.slot][:, :], x3k[it.slot][:, :]).then_inc(q["kept"], 1)
                        next(chain, None)
                    if edges and (it := st.item(S3P)):
                        src.wait(ve, it)
                        rows = src.rows[it.slot]
                        need(ve, q["s3p_done"], it, 1)
                        ve.tensor_tensor(as_tiles(sz), wide(rows, 1), as_tiles(sh.bn_scale_4), ALU.mult)\
                          .then_inc(q["sz1"], 1)
                        next(chain, None)
                        need(ve, q["sz1"], it)
                        ve.tensor_tensor(sz[:, :], sz[:, :], sh.bn_shift_4[:, :], ALU.add).then_inc(q["sz2"], 1)
                        next(chain, None)
                        need(ve, q["sz2"], it)
                        need(ve, q["s3_done"], it, 2)
                        ve.scalar_tensor_tensor(out=as_tiles(s3p[it.slot]), in0=as_tiles(sz), scalar=0.0,
                                                in1=wide(rows, 0), op0=ALU.max, op1=ALU.add)\
                          .then_inc(q["s3p_done"], 1)
                        next(chain, None)
                        need(ve, q["s3p_done"], it)
                        norms.take(ve, st, 4, s3p[it.slot], chain).then_inc(q["meas4"], 1)
                    if it := st.item(FFN2):
                        need(ve, q["mmo"], it)
                        need(ve, q["tb2"], it)
                        need(ve, q["n2_done"], it, 2)
                        ve.tensor_tensor(t2p[it.slot][:, :], bO[:, :], tb[it.slot][:, :], ALU.add)\
                          .then_inc(q["t2p_done"], 1)
                        next(chain, None)
                        need(ve, q["t2p_done"], it)
                        norms.take(ve, st, 2, t2p[it.slot], chain).then_inc(q["meas2"], 1)
                    if edges and (it := st.item(MMS)):
                        same = sh.same[:, bass.ds(it.n * GROUP, GROUP)]
                        need(ve, q["hmax"], it, 1)
                        ve.tensor_scalar(big[:, :], same, 0.5, 2.0 * BIG, ALU.subtract, ALU.mult)\
                          .then_inc(q["big_done"], 1)
                        next(chain, None)
                        need(ve, q["big_done"], it)
                        need(ve, q["mms"], it)
                        need(ve, q["hmax_b"], it, 2)
                        start = -BIG
                        if not (isinstance(it.n, int) and it.n == 0):
                            start = hmax[it.slot - 1][:, GROUP - 1:GROUP]
                        ve.tensor_tensor_scan(hmax[it.slot][:, :], big[:, :], bS[:, :], start, ALU.min,
                                              ALU.max).then_inc(q["hmax"], 1)
                    for _ in chain:
                        pass
                    if it := st.item(NORM0):
                        norms.ready(ve, st)
                        need(ve, q["x3_T"], it, 2)
                        need(ve, q["x3k_done"], it, 2)
                        norms.apply_vector(ve, st, 0, x3[it.slot], x3p[it.slot]).then_inc(q["x3_done"], 1)
                    if edges and (it := st.item(NORM_S)):
                        norms.ready(ve, st)
                        need(ve, q["s3_T"], it, 2)
                        norms.apply_vector(ve, st, 4, s3[it.slot], s3p[it.slot]).then_inc(q["s3_done"], 1)
                    if edges and (it := st.item(MD)):
                        need(ve, q["hmax_b"], it)
                        need(ve, q["h_out"], it)
                        ve.tensor_tensor(md[it.slot][:, :], md[it.slot][:, :], hT[:, :], ALU.subtract)\
                          .then_inc(q["md_done"], 1)
                    if it := st.item(Y):
                        need(ve, q["mmy"], it)
                        need(ve, q["n1_done"], it, 2)
                        ve.tensor_tensor(t1p[it.slot][:, :], bY[:, :], sh.fold_bias_4[:, :], ALU.add)\
                          .then_inc(q["t1p_done"], 1)
                        need(ve, q["t1p_done"], it)
                        norms.take(ve, st, 1, t1p[it.slot], chain).then_inc(q["meas1"], 1)

                run_steps(ve, count, LAGS, R, step)


def repeat_rows_phase(nc, sh):
    with ExitStack() as stack:
        s = Scope(nc, stack, "rep")
        copied = s.sem("copied")
        with nc.Block() as block:

            @block.vector
            def _(ve):
                link = Link(ve, copied, 0)
                for out, row in ((sh.b2_4, sh.vrow["L0_b2"]), (sh.l1b2_4, sh.vrow["L1_b2"]),
                                 (sh.ln1_g_4, sh.vrow["ln1_g"]), (sh.ln1_b_f2_4, sh.ln1_b_f2[:, :]),
                                 (sh.ln2_g_4, sh.vrow["ln2_g"]), (sh.ln2_b_4, sh.vrow["ln2_b"]),
                                 (sh.fold_bias_4, sh.fold_bias[:, :])):
                    for j in range(TILES):
                        link(ve.tensor_copy(tile(out, j), row))
                link(ve.memset(sh.sum1[:, :, :], 0.0))
                link(ve.memset(sh.sum2[:, :, :], 0.0))
                link(ve.memset(sh.two[:, :], 2.0))


class Tables:
    pass


def graph_layers(nc, x, src_cols, dst_cols, next_cols, dst_row, edge_attr, mats, vcols, vrows, out):
    dram, sh = Tables(), Shared()
    dram.x, dram.src_cols, dram.dst_cols, dram.next_cols, dram.dst_row = x, src_cols, dst_cols, next_cols, dst_row
    dram.edge_attr, dram.mats, dram.vcols, dram.vrows, dram.out = edge_attr, mats, vcols, vrows, out
    scratch = lambda name, shape: nc.dram_tensor(name, shape, F32, kind="Internal").ap()
    dram.map = scratch("node_map", (NPAD, 2))
    dram.h2 = scratch("h2", (ROWS, P))
    dram.x1 = scratch("x1", (ROWS, P))
    dram.x2h = scratch("x2h", (ROWS, 2 * P))
    dram.x_own = scratch("x_own", (EPAD, P))
    dram.count_row = scratch("count_row", (1, EPAD))
    with ExitStack() as stack:
        s = Scope(nc, stack, "sh")
        sh.mats = s.sb("mats", [P, len(MATS) * P])
        sh.vcols = s.sb("vcols", [P, len(VECS)])
        sh.mat = {n: sh.mats[:, k * P:(k + 1) * P] for k, n in enumerate(MATS)}
        sh.vcol = {n: sh.vcols[:, k:k + 1] for k, n in enumerate(VECS)}
        sh.ident = s.sb("ident", [P, P])
        sh.started = s.sem("started")
        sh.same = s.sb("same", [P, EPAD], BF16)
        sh.src_cols, sh.dst_cols, sh.rep_rows, sh.src_row, sh.dst_row = (
            s.sb(n, [P, ECOLS], I32) for n in ("src_cols", "dst_cols", "rep_rows", "src_row", "dst_row"))
        sh.is_rep, sh.src_root, sh.dst_root = (s.sb(n, [P, ECOLS]) for n in ("is_rep", "src_root", "dst_root"))
        sh.fold_self, sh.fold_bot = s.sb("fold_self", [P, P]), s.sb("fold_bot", [P, P])
        (sh.b2_4, sh.l1b2_4, sh.ln1_g_4, sh.ln1_b_f2_4, sh.ln2_g_4, sh.ln2_b_4, sh.fold_bias_4, sh.bn_scale_4,
         sh.bn_shift_4) = (s.sb(n, [P, GROUP]) for n in (
            "b2_4", "l1b2_4", "ln1_g_4", "ln1_b_f2_4", "ln2_g_4", "ln2_b_4", "fold_bias_4", "bn_scale_4", "bn_shift_4"))
        with ExitStack() as front_stack:
            f = Scope(nc, front_stack, "shf")
            sh.vrows = f.sb("vrows", [P, len(VECS) * P])
            sh.vrow = {n: sh.vrows[:, k * P:(k + 1) * P] for k, n in enumerate(VECS)}
            sh.map_rows, sh.src_map, sh.dst_map = (
                f.sb(n, [P, ECOLS, 2]) for n in ("map_rows", "src_map", "dst_map"))
            sh.alone = f.sb("alone", [P, GROUPS * TILES])
            sh.two = f.sb("two", [P, 1])
            sh.sum1, sh.sum2 = f.sb("sum1", [P, TILES, P]), f.sb("sum2", [P, TILES, P])
            sh.att_both = f.sb("att_both", [P, 3, P])
            sh.bc_cols = f.sb("bc_cols", [P, 2, P])
            sh.fold_bias, sh.ln1_b_f2 = f.sb("fold_bias", [P, P]), f.sb("ln1_b_f2", [P, P])
            setup_phase(nc, sh, dram)
            repeat_rows_phase(nc, sh)
            map_phase(nc, sh, dram)
            dense_front_phase(nc, sh, dram)
            edge_gcn1_phase(nc, sh, dram)
            edge_gcn2_phase(nc, sh, dram)
            edge_gine_phase(nc, sh, dram)
            with ExitStack() as gat_stack:
                sh.gat_own = Scope(nc, gat_stack, "g").sb("gat_own", [P, EPAD])
                edge_gat_phase(nc, sh, dram)
                batch_norm_phase(nc, sh, dram)
        back_phase(nc, sh, dram, False)
        back_phase(nc, sh, dram, True)


def kernel(x, src, dst, edge_attr_128, edge_attr_16, **w):
    import numpy as np
    import concourse.bacc as bacc
    from concourse.bass_utils import run_bass_kernel_spmd

    def columns(a):
        return np.ascontiguousarray(a.reshape(ECOLS, P).T)

    def padded(a, fill):
        return np.concatenate([a, np.full((EPAD - EDGES,), fill, a.dtype)])

    W = {k: np.asarray(v) for k, v in w.items()}
    src, dst, x = np.asarray(src), padded(np.asarray(dst), NODES), np.asarray(x)
    x_pad = np.concatenate([x, np.zeros((NPAD - NODES, P), x.dtype)])
    edge_attr = np.asarray(edge_attr_128)
    edge_attr = np.concatenate([edge_attr, np.zeros((EPAD - EDGES, P), edge_attr.dtype)])
    w1t, w2t, upd = W["L0_gnn_W1"].T, W["L0_gnn_W2"].T, W["L3_gnn_W_upd_w"]
    f1, f2 = W["L3_gnn_ffn1_w"], W["L3_gnn_ffn2_w"]
    mats = [w1t[:, :P], w1t[:, P:], w2t[:P], w2t[P:], W["L1_gnn_W1"].T, W["L1_gnn_W2"].T, W["L2_gnn_W"],
            W["L3_gnn_W_in_w"], W["L3_gnn_W_in_w"].T, upd[:P].T, upd[P:].T, W["L3_gnn_W_out_w"]]
    mats += [f1[:, k * P:(k + 1) * P] for k in range(4)] + [f2[k * P:(k + 1) * P] for k in range(4)]
    f1b = W["L3_gnn_ffn1_b"]
    vecs = [W["L0_gnn_b1"][:P], W["L0_gnn_b1"][P:], W["L0_gnn_b2"], W["L1_gnn_b1"], W["L1_gnn_b2"],
            W["L2_gnn_att_src"], W["L2_gnn_att_dst"], W["L2_gnn_bias"], W["L2_gnn_gamma"], W["L2_gnn_beta"],
            W["L3_gnn_W_in_b"], W["L3_gnn_W_upd_b"], W["L3_gnn_W_out_b"], W["L3_gnn_ln1_g"], W["L3_gnn_ln1_b"],
            W["L3_gnn_ln2_g"], W["L3_gnn_ln2_b"]] + [f1b[k * P:(k + 1) * P] for k in range(4)] + [W["L3_gnn_ffn2_b"]]
    arrays = {
        "x": x_pad, "src_cols": columns(padded(src, 0)), "dst_cols": columns(dst),
        "next_cols": columns(np.concatenate([dst[1:], np.full((1,), NODES, dst.dtype)])),
        "dst_row": dst[None, :], "edge_attr": edge_attr,
        "mats": np.ascontiguousarray(np.concatenate(mats, axis=1)),
        "vcols": np.ascontiguousarray(np.stack(vecs, axis=1)), "vrows": np.concatenate(vecs)[None, :],
    }
    nc = bacc.Bacc("TRN2", target_bir_lowering=False, num_devices=1)
    args = [nc.dram_tensor(f"in_{n}", a.shape, mybir.dt.from_np(a.dtype), kind="ExternalInput").ap()
            for n, a in arrays.items()]
    out = nc.dram_tensor("out", (NPAD, P), F32, kind="ExternalOutput").ap()
    graph_layers(nc, *args, out)
    result = run_bass_kernel_spmd(nc, [{f"in_{n}": a for n, a in arrays.items()}], core_ids=[0])
    return result.results[0]["out"][:NODES]
```

```python
from contextlib import ExitStack

import concourse.bass as bass
from concourse import mybir

F32 = mybir.dt.float32
BF16 = mybir.dt.bfloat16
I32 = mybir.dt.int32
ALU = mybir.AluOpType
ACT = mybir.ActivationFunctionType

P = 128
TILES = 4
GROUP = TILES * P
NODES = 50000
EDGES = 12500
GROUPS = -(-NODES // GROUP)
NPAD = GROUPS * GROUP
CHUNKS = -(-EDGES // GROUP)
EPAD = CHUNKS * GROUP
ECOLS = EPAD // P
ROWS = NPAD + EPAD
EPS = 1e-5
SKIP = 1 << 20
BIG = 1.5e38
RSQRT_MAGIC = 0x5F3759DF

MATS = ["L0_W1a", "L0_W1b", "L0_W2a", "L0_W2b", "L1_W1", "L1_W2", "L2_W", "W_in", "W_inT", "W_topT", "W_botT",
        "W_out", "F1a", "F1b", "F1c", "F1d", "F2a", "F2b", "F2c", "F2d"]
VECS = ["L0_b1a", "L0_b1b", "L0_b2", "L1_b1", "L1_b2", "att_src", "att_dst", "bias", "gamma", "beta",
        "b_in", "b_upd", "b_out", "ln1_g", "ln1_b", "ln2_g", "ln2_b", "f1_ba", "f1_bb", "f1_bc", "f1_bd", "f2_b"]


class Item:

    def __init__(self, turn, offset, ring):
        self.turn = turn + offset // ring
        self.slot = offset % ring
        self.n = self.turn * ring + self.slot
        self.ring = ring


class Step:
    def __init__(self, turn, offset, ring, count):
        self.turn, self.offset, self.ring, self.count = turn, offset, ring, count
        self.i = turn * ring + offset

    def item(self, lag):
        it = Item(self.turn, self.offset - lag, self.ring)
        if isinstance(it.n, int) and not 0 <= it.n < self.count:
            return None
        return it


def run_steps(engine, count, lags, ring, step):
    head = -(-(lags + ring) // ring)
    tail = count // ring
    for i in range(head * ring):
        step(Step(i // ring, i % ring, ring, count))
    with engine.Fori(head, tail) as turn:
        for u in range(ring):
            step(Step(turn, u, ring, count))
    for i in range(tail * ring, count + lags):
        step(Step(i // ring, i % ring, ring, count))


def need(engine, sem, item, back=0):
    value = item.n + 1 - back
    if not isinstance(value, int) or value > 0:
        engine.wait_ge(sem, value)


def need_dma(engine, sems, item, back=0, dmas=1):
    value = (item.turn + 1 - back) * (16 * dmas)
    if not isinstance(value, int) or value > 0:
        engine.wait_ge(sems[item.slot], value)


def need_apart(engine, started, sem, item):
    value = item.n + 1
    if not isinstance(value, int):
        value = engine.to_reg(value)
    engine.wait_ge(started, 1)
    engine.wait_ge(sem, value)


class Scope:

    def __init__(self, nc, stack, prefix):
        self.nc, self.stack, self.prefix, self.handles = nc, stack, prefix, []
        stack.callback(self.release)

    def release(self):
        if self.handles:
            self.nc.clear_and_free_semaphores(self.handles)
            self.nc.all_engine_barrier()

    def sb(self, name, shape, dt=F32):
        return self.stack.enter_context(self.nc.sbuf_tensor(f"{self.prefix}_{name}", shape, dt))

    def ring(self, name, depth, shape=(P, GROUP), dt=F32):
        return [self.sb(f"{name}{k}", list(shape), dt) for k in range(depth)]

    def pair(self, name, ring):
        return self.ring(name, 2) * (ring // 2)

    def bank(self, name):
        return self.stack.enter_context(self.nc.psum_tensor(f"{self.prefix}_{name}", [P, GROUP], F32))

    def sem(self, name):
        handle = self.nc.alloc_semaphore(name=f"{self.prefix}_{name}")
        self.handles.append(handle)
        return handle

    def sems(self, name, depth):
        return [self.sem(f"{name}{k}") for k in range(depth)]


def tile(buf, j):
    return buf[:, j * P:(j + 1) * P]


def transpose4(pe, out, in_, ident):
    for j in range(TILES):
        last = pe.transpose(tile(out, j), tile(in_, j), ident)
    return last


def product_nm(pe, out, pairs):
    for j in range(TILES):
        for n, (operand, matrix) in enumerate(pairs):
            last = pe.matmul(tile(out, j), tile(operand, j), matrix, start=(n == 0), stop=(n == len(pairs) - 1))
    return last


class Link:

    def __init__(self, ve, sem, base):
        self.ve, self.sem, self.base, self.n = ve, sem, base, 0

    def __call__(self, instruction):
        self.n += 1
        instruction.then_inc(self.sem, 1)
        self.ve.wait_ge(self.sem, self.base + self.n)


RSQRT_LINKS = 2 + 3 * 3


def rsqrt(ve, link, y, v, half, t):
    link(ve.tensor_scalar(y.bitcast(I32), v.bitcast(I32), 1, None, ALU.logical_shift_right))
    link(ve.tensor_scalar(y.bitcast(I32), y.bitcast(I32), -1.0, float(RSQRT_MAGIC), ALU.mult, ALU.add))
    for _ in range(3):
        link(ve.tensor_tensor(t, y, y, ALU.mult))
        link(ve.tensor_tensor(t, t, half, ALU.mult))
        link(ve.scalar_tensor_tensor(out=y, in0=t, scalar=1.5, in1=y, op0=ALU.add, op1=ALU.mult))


NORM_LINKS = 8 + RSQRT_LINKS + 1


class Norms:

    def __init__(self, scope, count, last):
        cols = count * TILES
        self.last = last
        self.stats = scope.ring("stats", 2, (P, cols, 6))
        self.work = scope.sb("norm_work", [P, 4, cols])
        self.result = scope.ring("norm_result", 2, (P, 3, cols))
        self.sem = scope.sem("norm_link")
        self.init = scope.sem("norm_init")

    def prepare(self, ve):
        for k in range(2):
            ve.memset(self.stats[k][:, :, :], 1.0).then_inc(self.init, 1)
        ve.wait_ge(self.init, 2)

    def take(self, ve, step, which, buf, chain):
        for j in range(TILES):
            last = ve.bn_stats(self.stats[step.offset % 2][:, which * TILES + j, :], tile(buf, j))
            if j < TILES - 1:
                next(chain, None)
        return last

    def chain(self, ve, step, measured):
        if isinstance(step.i, int) and step.i > self.last:
            return
        for sem, item in measured:
            if item:
                need(ve, sem, item)
                break
        base = step.i * NORM_LINKS
        s = self.stats[(step.offset - 1) % 2]
        t, v, half, d = (self.work[:, k, :] for k in range(4))
        mean, rstd, shift = (self.result[step.offset % 2][:, k, :] for k in range(3))
        if not isinstance(base, int) or base > 0:
            ve.wait_ge(self.sem, base)
        ve.tensor_tensor(mean, s[:, :, 1], s[:, :, 4], ALU.add).then_inc(self.sem, 1)
        yield
        ve.wait_ge(self.sem, base + 1)
        ve.tensor_tensor(d, s[:, :, 1], s[:, :, 4], ALU.subtract).then_inc(self.sem, 1)
        yield
        ve.tensor_tensor(v, s[:, :, 2], s[:, :, 5], ALU.add).then_inc(self.sem, 1)
        ve.wait_ge(self.sem, base + 2)
        ve.tensor_tensor(d, d, d, ALU.mult).then_inc(self.sem, 1)
        yield
        ve.wait_ge(self.sem, base + 4)
        ve.scalar_tensor_tensor(out=v, in0=d, scalar=P / 4.0, in1=v, op0=ALU.mult, op1=ALU.add).then_inc(self.sem, 1)
        yield
        ve.wait_ge(self.sem, base + 5)
        ve.tensor_scalar(v, v, 1.0 / P, EPS, ALU.mult, ALU.add).then_inc(self.sem, 1)
        ve.tensor_scalar(mean, mean, 0.5, None, ALU.mult).then_inc(self.sem, 1)
        yield
        ve.wait_ge(self.sem, base + 7)
        ve.tensor_scalar(half, v, -0.5, None, ALU.mult).then_inc(self.sem, 1)
        ve.tensor_scalar(rstd.bitcast(I32), v.bitcast(I32), 1, None, ALU.logical_shift_right).then_inc(self.sem, 1)
        yield
        ve.wait_ge(self.sem, base + 9)
        ve.tensor_scalar(rstd.bitcast(I32), rstd.bitcast(I32), -1.0, float(RSQRT_MAGIC), ALU.mult, ALU.add)\
          .then_inc(self.sem, 1)
        yield
        for k in range(3):
            ve.wait_ge(self.sem, base + 10 + 3 * k)
            ve.tensor_tensor(t, rstd, rstd, ALU.mult).then_inc(self.sem, 1)
            yield
            ve.wait_ge(self.sem, base + 11 + 3 * k)
            ve.tensor_tensor(t, t, half, ALU.mult).then_inc(self.sem, 1)
            yield
            ve.wait_ge(self.sem, base + 12 + 3 * k)
            ve.scalar_tensor_tensor(out=rstd, in0=t, scalar=1.5, in1=rstd, op0=ALU.add, op1=ALU.mult)\
              .then_inc(self.sem, 1)
            yield
        ve.wait_ge(self.sem, base + 19)
        ve.scalar_tensor_tensor(out=shift, in0=mean, scalar=-1.0, in1=rstd, op0=ALU.mult, op1=ALU.mult)\
          .then_inc(self.sem, 1)
        yield

    def ready(self, engine, step):
        done = min(step.i, self.last) + 1 if isinstance(step.i, int) else step.i + 1
        engine.wait_ge(self.sem, done * NORM_LINKS)

    def columns(self, step, which, j):
        c = which * TILES + j
        return [self.result[step.offset % 2][:, k, c:c + 1] for k in range(3)]

    def apply_vector(self, ve, step, which, out, in_):
        for j in range(TILES):
            mean, rstd, _ = self.columns(step, which, j)
            last = ve.tensor_scalar(tile(out, j), tile(in_, j), mean, rstd, ALU.subtract, ALU.mult)
        return last

    def apply_scalar(self, act, step, which, out, in_):
        for j in range(TILES):
            _, rstd, shift = self.columns(step, which, j)
            last = act.activation(tile(out, j), tile(in_, j), ACT.Identity, bias=shift, scale=rstd)
        return last


class Shared:
    pass


def node_rows(table, item):
    return table[bass.ds(item.n * GROUP, GROUP), :].rearrange("(p j) d -> p j d", j=TILES)


def edge_rows(table, item, first=NPAD):
    return table[bass.ds(item.n * GROUP + first, GROUP), :].rearrange("(j p) d -> p j d", p=P)


def as_tiles(buf):
    return buf[:, :].rearrange("p (j d) -> p j d", j=TILES)


def wide(buf, half):
    return buf[:, :, half * P:(half + 1) * P]


def setup_phase(nc, sh, dram):
    with ExitStack() as stack:
        s = Scope(nc, stack, "set")
        dst_bc = s.sb("dst_bc", [P, EPAD], I32)
        count_bc = s.sb("count_bc", [P, EPAD])
        next_cols = s.sb("next_cols", [P, ECOLS], I32)
        map_init = s.sb("map_init", [P, NPAD // P, 2])
        node_ids = s.sb("node_ids", [P, NPAD // P], I32)
        slot_ids = s.sb("slot_ids", [P, ECOLS], I32)
        counts = s.sb("counts", [P, ECOLS])
        skip = s.sb("skip", [P, ECOLS])
        ones_row = s.sb("ones_row", [P, 1])
        banks = [s.bank(f"fold{k}") for k in range(5)]
        top_out = s.sb("top_out", [P, P])
        loaded, ids, built, init_stored = s.sem("loaded"), s.sem("ids"), s.sem("built"), s.sem("init_stored")
        count_stored, counts_back = s.sem("count_stored"), s.sem("counts_back")
        ident_done, folded, fold_read = s.sem("ident_done"), s.sem("folded"), s.sem("fold_read")
        mat, vcol, vrow = sh.mat, sh.vcol, sh.vrow
        with nc.Block() as block:

            @block.sync
            def _(sp):
                sp.sem_inc(sh.started, 1)
                sp.dma_start(dst_bc[:, :], dram.dst_row.to_broadcast([P, EPAD])).then_inc(loaded, 16)
                sp.dma_start(next_cols[:, :], dram.next_cols).then_inc(loaded, 16)
                sp.dma_start(sh.src_cols[:, :], dram.src_cols).then_inc(loaded, 16)
                sp.dma_start(sh.dst_cols[:, :], dram.dst_cols).then_inc(loaded, 16)
                sp.dma_start(sh.mats[:, :], dram.mats).then_inc(loaded, 16)
                sp.dma_start(sh.vcols[:, :], dram.vcols).then_inc(loaded, 16)
                sp.dma_start(sh.vrows[:, :], dram.vrows.to_broadcast([P, len(VECS) * P])).then_inc(loaded, 16)
                sp.wait_ge(built, 1)
                sp.dma_start(dram.map[0:NPAD, :].rearrange("(p c) t -> p (c t)", p=P),
                             map_init[:, :, :].rearrange("p c t -> p (c t)")).then_inc(init_stored, 16)
                sp.wait_ge(built, 2)
                sp.dma_start(dram.count_row, count_bc[0:1, :]).then_inc(count_stored, 16)
                sp.wait_ge(count_stored, 16)
                with nc.allow_non_contiguous_dma(reason="12800 counts, once"):
                    sp.dma_start(counts[:, :], dram.count_row.rearrange("a (c p) -> p (a c)", p=P))\
                      .then_inc(counts_back, 16)
                sp.wait_ge(init_stored, 16)

            @block.gpsimd
            def _(pool):
                pool.iota(node_ids[:, :], pattern=[[1, NPAD // P]], base=0, channel_multiplier=NPAD // P)\
                    .then_inc(ids, 1)
                pool.iota(slot_ids[:, :], pattern=[[P, ECOLS]], base=NPAD, channel_multiplier=1).then_inc(ids, 1)
                pool.memset(sh.ident[:, :], 0.0).then_inc(ident_done, 1)
                pool.wait_ge(ident_done, 1)
                pool.affine_select(out=sh.ident[:, :], in_=sh.ident[:, :], compare_op=ALU.not_equal, fill=1.0,
                                   base=0, pattern=[[-1, P]], channel_multiplier=1).then_inc(ident_done, 1)

            @block.vector
            def _(ve):
                link = Link(ve, s.sem("link"), 0)
                ve.wait_ge(ids, 2)
                link(ve.memset(map_init[:, :, 1], 1.0))
                link(ve.tensor_copy(map_init[:, :, 0], node_ids[:, :]))
                ve.nop().then_inc(built, 1)
                link(ve.memset(ones_row[:, :], 1.0))
                link(ve.memset(sh.same[:, 0:1], 0.0))
                ve.wait_ge(loaded, 16 * 7)
                link(ve.tensor_tensor(sh.same[:, 1:EPAD], dst_bc[:, 1:EPAD], dst_bc[:, 0:EPAD - 1], ALU.is_equal))
                link(ve.tensor_tensor_scan(count_bc[:, :], sh.same[:, :], ones_row[:, 0:1].to_broadcast([P, EPAD]),
                                           0.0, ALU.mult, ALU.add))
                ve.nop().then_inc(built, 1)
                link(ve.tensor_tensor(sh.is_rep[:, :], sh.dst_cols[:, :], next_cols[:, :], ALU.not_equal))
                link(ve.tensor_scalar(skip[:, :], sh.is_rep[:, :], -float(SKIP), float(SKIP), ALU.mult, ALU.add))
                link(ve.tensor_tensor(sh.rep_rows[:, :], sh.dst_cols[:, :], skip[:, :], ALU.add))
                ve.wait_ge(counts_back, 16)
                link(ve.tensor_scalar(sh.map_rows[:, :, 1], counts[:, :], 1.0, None, ALU.add))
                link(ve.tensor_copy(sh.map_rows[:, :, 0], slot_ids[:, :]))
                link(ve.tensor_tensor(sh.ln1_b_f2[:, :], vrow["ln1_b"], vrow["f2_b"], ALU.add))
                link(ve.tensor_tensor(sh.att_both[:, 2, :], vcol["att_src"].to_broadcast([P, P]),
                                      vcol["att_dst"].to_broadcast([P, P]), ALU.add))
                link(ve.tensor_copy(sh.att_both[:, 0, :], vcol["att_src"].to_broadcast([P, P])))
                link(ve.tensor_copy(sh.att_both[:, 1, :], vcol["att_dst"].to_broadcast([P, P])))
                for k, (out, bank) in enumerate(zip([top_out, sh.fold_bot], banks)):
                    ve.wait_ge(folded, k + 1)
                    link(ve.tensor_copy(out[:, :], tile(bank, 0)))
                ve.nop().then_inc(fold_read, 1)
                link(ve.tensor_copy(sh.bc_cols[:, 0, :], vcol["b_in"].to_broadcast([P, P])))
                link(ve.tensor_copy(sh.bc_cols[:, 1, :], vcol["b_upd"].to_broadcast([P, P])))
                ve.nop().then_inc(fold_read, 1)
                ve.wait_ge(folded, 3)
                link(ve.tensor_tensor(sh.fold_self[:, :], tile(banks[2], 0), sh.ident[:, :], ALU.add))
                ve.wait_ge(folded, 4)
                link(ve.tensor_tensor(sh.fold_bias[:, :], tile(banks[3], 0), vrow["b_out"], ALU.add))

            @block.tensor
            def _(pe):
                pe.wait_ge(loaded, 16 * 7)
                pe.matmul(tile(banks[0], 0), mat["W_topT"], mat["W_out"], start=True, stop=True).then_inc(folded, 1)
                pe.matmul(tile(banks[1], 0), mat["W_botT"], mat["W_out"], start=True, stop=True).then_inc(folded, 1)
                pe.wait_ge(fold_read, 1)
                pe.wait_ge(ident_done, 2)
                pe.matmul(tile(banks[2], 0), mat["W_inT"], top_out[:, :], start=True, stop=True).then_inc(folded, 1)
                pe.wait_ge(fold_read, 2)
                pe.matmul(tile(banks[3], 0), sh.bc_cols[:, 0, :], top_out[:, :], start=True, stop=False)
                pe.matmul(tile(banks[3], 0), sh.bc_cols[:, 1, :], mat["W_out"], start=False, stop=True)\
                  .then_inc(folded, 1)


def map_phase(nc, sh, dram):
    with ExitStack() as stack:
        s = Scope(nc, stack, "map")
        R = 4
        idx = s.ring("idx", R, (P, TILES), I32)
        rows = s.ring("rows", R, (P, TILES, 2))
        copied, scattered = s.sem("copied"), s.sems("scattered", R)
        with nc.Block() as block:

            @block.gpsimd
            def _(pool):
                def scatter(step):
                    it = step.item(0)
                    need_dma(pool, scattered, it, 1, TILES)
                    cols = bass.ds(it.n * TILES, TILES)
                    pool.tensor_copy(idx[it.slot][:, :], sh.rep_rows[:, cols])
                    pool.tensor_copy(rows[it.slot][:, :, :], sh.map_rows[:, cols, :]).then_inc(copied, 1)
                    need_apart(pool, sh.started, copied, it)
                    for j in range(TILES):
                        pool.indirect_dma_start(dram.map, bass.IndirectOffsetOnAxis(ap=idx[it.slot][:, j:j + 1], axis=0),
                                                rows[it.slot][:, j, :], None, bounds_check=NPAD - 1,
                                                oob_is_err=False).then_inc(scattered[it.slot], 16)

                run_steps(pool, CHUNKS, 0, R, scatter)
                for k in range(R):
                    pool.wait_ge(scattered[k], 16 * TILES * len(range(k, CHUNKS, R)))

    with ExitStack() as stack:
        s = Scope(nc, stack, "mask")
        deg = s.sb("deg", [P, GROUPS, TILES, 2])
        loaded, relued, masked = s.sem("loaded"), s.sem("relued"), s.sem("masked")
        with nc.Block() as block:

            @block.sync
            def _(sp):
                sp.dma_start(deg[:, :, :, :], dram.map[0:NPAD, :].rearrange("(g p j) t -> p g (j t)", p=P, j=TILES)
                             .rearrange("p g (j t) -> p g j t", j=TILES)).then_inc(loaded, 16)

            @block.scalar
            def _(act):
                act.wait_ge(loaded, 16)
                act.activation(sh.alone[:, :].rearrange("p (g j) -> p g j", j=TILES), deg[:, :, :, 1], ACT.Relu,
                               bias=sh.two[:, :], scale=-1.0).then_inc(relued, 1)

            @block.gpsimd
            def _(pool):
                pool.wait_ge(relued, 1)
                last = sh.alone[:, (GROUPS - 1) * TILES:GROUPS * TILES]
                pool.affine_select(out=last, in_=last, compare_op=ALU.is_gt, fill=0.0,
                                   base=NODES - (GROUPS - 1) * GROUP, pattern=[[-1, TILES]],
                                   channel_multiplier=-TILES).then_inc(masked, 1)
                pool.wait_ge(masked, 1)


def dense_front_phase(nc, sh, dram):
    with ExitStack() as stack:
        s = Scope(nc, stack, "fr")
        R = 4
        T_X, MM1, MM2, NORM1, T_X1, MM3, MM4, NORM2, T_X2, MMH, SUM = 1, 2, 3, 4, 5, 6, 7, 8, 9, 10, 11
        LAGS = SUM
        mat, vcol = sh.mat, sh.vcol
        xin, x1, x1b, h2 = (s.ring(n, R) for n in ("xin", "x1", "x1b", "h2"))
        xb, xT, r1a, r1b, pre1, x1T, r3, pre2, x2T, sq = (s.pair(n, R) for n in (
            "xb", "xT", "r1a", "r1b", "pre1", "x1T", "r3", "pre2", "x2T", "sq"))
        x2h = s.ring("x2h", R, (P, TILES, 2 * P))
        norms = Norms(s, 2, GROUPS - 1 + NORM2)
        LOOK_KEEP = 2
        ends = (("src", sh.src_cols, sh.src_map), ("dst", sh.dst_cols, sh.dst_map))
        look_idx = {e: s.ring(f"idx_{e}", R, (P, 1), I32) for e, _, _ in ends}
        looked_up = {e: s.ring(f"got_{e}", R, (P, 2)) for e, _, _ in ends}
        x_ends = s.ring("x_ends", R, (P, 2, P))
        idx_copied, looked, look_kept = s.sem("idx_copied"), s.sems("looked", R), s.sem("look_kept")
        x_landed, x_ends_stored = s.sems("xlanded", R), s.sems("xends", R)
        deg, half, t = (s.sb(n, [P, ECOLS]) for n in ("deg", "half", "root_t"))
        bT, bMa, bMb, bC, bD, bE, bF, bH = (s.bank(n) for n in ("T", "Ma", "Mb", "C", "D", "E", "F", "H"))
        x_loaded, h2_stored, x1_stored, x2h_stored = (s.sems(n, R) for n in ("xld", "h2st", "x1st", "x2hst"))
        names = ["x_T", "xT_out", "xb_done", "mm1", "relu1", "mm2", "h2_out", "pre1_done", "meas1", "x1_done", "x1_T",
                 "x1T_out", "x1b_done", "mm3", "relu3", "mm4", "pre2_done", "meas2", "x2_done", "x2_T", "x2T_out",
                 "mmh", "h_out", "sq_out", "summed"]
        q = {n: s.sem(n) for n in names}
        with nc.Block() as block:

            @block.sync
            def _(sp):
                def step(st):
                    if it := st.item(0):
                        need(sp, q["x_T"], it, R)
                        need(sp, q["xb_done"], it, R)
                        sp.dma_start(as_tiles(xin[it.slot]), node_rows(dram.x, it)).then_inc(x_loaded[it.slot], 16)
                    if it := Step(st.turn, st.offset, R, ECOLS).item(LOOK_KEEP):
                        need_dma(sp, x_landed, it, 0, 2)
                        sp.dma_start(dram.x_ends[bass.ds(it.n * P, P), :].rearrange("p (k d) -> p k d", k=2),
                                     x_ends[it.slot][:, :, :]).then_inc(x_ends_stored[it.slot], 16)
                    if it := st.item(MM2):
                        need(sp, q["h2_out"], it)
                        sp.dma_start(node_rows(dram.h2, it), as_tiles(h2[it.slot])).then_inc(h2_stored[it.slot], 16)
                    if it := st.item(NORM1):
                        need(sp, q["x1_done"], it)
                        sp.dma_start(node_rows(dram.x1, it), as_tiles(x1[it.slot])).then_inc(x1_stored[it.slot], 16)
                    if it := st.item(MMH):
                        need(sp, q["x2_done"], it)
                        need(sp, q["h_out"], it)
                        sp.dma_start(node_rows(dram.x2h, it), x2h[it.slot][:, :, :]).then_inc(x2h_stored[it.slot], 16)

                run_steps(sp, GROUPS, LAGS, R, step)
                for sems, count in ((h2_stored, GROUPS), (x1_stored, GROUPS), (x2h_stored, GROUPS),
                                    (x_ends_stored, ECOLS)):
                    for k in range(R):
                        sp.wait_ge(sems[k], 16 * len(range(k, count, R)))

            @block.gpsimd
            def _(pool):
                def step(st):
                    if it := st.item(MM1):
                        need_dma(pool, x_loaded, it)
                        need(pool, q["pre1_done"], it, 2)
                        pool.tensor_tensor(xb[it.slot][:, :], xin[it.slot][:, :], sh.b2_4[:, :], ALU.add)\
                            .then_inc(q["xb_done"], 1)
                    if it := st.item(T_X1):
                        need(pool, q["x1_done"], it)
                        need(pool, q["pre2_done"], it, R)
                        pool.tensor_tensor(x1b[it.slot][:, :], x1[it.slot][:, :], sh.l1b2_4[:, :], ALU.add)\
                            .then_inc(q["x1b_done"], 1)
                    tiles = Step(st.turn, st.offset, R, ECOLS)
                    if it := tiles.item(LOOK_KEEP):
                        need_dma(pool, looked, it, 0, 2)
                        need_dma(pool, x_landed, it, 0, 2)
                        for e, _, kept in ends:
                            last = pool.tensor_copy(kept[:, bass.ds(it.n, 1), :],
                                                    looked_up[e][it.slot][:, :].rearrange("p (a t) -> p a t", a=1))
                        last.then_inc(look_kept, 1)
                    if it := tiles.item(0):
                        need(pool, look_kept, it, R)
                        need_dma(pool, x_ends_stored, it, 1)
                        for e, cols, _ in ends:
                            last = pool.tensor_copy(look_idx[e][it.slot][:, :], cols[:, bass.ds(it.n, 1)])
                        last.then_inc(idx_copied, 1)
                        need_apart(pool, sh.started, idx_copied, it)
                        for e, _, _ in ends:
                            pool.indirect_dma_start(looked_up[e][it.slot][:, :], None, dram.map,
                                                    bass.IndirectOffsetOnAxis(ap=look_idx[e][it.slot][:, 0:1], axis=0))\
                                .then_inc(looked[it.slot], 16)
                        for k, (e, _, _) in enumerate(ends):
                            pool.indirect_dma_start(x_ends[it.slot][:, k, :], None, dram.x,
                                                    bass.IndirectOffsetOnAxis(ap=look_idx[e][it.slot][:, 0:1], axis=0))\
                                .then_inc(x_landed[it.slot], 16)

                run_steps(pool, GROUPS, LAGS, R, step)

            @block.tensor
            def _(pe):
                def step(st):
                    if it := st.item(MM1):
                        need(pe, q["xT_out"], it)
                        need(pe, q["relu1"], it, 1)
                        pe.matmul(bMa[:, :], mat["L0_W1a"], xT[it.slot][:, :], start=True, stop=True)
                        pe.matmul(bMb[:, :], mat["L0_W1b"], xT[it.slot][:, :], start=True, stop=True)\
                          .then_inc(q["mm1"], 1)
                    if it := st.item(MM2):
                        need(pe, q["relu1"], it)
                        need(pe, q["h2_out"], it, 1)
                        product_nm(pe, bC, [(r1a[it.slot], mat["L0_W2a"]), (r1b[it.slot], mat["L0_W2b"])])\
                            .then_inc(q["mm2"], 1)
                    if it := st.item(T_X1):
                        need(pe, q["x1_done"], it)
                        need(pe, q["x1T_out"], it, 1)
                        transpose4(pe, bD, x1[it.slot], sh.ident[:, :]).then_inc(q["x1_T"], 1)
                    if it := st.item(T_X):
                        need_dma(pe, x_loaded, it)
                        need(pe, q["xT_out"], it, 1)
                        if other := st.item(T_X2 + 1):
                            need(pe, q["x2T_out"], other)
                        transpose4(pe, bT, xin[it.slot], sh.ident[:, :]).then_inc(q["x_T"], 1)
                    if it := st.item(MM4):
                        need(pe, q["relu3"], it)
                        need(pe, q["pre2_done"], it, 1)
                        product_nm(pe, bF, [(r3[it.slot], mat["L1_W2"])]).then_inc(q["mm4"], 1)
                    if it := st.item(MM3):
                        need(pe, q["x1T_out"], it)
                        need(pe, q["relu3"], it, 1)
                        pe.matmul(bE[:, :], mat["L1_W1"], x1T[it.slot][:, :], start=True, stop=True)\
                          .then_inc(q["mm3"], 1)
                    if it := st.item(MMH):
                        need(pe, q["x2T_out"], it)
                        need(pe, q["sq_out"], it, 1)
                        product_nm(pe, bH, [(x2T[it.slot], mat["L2_W"])]).then_inc(q["mmh"], 1)
                    if it := st.item(T_X2):
                        need(pe, q["x2_done"], it)
                        need(pe, q["x2T_out"], it, 1)
                        if other := st.item(T_X):
                            need(pe, q["xT_out"], other)
                        for j in range(TILES):
                            last = pe.transpose(tile(bT, j), wide(x2h[it.slot], 0)[:, j, :], sh.ident[:, :])
                        last.then_inc(q["x2_T"], 1)

                run_steps(pe, GROUPS, LAGS, R, step)

            @block.scalar
            def _(act):
                def step(st):
                    if it := st.item(MM1):
                        need(act, q["mm1"], it)
                        need(act, q["mm2"], it, 2)
                        act.activation(r1a[it.slot][:, :], bMa[:, :], ACT.Relu, bias=vcol["L0_b1a"])
                        act.activation(r1b[it.slot][:, :], bMb[:, :], ACT.Relu, bias=vcol["L0_b1b"])\
                           .then_inc(q["relu1"], 1)
                    if it := st.item(MM2):
                        need(act, q["mm2"], it)
                        need_dma(act, h2_stored, it, 1)
                        need(act, q["pre1_done"], it, R)
                        act.activation(h2[it.slot][:, :], bC[:, :], ACT.Copy).then_inc(q["h2_out"], 1)
                    if it := st.item(T_X1):
                        need(act, q["x1_T"], it)
                        need(act, q["mm3"], it, 2)
                        act.activation(x1T[it.slot][:, :], bD[:, :], ACT.Copy).then_inc(q["x1T_out"], 1)
                    if it := st.item(T_X):
                        need(act, q["x_T"], it)
                        need(act, q["mm1"], it, 2)
                        act.activation(xT[it.slot][:, :], bT[:, :], ACT.Copy).then_inc(q["xT_out"], 1)
                    if it := st.item(MM3):
                        need(act, q["mm3"], it)
                        need(act, q["mm4"], it, 2)
                        act.activation(r3[it.slot][:, :], bE[:, :], ACT.Relu, bias=vcol["L1_b1"])\
                           .then_inc(q["relu3"], 1)
                    if it := st.item(MMH):
                        need(act, q["mmh"], it)
                        need(act, q["summed"], it, 2)
                        act.activation(wide(x2h[it.slot], 1), as_tiles(bH), ACT.Copy).then_inc(q["h_out"], 1)
                        act.activation(sq[it.slot][:, :], bH[:, :], ACT.Square).then_inc(q["sq_out"], 1)
                    if it := st.item(T_X2):
                        need(act, q["x2_T"], it)
                        need(act, q["mmh"], it, 2)
                        act.activation(x2T[it.slot][:, :], bT[:, :], ACT.Copy).then_inc(q["x2T_out"], 1)
                    if it := st.item(NORM2):
                        norms.ready(act, st)
                        need_dma(act, x2h_stored, it, 1)
                        need(act, q["summed"], it, R)
                        for j in range(TILES):
                            _, rstd, shift = norms.columns(st, 1, j)
                            last = act.activation(wide(x2h[it.slot], 0)[:, j, :], tile(pre2[it.slot], j), ACT.Identity,
                                                  bias=shift, scale=rstd)
                        last.then_inc(q["x2_done"], 1)

                run_steps(act, GROUPS, LAGS, R, step)

            @block.vector
            def _(ve):
                norms.prepare(ve)

                def step(st):
                    chain = norms.chain(ve, st, [(q["meas2"], st.item(MM4 + 1)), (q["meas1"], st.item(MM2 + 1))])
                    if it := st.item(SUM):
                        need(ve, q["h_out"], it)
                        need(ve, q["sq_out"], it)
                        need(ve, q["summed"], it, 1)
                        for j in range(TILES):
                            alone = sh.alone[:, bass.ds(it.n * TILES + j, 1)]
                            ve.scalar_tensor_tensor(out=sh.sum1[:, j, :], in0=wide(x2h[it.slot], 1)[:, j, :],
                                                    scalar=alone, in1=sh.sum1[:, j, :], op0=ALU.mult, op1=ALU.add)
                            next(chain, None)
                            last = ve.scalar_tensor_tensor(out=sh.sum2[:, j, :], in0=tile(sq[it.slot], j),
                                                           scalar=alone, in1=sh.sum2[:, j, :], op0=ALU.mult,
                                                           op1=ALU.add)
                            if j < TILES - 1:
                                next(chain, None)
                        last.then_inc(q["summed"], 1)
                        next(chain, None)
                    if it := st.item(MM2):
                        need(ve, q["h2_out"], it)
                        need(ve, q["xb_done"], it)
                        need(ve, q["x1_done"], it, 2)
                        ve.tensor_tensor(pre1[it.slot][:, :], h2[it.slot][:, :], xb[it.slot][:, :], ALU.add)\
                          .then_inc(q["pre1_done"], 1)
                        next(chain, None)
                        need(ve, q["pre1_done"], it)
                        norms.take(ve, st, 0, pre1[it.slot], chain).then_inc(q["meas1"], 1)
                    if it := st.item(MM4):
                        need(ve, q["mm4"], it)
                        need(ve, q["x1b_done"], it)
                        need(ve, q["x2_done"], it, 2)
                        ve.tensor_tensor(pre2[it.slot][:, :], bF[:, :], x1b[it.slot][:, :], ALU.add)\
                          .then_inc(q["pre2_done"], 1)
                        next(chain, None)
                        need(ve, q["pre2_done"], it)
                        norms.take(ve, st, 1, pre2[it.slot], chain).then_inc(q["meas2"], 1)
                    for _ in chain:
                        pass
                    if it := st.item(NORM1):
                        norms.ready(ve, st)
                        need_dma(ve, x1_stored, it, 1)
                        need(ve, q["x1_T"], it, R)
                        need(ve, q["x1b_done"], it, R)
                        norms.apply_vector(ve, st, 0, x1[it.slot], pre1[it.slot]).then_inc(q["x1_done"], 1)

                run_steps(ve, GROUPS, LAGS, R, step)
                ve.wait_ge(look_kept, ECOLS)
                link = Link(ve, s.sem("link"), 0)
                for (_, _, m), row, root in zip(ends, (sh.src_row, sh.dst_row), (sh.src_root, sh.dst_root)):
                    link(ve.tensor_copy(row[:, :], m[:, :, 0]))
                    link(ve.tensor_copy(deg[:, :], m[:, :, 1]))
                    link(ve.tensor_scalar(half[:, :], deg[:, :], -0.5, None, ALU.mult))
                    rsqrt(ve, link, root[:, :], deg[:, :], half[:, :], t[:, :])


class Gathers:

    def __init__(self, scope, started, name, table, columns, width, ring):
        self.table, self.columns, self.ring, self.started = table, columns, ring, started
        self.idx = scope.ring(f"{name}_idx", ring, (P, TILES), I32)
        self.rows = scope.ring(f"{name}_rows", ring, (P, TILES, width))
        self.copied = scope.sem(f"{name}_copied")
        self.landed = scope.sems(f"{name}_landed", ring)

    def issue(self, pool, it):
        pool.tensor_copy(self.idx[it.slot][:, :], self.columns[:, bass.ds(it.n * TILES, TILES)])\
            .then_inc(self.copied, 1)
        need_apart(pool, self.started, self.copied, it)
        for j in range(TILES):
            pool.indirect_dma_start(self.rows[it.slot][:, j, :], None, self.table,
                                    bass.IndirectOffsetOnAxis(ap=self.idx[it.slot][:, j:j + 1], axis=0))\
                .then_inc(self.landed[it.slot], 16)

    def wait(self, engine, it, back=0):
        need_dma(engine, self.landed, it, back, TILES)


def flat(rows):
    return rows[:, :, :].rearrange("p j d -> p (j d)")


def segment_sum(ve, it, sums, same, values):
    start = 0.0
    if not (isinstance(it.n, int) and it.n == 0):
        start = sums[(it.slot - 1) % len(sums)][:, GROUP - 1:GROUP]
    return ve.tensor_tensor_scan(sums[it.slot][:, :], same, values, start, ALU.mult, ALU.add)


def column(cols, it, j):
    return cols[:, bass.ds(it.n * TILES + j, 1)]


def edge_gcn1_phase(nc, sh, dram):
    with ExitStack() as stack:
        s = Scope(nc, stack, "e1")
        R = 4
        SCALE, T_SRC, T_SUM, T_U, MM1, MM2 = 1, 2, 3, 4, 5, 6
        LAGS = MM2
        mat, vcol = sh.mat, sh.vcol
        ends = s.ring("ends", R, (P, TILES, 2 * P))
        h2s, xob = s.ring("h2s", R), s.ring("xob", R)
        scaled, sums, v, u, uT, r1a, r1b = (s.pair(n, R) for n in ("scaled", "sums", "v", "u", "uT", "r1a", "r1b"))
        bS, bA, bU, bMa, bMb, bH = (s.bank(n) for n in ("S", "A", "U", "Ma", "Mb", "H"))
        ends_loaded, h2_stored, xob_stored = s.sems("endsld", R), s.sems("h2st", R), s.sems("xobst", R)
        q = {n: s.sem(n) for n in ["scaled", "src_T", "summed", "sum_T", "v_done", "u_done", "u_T", "uT_out", "mm1",
                                   "relu1", "mm2", "h2_out", "xob_done"]}
        with nc.Block() as block:

            @block.sync
            def _(sp):
                def step(st):
                    if it := st.item(0):
                        need(sp, q["scaled"], it, R)
                        need(sp, q["v_done"], it, R)
                        need(sp, q["xob_done"], it, R)
                        sp.dma_start(ends[it.slot][:, :, :], edge_rows(dram.x_ends, it, 0))\
                          .then_inc(ends_loaded[it.slot], 16)
                    if it := st.item(SCALE):
                        need(sp, q["xob_done"], it)
                        sp.dma_start(edge_rows(dram.x_own, it, 0), as_tiles(xob[it.slot])).then_inc(xob_stored[it.slot], 16)
                    if it := st.item(MM2):
                        need(sp, q["h2_out"], it)
                        sp.dma_start(edge_rows(dram.h2, it), as_tiles(h2s[it.slot])).then_inc(h2_stored[it.slot], 16)

                run_steps(sp, CHUNKS, LAGS, R, step)
                for sems in (xob_stored, h2_stored):
                    for k in range(R):
                        sp.wait_ge(sems[k], 16 * len(range(k, CHUNKS, R)))

            @block.gpsimd
            def _(pool):
                def step(st):
                    if it := st.item(SCALE):
                        need_dma(pool, ends_loaded, it)
                        need_dma(pool, xob_stored, it, 1)
                        pool.tensor_tensor(as_tiles(xob[it.slot]), wide(ends[it.slot], 1), as_tiles(sh.b2_4), ALU.add)\
                            .then_inc(q["xob_done"], 1)

                run_steps(pool, CHUNKS, LAGS, R, step)

            @block.vector
            def _(ve):
                def step(st):
                    if it := st.item(SCALE):
                        need_dma(ve, ends_loaded, it)
                        need(ve, q["src_T"], it, 2)
                        for j in range(TILES):
                            last = ve.tensor_scalar(tile(scaled[it.slot], j), wide(ends[it.slot], 0)[:, j, :],
                                                    column(sh.src_root, it, j), None, ALU.mult)
                        last.then_inc(q["scaled"], 1)
                    if it := st.item(T_SRC):
                        need(ve, q["src_T"], it)
                        need(ve, q["sum_T"], it, 2)
                        need(ve, q["summed"], it, 1)
                        segment_sum(ve, it, sums, sh.same[:, bass.ds(it.n * GROUP, GROUP)], bS[:, :])\
                            .then_inc(q["summed"], 1)
                    if it := st.item(T_SUM):
                        need(ve, q["sum_T"], it)
                        need(ve, q["u_done"], it, 2)
                        for j in range(TILES):
                            last = ve.scalar_tensor_tensor(out=tile(v[it.slot], j), in0=wide(ends[it.slot], 1)[:, j, :],
                                                           scalar=column(sh.dst_root, it, j), in1=tile(bA, j),
                                                           op0=ALU.mult, op1=ALU.add)
                        last.then_inc(q["v_done"], 1)

                run_steps(ve, CHUNKS, LAGS, R, step)

            @block.scalar
            def _(act):
                def step(st):
                    if it := st.item(MM1):
                        need(act, q["mm1"], it)
                        need(act, q["mm2"], it, 2)
                        act.activation(r1a[it.slot][:, :], bMa[:, :], ACT.Relu, bias=vcol["L0_b1a"])
                        act.activation(r1b[it.slot][:, :], bMb[:, :], ACT.Relu, bias=vcol["L0_b1b"])\
                           .then_inc(q["relu1"], 1)
                    if it := st.item(T_U):
                        need(act, q["u_T"], it)
                        need(act, q["mm1"], it, 2)
                        act.activation(uT[it.slot][:, :], bU[:, :], ACT.Copy).then_inc(q["uT_out"], 1)
                    if it := st.item(MM2):
                        act.wait_ge(sh.started, 1)
                        need(act, q["mm2"], it)
                        need_dma(act, h2_stored, it, 1)
                        for j in range(TILES):
                            last = act.activation(tile(h2s[it.slot], j), tile(bH, j), ACT.Copy,
                                                  scale=column(sh.dst_root, it, j))
                        last.then_inc(q["h2_out"], 1)
                    if it := st.item(T_SUM):
                        act.wait_ge(sh.started, 1)
                        need(act, q["v_done"], it)
                        for j in range(TILES):
                            last = act.activation(tile(u[it.slot], j), tile(v[it.slot], j), ACT.Copy,
                                                  scale=column(sh.dst_root, it, j))
                        last.then_inc(q["u_done"], 1)

                run_steps(act, CHUNKS, LAGS, R, step)

            @block.tensor
            def _(pe):
                def step(st):
                    if it := st.item(MM1):
                        need(pe, q["uT_out"], it)
                        need(pe, q["relu1"], it, 1)
                        pe.matmul(bMa[:, :], mat["L0_W1a"], uT[it.slot][:, :], start=True, stop=True)
                        pe.matmul(bMb[:, :], mat["L0_W1b"], uT[it.slot][:, :], start=True, stop=True)\
                          .then_inc(q["mm1"], 1)
                    if it := st.item(T_SRC):
                        need(pe, q["scaled"], it)
                        need(pe, q["summed"], it, 1)
                        transpose4(pe, bS, scaled[it.slot], sh.ident[:, :]).then_inc(q["src_T"], 1)
                    if it := st.item(T_SUM):
                        need(pe, q["summed"], it)
                        need(pe, q["v_done"], it, 1)
                        transpose4(pe, bA, sums[it.slot], sh.ident[:, :]).then_inc(q["sum_T"], 1)
                    if it := st.item(T_U):
                        need(pe, q["u_done"], it)
                        need(pe, q["uT_out"], it, 1)
                        transpose4(pe, bU, u[it.slot], sh.ident[:, :]).then_inc(q["u_T"], 1)
                    if it := st.item(MM2):
                        need(pe, q["relu1"], it)
                        need(pe, q["h2_out"], it, 1)
                        product_nm(pe, bH, [(r1a[it.slot], mat["L0_W2a"]), (r1b[it.slot], mat["L0_W2b"])])\
                            .then_inc(q["mm2"], 1)

                run_steps(pe, CHUNKS, LAGS, R, step)


def edge_gcn2_phase(nc, sh, dram):
    with ExitStack() as stack:
        s = Scope(nc, stack, "e2")
        R = 4
        T_SRC, T_SUM, NORM = 1, 2, 3
        LAGS = NORM
        src = Gathers(s, sh.started, "src", dram.h2, sh.src_row, P, R)
        xob, h2o, x1, pre = (s.ring(n, R) for n in ("xob", "h2o", "x1", "pre"))
        sums, w = (s.pair(n, R) for n in ("sums", "w"))
        norms = Norms(s, 1, CHUNKS - 1 + NORM)
        bS, bA = s.bank("S"), s.bank("A")
        own_loaded, x1_stored = s.sems("ownld", R), s.sems("x1st", R)
        q = {n: s.sem(n) for n in ["src_T", "summed", "sum_T", "w_done", "pre_done", "meas", "x1_done"]}
        with nc.Block() as block:

            @block.gpsimd
            def _(pool):
                def step(st):
                    if it := st.item(0):
                        need(pool, q["src_T"], it, R)
                        src.issue(pool, it)

                run_steps(pool, CHUNKS, LAGS, R, step)

            @block.sync
            def _(sp):
                def step(st):
                    if it := st.item(0):
                        need(sp, q["pre_done"], it, R)
                        sp.dma_start(as_tiles(xob[it.slot]), edge_rows(dram.x_own, it, 0)).then_inc(own_loaded[it.slot], 16)
                        sp.dma_start(as_tiles(h2o[it.slot]), edge_rows(dram.h2, it)).then_inc(own_loaded[it.slot], 16)
                    if it := st.item(NORM):
                        need(sp, q["x1_done"], it)
                        sp.dma_start(edge_rows(dram.x1, it), as_tiles(x1[it.slot])).then_inc(x1_stored[it.slot], 16)

                run_steps(sp, CHUNKS, LAGS, R, step)
                for k in range(R):
                    sp.wait_ge(x1_stored[k], 16 * len(range(k, CHUNKS, R)))

            @block.tensor
            def _(pe):
                def step(st):
                    if it := st.item(T_SUM):
                        need(pe, q["summed"], it)
                        need(pe, q["w_done"], it, 1)
                        transpose4(pe, bA, sums[it.slot], sh.ident[:, :]).then_inc(q["sum_T"], 1)
                    if it := st.item(T_SRC):
                        src.wait(pe, it)
                        need(pe, q["summed"], it, 1)
                        transpose4(pe, bS, flat(src.rows[it.slot]), sh.ident[:, :]).then_inc(q["src_T"], 1)

                run_steps(pe, CHUNKS, LAGS, R, step)

            @block.vector
            def _(ve):
                norms.prepare(ve)

                def step(st):
                    chain = norms.chain(ve, st, [(q["meas"], st.item(T_SUM + 1))])
                    if before := st.item(NORM + 2):
                        need(ve, q["x1_done"], before)
                    next(chain, None)
                    if it := st.item(T_SUM):
                        need(ve, q["sum_T"], it)
                        need_dma(ve, own_loaded, it, 0, 2)
                        ve.tensor_tensor(w[it.slot][:, :], bA[:, :], h2o[it.slot][:, :], ALU.add)\
                          .then_inc(q["w_done"], 1)
                        next(chain, None)
                        need(ve, q["w_done"], it)
                        need(ve, q["x1_done"], it, R)
                        for j in range(TILES):
                            last = ve.scalar_tensor_tensor(out=tile(pre[it.slot], j), in0=tile(w[it.slot], j),
                                                           scalar=column(sh.dst_root, it, j), in1=tile(xob[it.slot], j),
                                                           op0=ALU.mult, op1=ALU.add)
                            if j < TILES - 1:
                                next(chain, None)
                        last.then_inc(q["pre_done"], 1)
                        next(chain, None)
                        need(ve, q["pre_done"], it)
                        norms.take(ve, st, 0, pre[it.slot], chain).then_inc(q["meas"], 1)
                    if it := st.item(T_SRC):
                        need(ve, q["src_T"], it)
                        need(ve, q["sum_T"], it, 2)
                        need(ve, q["summed"], it, 1)
                        segment_sum(ve, it, sums, sh.same[:, bass.ds(it.n * GROUP, GROUP)], bS[:, :])\
                            .then_inc(q["summed"], 1)
                    for _ in chain:
                        pass

                run_steps(ve, CHUNKS, LAGS, R, step)

            @block.scalar
            def _(act):
                def step(st):
                    if it := st.item(NORM):
                        norms.ready(act, st)
                        need_dma(act, x1_stored, it, 1)
                        norms.apply_scalar(act, st, 0, x1[it.slot], pre[it.slot]).then_inc(q["x1_done"], 1)

                run_steps(act, CHUNKS, LAGS, R, step)


def edge_gine_phase(nc, sh, dram):
    with ExitStack() as stack:
        s = Scope(nc, stack, "e3")
        R = 4
        MSG, T_IN, MM3, MM4, NORM, T_X2, MMH = 1, 2, 3, 4, 5, 6, 7
        LAGS = MMH
        mat, vcol = sh.mat, sh.vcol
        src = Gathers(s, sh.started, "src", dram.x1, sh.src_row, P, R)
        ea, x1o = s.ring("ea", R), s.ring("x1o", R)
        x1b, pre = s.ring("x1b", R), s.ring("pre", R)
        msg, sums, uT, r3, x2T = (s.pair(n, R) for n in ("msg", "sums", "uT", "r3", "x2T"))
        x2h = s.ring("x2h", R, (P, TILES, 2 * P))
        norms = Norms(s, 1, CHUNKS - 1 + NORM)
        bS, bO, bE, bF, bT, bH = (s.bank(n) for n in ("S", "O", "E", "F", "T", "H"))
        loaded, stored = s.sems("ld", R), s.sems("st", R)
        q = {n: s.sem(n) for n in ["msg", "msg_relu", "src_T", "own_T", "x1b_done", "summed", "u_done", "mm3", "relu3",
                                   "mm4", "pre_done", "meas", "x2_done", "x2_T", "x2T_out", "mmh", "h_out"]}
        with nc.Block() as block:

            @block.gpsimd
            def _(pool):
                def step(st):
                    if it := st.item(0):
                        need(pool, q["msg"], it, R)
                        src.issue(pool, it)
                    if it := st.item(T_IN):
                        need_dma(pool, loaded, it, 0, 2)
                        need(pool, q["pre_done"], it, R)
                        pool.tensor_tensor(x1b[it.slot][:, :], x1o[it.slot][:, :], sh.l1b2_4[:, :], ALU.add)\
                            .then_inc(q["x1b_done"], 1)

                run_steps(pool, CHUNKS, LAGS, R, step)

            @block.sync
            def _(sp):
                def step(st):
                    if it := st.item(0):
                        need(sp, q["msg"], it, R)
                        need(sp, q["own_T"], it, R)
                        need(sp, q["x1b_done"], it, R)
                        sp.dma_start(as_tiles(ea[it.slot]), edge_rows(dram.edge_attr, it, 0)).then_inc(loaded[it.slot], 16)
                        sp.dma_start(as_tiles(x1o[it.slot]), edge_rows(dram.x1, it)).then_inc(loaded[it.slot], 16)
                    if it := st.item(MMH):
                        need(sp, q["x2_done"], it)
                        need(sp, q["h_out"], it)
                        sp.dma_start(edge_rows(dram.x2h, it), x2h[it.slot][:, :, :]).then_inc(stored[it.slot], 16)

                run_steps(sp, CHUNKS, LAGS, R, step)
                for k in range(R):
                    sp.wait_ge(stored[k], 16 * len(range(k, CHUNKS, R)))

            @block.tensor
            def _(pe):
                def step(st):
                    if it := st.item(T_IN):
                        need(pe, q["msg_relu"], it)
                        need(pe, q["summed"], it, 1)
                        transpose4(pe, bS, msg[it.slot], sh.ident[:, :]).then_inc(q["src_T"], 1)
                        need_dma(pe, loaded, it, 0, 2)
                        need(pe, q["u_done"], it, 1)
                        transpose4(pe, bO, x1o[it.slot], sh.ident[:, :]).then_inc(q["own_T"], 1)
                    if it := st.item(MM4):
                        need(pe, q["relu3"], it)
                        need(pe, q["pre_done"], it, 1)
                        product_nm(pe, bF, [(r3[it.slot], mat["L1_W2"])]).then_inc(q["mm4"], 1)
                    if it := st.item(MMH):
                        need(pe, q["x2T_out"], it)
                        need(pe, q["h_out"], it, 1)
                        product_nm(pe, bH, [(x2T[it.slot], mat["L2_W"])]).then_inc(q["mmh"], 1)
                    if it := st.item(MM3):
                        need(pe, q["u_done"], it)
                        need(pe, q["relu3"], it, 1)
                        pe.matmul(bE[:, :], mat["L1_W1"], uT[it.slot][:, :], start=True, stop=True)\
                          .then_inc(q["mm3"], 1)
                    if it := st.item(T_X2):
                        need(pe, q["x2_done"], it)
                        need(pe, q["x2T_out"], it, 1)
                        for j in range(TILES):
                            last = pe.transpose(tile(bT, j), wide(x2h[it.slot], 0)[:, j, :], sh.ident[:, :])
                        last.then_inc(q["x2_T"], 1)

                run_steps(pe, CHUNKS, LAGS, R, step)

            @block.vector
            def _(ve):
                norms.prepare(ve)

                def step(st):
                    chain = norms.chain(ve, st, [(q["meas"], st.item(MM4 + 1))])
                    if before := st.item(NORM + 2):
                        need(ve, q["x2_done"], before)
                    next(chain, None)
                    if it := st.item(MSG):
                        src.wait(ve, it)
                        need_dma(ve, loaded, it, 0, 2)
                        need(ve, q["src_T"], it, 2)
                        ve.tensor_tensor(msg[it.slot][:, :], flat(src.rows[it.slot]), ea[it.slot][:, :], ALU.add)\
                          .then_inc(q["msg"], 1)
                        next(chain, None)
                    if it := st.item(T_IN):
                        need(ve, q["src_T"], it)
                        need(ve, q["summed"], it, 1)
                        need(ve, q["u_done"], it, 2)
                        segment_sum(ve, it, sums, sh.same[:, bass.ds(it.n * GROUP, GROUP)], bS[:, :])\
                            .then_inc(q["summed"], 1)
                        next(chain, None)
                        need(ve, q["own_T"], it)
                        need(ve, q["summed"], it)
                        need(ve, q["mm3"], it, 2)
                        ve.tensor_tensor(uT[it.slot][:, :], bO[:, :], sums[it.slot][:, :], ALU.add)\
                          .then_inc(q["u_done"], 1)
                        next(chain, None)
                    if it := st.item(MM4):
                        need(ve, q["mm4"], it)
                        need(ve, q["x1b_done"], it)
                        need(ve, q["x2_done"], it, R)
                        ve.tensor_tensor(pre[it.slot][:, :], bF[:, :], x1b[it.slot][:, :], ALU.add)\
                          .then_inc(q["pre_done"], 1)
                        next(chain, None)
                        need(ve, q["pre_done"], it)
                        norms.take(ve, st, 0, pre[it.slot], chain).then_inc(q["meas"], 1)
                    for _ in chain:
                        pass

                run_steps(ve, CHUNKS, LAGS, R, step)

            @block.scalar
            def _(act):
                def step(st):
                    if it := st.item(MSG):
                        need(act, q["msg"], it)
                        act.activation(msg[it.slot][:, :], msg[it.slot][:, :], ACT.Relu).then_inc(q["msg_relu"], 1)
                    if it := st.item(MMH):
                        need(act, q["mmh"], it)
                        act.activation(wide(x2h[it.slot], 1), as_tiles(bH), ACT.Copy).then_inc(q["h_out"], 1)
                    if it := st.item(MM3):
                        need(act, q["mm3"], it)
                        need(act, q["mm4"], it, 2)
                        act.activation(r3[it.slot][:, :], bE[:, :], ACT.Relu, bias=vcol["L1_b1"])\
                           .then_inc(q["relu3"], 1)
                    if it := st.item(T_X2):
                        need(act, q["x2_T"], it)
                        need(act, q["mmh"], it, 2)
                        act.activation(x2T[it.slot][:, :], bT[:, :], ACT.Copy).then_inc(q["x2T_out"], 1)
                    if it := st.item(NORM):
                        norms.ready(act, st)
                        need_dma(act, stored, it, 1)
                        for j in range(TILES):
                            _, rstd, shift = norms.columns(st, 0, j)
                            last = act.activation(wide(x2h[it.slot], 0)[:, j, :], tile(pre[it.slot], j), ACT.Identity,
                                                  bias=shift, scale=rstd)
                        last.then_inc(q["x2_done"], 1)

                run_steps(act, CHUNKS, LAGS, R, step)


def edge_gat_phase(nc, sh, dram):
    with ExitStack() as stack:
        s = Scope(nc, stack, "e4")
        R = 4
        T_IN, LOGIT, MAXIMUM, EXPONENT, SUMS, T_OUT, SUM = 1, 2, 3, 4, 5, 6, 7
        LAGS = SUM
        src = Gathers(s, sh.started, "src", dram.x2h, sh.src_row, 2 * P, 2)
        dst = Gathers(s, sh.started, "dst", dram.x2h, sh.dst_row, 2 * P, 2)
        hsT, hdT, es = (s.ring(n, R) for n in ("hsT", "hdT", "es"))
        e, w, c, S, L, num, den, sq = (s.pair(n, R) for n in ("e", "w", "c", "S", "L", "num", "den", "sq"))
        e_top, big, wh = (s.sb(n, [P, GROUP]) for n in ("e_top", "big", "wh"))
        m = s.ring("m", 2, (P, GROUP + 1)) * (R // 2)
        rden = s.ring("rden", R, (P, TILES))
        bS, bD, bZ, bZs, bN, bL = (s.bank(n) for n in ("S", "D", "Z", "Zs", "N", "L"))
        q = {n: s.sem(n) for n in ["src_T", "dst_T", "hsT_out", "hdT_out", "logits", "z_out", "zs_out", "e_done",
                                   "es_done", "e_top_done", "big_done", "m_done", "carry", "c1", "c2", "w1",
                                   "ws1", "c_exp", "w_exp", "ws_exp", "c_done", "wh_done", "S_done", "L_done",
                                   "num1", "num_done", "den_done", "num_T", "den_T", "rden_done", "o_out", "sq_out",
                                   "summed"]}

        def rows_item(it):
            return Item(it.turn * 2, it.slot, 2)

        with nc.Block() as block:

            @block.gpsimd
            def _(pool):
                def step(st):
                    if it := st.item(SUMS):
                        need(pool, q["c_exp"], it)
                        pool.tensor_tensor(c[it.slot][:, :], c[it.slot][:, :], sh.same[:, bass.ds(it.n * GROUP, GROUP)],
                                           ALU.mult).then_inc(q["c_done"], 1)
                        need(pool, q["ws_exp"], it)
                        need(pool, q["num_T"], it, 2)
                        pool.tensor_tensor(num[it.slot][:, :], es[it.slot][:, :], hdT[it.slot][:, :], ALU.mult)\
                            .then_inc(q["num1"], 1)
                    if it := st.item(0):
                        need(pool, q["src_T"], it, 2)
                        src.issue(pool, rows_item(it))
                        need(pool, q["dst_T"], it, 2)
                        dst.issue(pool, rows_item(it))

                run_steps(pool, CHUNKS, LAGS, R, step)

            @block.tensor
            def _(pe):
                def step(st):
                    if it := st.item(LOGIT):
                        need(pe, q["hsT_out"], it)
                        need(pe, q["hdT_out"], it)
                        need(pe, q["e_done"], it, 1)
                        need(pe, q["es_done"], it, 1)
                        pe.matmul(bZ[:, :], sh.att_both[:, 0, :], hsT[it.slot][:, :], start=True, stop=False)
                        pe.matmul(bZ[:, :], sh.att_both[:, 1, :], hdT[it.slot][:, :], start=False, stop=True)
                        pe.matmul(bZs[:, :], sh.att_both[:, 2, :], hdT[it.slot][:, :], start=True, stop=True)\
                          .then_inc(q["logits"], 1)
                    if it := st.item(T_OUT):
                        need(pe, q["den_done"], it)
                        need(pe, q["rden_done"], it, 1)
                        transpose4(pe, bL, den[it.slot], sh.ident[:, :]).then_inc(q["den_T"], 1)
                        need(pe, q["num_done"], it)
                        need(pe, q["o_out"], it, 1)
                        transpose4(pe, bN, num[it.slot], sh.ident[:, :]).then_inc(q["num_T"], 1)
                    if it := st.item(T_IN):
                        here = rows_item(it)
                        src.wait(pe, here)
                        need(pe, q["hsT_out"], it, 1)
                        for j in range(TILES):
                            last = pe.transpose(tile(bS, j), wide(src.rows[here.slot], 1)[:, j, :], sh.ident[:, :])
                        last.then_inc(q["src_T"], 1)
                        dst.wait(pe, here)
                        need(pe, q["hdT_out"], it, 1)
                        for j in range(TILES):
                            last = pe.transpose(tile(bD, j), wide(dst.rows[here.slot], 1)[:, j, :], sh.ident[:, :])
                        last.then_inc(q["dst_T"], 1)

                run_steps(pe, CHUNKS, LAGS, R, step)

            @block.scalar
            def _(act):
                def step(st):
                    if it := st.item(LOGIT):
                        need(act, q["logits"], it)
                        need(act, q["w1"], it, 2)
                        act.activation(e[it.slot][:, :], bZ[:, :], ACT.Copy, scale=0.2).then_inc(q["z_out"], 1)
                        need(act, q["den_done"], it, R)
                        need(act, q["num1"], it, R)
                        act.activation(es[it.slot][:, :], bZs[:, :], ACT.Copy, scale=0.2).then_inc(q["zs_out"], 1)
                    if it := st.item(T_OUT):
                        act.wait_ge(sh.started, 1)
                        need(act, q["num_T"], it)
                        need(act, q["rden_done"], it)
                        out = sh.gat_own[:, bass.ds(it.n * GROUP, GROUP)]
                        for j in range(TILES):
                            last = act.activation(sh.gat_own[:, bass.ds(it.n * GROUP + j * P, P)], tile(bN, j), ACT.Copy,
                                                  scale=rden[it.slot][:, j:j + 1])
                        last.then_inc(q["o_out"], 1)
                        act.wait_ge(sh.started, 1)
                        need(act, q["o_out"], it)
                        act.activation(sq[it.slot][:, :], out, ACT.Square).then_inc(q["sq_out"], 1)
                    if it := st.item(T_IN):
                        need(act, q["src_T"], it)
                        need(act, q["wh_done"], it, R)
                        act.activation(hsT[it.slot][:, :], bS[:, :], ACT.Copy).then_inc(q["hsT_out"], 1)
                        need(act, q["dst_T"], it)
                        need(act, q["num1"], it, R)
                        act.activation(hdT[it.slot][:, :], bD[:, :], ACT.Copy).then_inc(q["hdT_out"], 1)
                    if it := st.item(EXPONENT):
                        need(act, q["c2"], it)
                        act.activation(c[it.slot][:, :], c[it.slot][:, :], ACT.Exp).then_inc(q["c_exp"], 1)
                        need(act, q["w1"], it)
                        act.activation(w[it.slot][:, :], w[it.slot][:, :], ACT.Exp).then_inc(q["w_exp"], 1)
                        need(act, q["ws1"], it)
                        act.activation(es[it.slot][:, :], es[it.slot][:, :], ACT.Exp).then_inc(q["ws_exp"], 1)

                run_steps(act, CHUNKS, LAGS, R, step)

            @block.vector
            def _(ve):
                def step(st):
                    if it := st.item(SUMS):
                        need(ve, q["w_exp"], it)
                        need(ve, q["S_done"], it, 1)
                        ve.tensor_tensor(wh[:, :], w[it.slot][:, :], hsT[it.slot][:, :], ALU.mult)\
                          .then_inc(q["wh_done"], 1)
                        need(ve, q["c_done"], it)
                        need(ve, q["den_done"], it, 2)
                        segment_sum(ve, it, L, c[it.slot][:, :], w[it.slot][:, :]).then_inc(q["L_done"], 1)
                        need(ve, q["wh_done"], it)
                        need(ve, q["num_done"], it, 1)
                        segment_sum(ve, it, S, c[it.slot][:, :], wh[:, :]).then_inc(q["S_done"], 1)
                        need(ve, q["ws_exp"], it)
                        need(ve, q["den_T"], it, 2)
                        need(ve, q["L_done"], it)
                        ve.tensor_tensor(den[it.slot][:, :], es[it.slot][:, :], L[it.slot][:, :], ALU.add)\
                          .then_inc(q["den_done"], 1)
                        need(ve, q["num1"], it)
                        need(ve, q["S_done"], it)
                        ve.tensor_tensor(num[it.slot][:, :], num[it.slot][:, :], S[it.slot][:, :], ALU.add)\
                          .then_inc(q["num_done"], 1)
                    if it := st.item(EXPONENT):
                        before, now = m[it.slot][:, 0:GROUP], m[it.slot][:, 1:GROUP + 1]
                        need(ve, q["m_done"], it)
                        need(ve, q["S_done"], it, 2)
                        ve.tensor_tensor(c[it.slot][:, :], before, now, ALU.min).then_inc(q["c1"], 1)
                        ve.tensor_tensor(w[it.slot][:, :], e[it.slot][:, :], now, ALU.subtract).then_inc(q["w1"], 1)
                        need(ve, q["c1"], it)
                        ve.tensor_tensor(c[it.slot][:, :], c[it.slot][:, :], now, ALU.subtract).then_inc(q["c2"], 1)
                        ve.tensor_tensor(es[it.slot][:, :], es[it.slot][:, :], now, ALU.subtract).then_inc(q["ws1"], 1)
                    if it := st.item(T_OUT):
                        need(ve, q["den_T"], it)
                        need(ve, q["o_out"], it, R)
                        ve.reciprocal(rden[it.slot][:, :], as_tiles(bL)[:, :, 0]).then_inc(q["rden_done"], 1)
                    if it := st.item(LOGIT):
                        need(ve, q["z_out"], it)
                        ve.tensor_tensor(e[it.slot][:, :], e[it.slot][:, :], bZ[:, :], ALU.max).then_inc(q["e_done"], 1)
                        need(ve, q["zs_out"], it)
                        ve.tensor_tensor(es[it.slot][:, :], es[it.slot][:, :], bZs[:, :], ALU.max)\
                          .then_inc(q["es_done"], 1)
                    if it := st.item(MAXIMUM):
                        same = sh.same[:, bass.ds(it.n * GROUP, GROUP)]
                        need(ve, q["m_done"], it, 1)
                        ve.tensor_scalar(big[:, :], same, 0.5, 2.0 * BIG, ALU.subtract, ALU.mult)\
                          .then_inc(q["big_done"], 1)
                        need(ve, q["e_done"], it)
                        need(ve, q["es_done"], it)
                        ve.tensor_tensor(e_top[:, :], e[it.slot][:, :], es[it.slot][:, :], ALU.max)\
                          .then_inc(q["e_top_done"], 1)
                        mm, prev = m[it.slot], m[it.slot - 1]
                        first = isinstance(it.n, int) and it.n == 0
                        need(ve, q["c2"], it, 2)
                        need(ve, q["ws1"], it, 2)
                        (ve.memset(mm[:, 0:1], 0.0) if first else ve.tensor_copy(mm[:, 0:1], prev[:, GROUP:GROUP + 1]))\
                            .then_inc(q["carry"], 1)
                        need(ve, q["carry"], it)
                        need(ve, q["e_top_done"], it)
                        need(ve, q["big_done"], it)
                        ve.tensor_tensor_scan(mm[:, 1:GROUP + 1], big[:, :], e_top[:, :], mm[:, 0:1],
                                              ALU.min, ALU.max).then_inc(q["m_done"], 1)
                    if it := st.item(SUM):
                        need(ve, q["o_out"], it)
                        need(ve, q["sq_out"], it)
                        need(ve, q["summed"], it, 1)
                        for j in range(TILES):
                            rep = column(sh.is_rep, it, j)
                            ve.scalar_tensor_tensor(out=sh.sum1[:, j, :],
                                                    in0=sh.gat_own[:, bass.ds(it.n * GROUP + j * P, P)],
                                                    scalar=rep, in1=sh.sum1[:, j, :], op0=ALU.mult, op1=ALU.add)
                            last = ve.scalar_tensor_tensor(out=sh.sum2[:, j, :], in0=tile(sq[it.slot], j),
                                                           scalar=rep, in1=sh.sum2[:, j, :], op0=ALU.mult, op1=ALU.add)
                        last.then_inc(q["summed"], 1)

                run_steps(ve, CHUNKS, LAGS, R, step)


def batch_norm_phase(nc, sh, dram):
    with ExitStack() as stack:
        s = Scope(nc, stack, "bn")
        b1, b2 = s.bank("one"), s.bank("two")
        ones = s.sb("ones", [P, P])
        mean, var, half, t, y, row = (s.sb(n, [P, P]) for n in ("mean", "var", "half", "t", "y", "row"))
        stored, summed, cleared = s.sem("stored"), s.sem("summed"), s.sem("cleared")
        with nc.Block() as block:

            @block.sync
            def _(sp):
                sp.dma_start(dram.x2h[NPAD:ROWS, P:2 * P].rearrange("(c p) d -> p c d", p=P),
                             sh.gat_own[:, :].rearrange("p (c d) -> p c d", d=P)).then_inc(stored, 16)
                sp.wait_ge(stored, 16)

            @block.tensor
            def _(pe):
                pe.wait_ge(cleared, 1)
                for j in range(TILES):
                    pe.matmul(tile(b1, 0), ones[:, :], sh.sum1[:, j, :], start=(j == 0), stop=(j == TILES - 1))
                for j in range(TILES):
                    last = pe.matmul(tile(b2, 0), ones[:, :], sh.sum2[:, j, :], start=(j == 0), stop=(j == TILES - 1))
                last.then_inc(summed, 1)

            @block.vector
            def _(ve):
                ve.memset(ones[:, :], 1.0).then_inc(cleared, 1)
                ve.wait_ge(cleared, 1)
                ve.wait_ge(summed, 1)
                link = Link(ve, s.sem("link"), 0)
                link(ve.tensor_scalar(mean[:, :], tile(b1, 0), 1.0 / NODES, None, ALU.mult))
                link(ve.tensor_scalar(var[:, :], tile(b2, 0), 1.0 / NODES, None, ALU.mult))
                link(ve.tensor_tensor(t[:, :], mean[:, :], mean[:, :], ALU.mult))
                link(ve.tensor_tensor(var[:, :], var[:, :], t[:, :], ALU.subtract))
                link(ve.tensor_scalar(var[:, :], var[:, :], 0.0, EPS, ALU.max, ALU.add))
                link(ve.tensor_scalar(half[:, :], var[:, :], -0.5, None, ALU.mult))
                rsqrt(ve, link, y[:, :], var[:, :], half[:, :], t[:, :])
                link(ve.tensor_tensor(y[:, :], y[:, :], sh.bn_row["gamma"], ALU.mult))
                link(ve.tensor_tensor(mean[:, :], mean[:, :], sh.bn_row["bias"], ALU.add))
                link(ve.tensor_tensor(t[:, :], sh.bn_row["bias"], mean[:, :], ALU.subtract))
                link(ve.tensor_tensor(t[:, :], t[:, :], y[:, :], ALU.mult))
                link(ve.tensor_tensor(row[:, :], t[:, :], sh.bn_row["beta"], ALU.add))
                for j in range(TILES):
                    link(ve.tensor_copy(tile(sh.bn_scale_4, j), y[:, :]))
                    link(ve.tensor_copy(tile(sh.bn_shift_4, j), row[:, :]))


def back_phase(nc, sh, dram, edges):
    with ExitStack() as stack:
        s = Scope(nc, stack, "be" if edges else "bk")
        R = 4
        count = CHUNKS if edges else GROUPS
        LOAD = 1 if edges else 0
        Z, X3P, NORM0, T_X3 = LOAD + 1, LOAD + 2, LOAD + 3, LOAD + 4
        S3P, NORM_S, T_S3, MMS, MD = 2, 3, 4, 5, 6
        Y = MD + 1 if edges else T_X3 + 1
        NORM1, T_N1, FFN1, FFN2, NORM2, X4P, NORM3 = (Y + k for k in range(1, 8))
        KEEP = X4P - R
        LAGS = NORM3 + 1 if edges else NORM3
        mat, vcol = sh.mat, sh.vcol
        xh = s.ring("xh", R, (P, TILES, 2 * P))
        x3k, x3l = s.ring("x3k", R), s.ring("x3l", R)
        depth = R if edges else 2
        x3T, x3p, tT = (s.ring(n, depth) * (R // depth) for n in ("x3T", "x3p", "tT"))
        x3, x4, z, t1p, n1, t2p, n2, x4p = (s.pair(n, R) for n in (
            "x3", "x4", "z", "t1p", "n1", "t2p", "n2", "x4p"))
        g = [s.pair(f"g{k}", R) for k in range(4)]
        norms = Norms(s, 5 if edges else 4, count - 1 + NORM3)
        bT, bY, bN, bO = (s.bank(n) for n in ("T", "Y", "N", "O"))
        bG = [s.bank(f"G{k}") for k in range(2 if edges else 4)]
        xh_loaded, out_stored = s.sems("xhld", R), s.sems("outst", R)
        names = ["z1", "z2", "x3p_done", "meas0", "x3_done", "x3_T", "x3T_out", "x3k_done", "kept", "mmy",
                 "t1p_done", "meas1", "n1_done", "n1_T", "tT_out", "tb1", "tb2", "mmg", "gelu", "mmo", "t2p_done",
                 "meas2", "n2_done", "u_done", "x4p_done", "meas3", "x4_done"]
        if edges:
            names += ["sz1", "sz2", "s3p_done", "meas4", "s3_done", "s3_T", "s3T_out", "mms", "mmh", "hmax",
                      "hmax_b", "h_out", "md_done", "big_done", "rep_copied"]
            src = Gathers(s, sh.started, "src", dram.x2h, sh.src_row, 2 * P, R)
            rep_idx = s.ring("rep_idx", R, (P, TILES), I32)
            scattered = s.sems("scattered", R)
            s3p = s.ring("s3p", R)
            s3, s3T, hmax, md = (s.pair(n, R) for n in ("s3", "s3T", "hmax", "md"))
            sz, hT, big = s.sb("sz", [P, GROUP]), s.sb("hT", [P, GROUP]), s.sb("big", [P, GROUP])
            bS, bH = s.bank("S"), s.bank("H")
        else:
            tb = s.ring("tb", R)
        q = {n: s.sem(n) for n in names}

        with nc.Block() as block:

            @block.sync
            def _(sp):
                def step(st):
                    if it := st.item(LOAD):
                        need(sp, q["x3p_done"], it, R)
                        rows = edge_rows(dram.x2h, it) if edges else node_rows(dram.x2h, it)
                        sp.dma_start(xh[it.slot][:, :, :], rows).then_inc(xh_loaded[it.slot], 16)
                    if not edges and (it := st.item(NORM3)):
                        need(sp, q["x4_done"], it)
                        sp.dma_start(node_rows(dram.out, it), as_tiles(x4[it.slot])).then_inc(out_stored[it.slot], 16)

                run_steps(sp, count, LAGS, R, step)
                for k in range(R):
                    if not edges:
                        sp.wait_ge(out_stored[k], 16 * len(range(k, count, R)))

            @block.gpsimd
            def _(pool):
                def step(st):
                    if it := st.item(X4P):
                        need(pool, q["n2_done"], it)
                        pool.tensor_tensor(n2[it.slot][:, :], n2[it.slot][:, :], sh.ln2_g_4[:, :], ALU.mult)\
                            .then_inc(q["u_done"], 1)
                    if edges and (it := st.item(LAGS)):
                        need_dma(pool, scattered, it, 1, TILES)
                        pool.tensor_copy(rep_idx[it.slot][:, :], sh.rep_rows[:, bass.ds(it.n * TILES, TILES)])\
                            .then_inc(q["rep_copied"], 1)
                        need_apart(pool, sh.started, q["rep_copied"], it)
                        need(pool, q["x4_done"], it)
                        for j in range(TILES):
                            pool.indirect_dma_start(dram.out, bass.IndirectOffsetOnAxis(ap=rep_idx[it.slot][:, j:j + 1], axis=0),
                                                    tile(x4[it.slot], j), None, bounds_check=NPAD - 1,
                                                    oob_is_err=False).then_inc(scattered[it.slot], 16)
                    if edges and (it := st.item(0)):
                        need(pool, q["s3p_done"], it, R)
                        src.issue(pool, it)
                    if it := st.item(T_X3):
                        need(pool, q["x3_done"], it)
                        need(pool, q["kept"], it, R)
                        pool.tensor_tensor(x3k[it.slot][:, :], x3[it.slot][:, :], sh.ln2_b_4[:, :], ALU.add)\
                            .then_inc(q["x3k_done"], 1)
                    if it := st.item(Z):
                        need_dma(pool, xh_loaded, it)
                        need(pool, q["x3p_done"], it, 2)
                        pool.tensor_tensor(as_tiles(z[it.slot]), wide(xh[it.slot], 1), as_tiles(sh.bn_scale_4), ALU.mult)\
                            .then_inc(q["z1"], 1)
                        need(pool, q["z1"], it)
                        pool.tensor_tensor(z[it.slot][:, :], z[it.slot][:, :], sh.bn_shift_4[:, :], ALU.add)\
                            .then_inc(q["z2"], 1)
                    if not edges and (it := st.item(T_N1)):
                        need(pool, q["n1_done"], it)
                        need(pool, q["t2p_done"], it, R)
                        pool.tensor_tensor(tb[it.slot][:, :], n1[it.slot][:, :], sh.ln1_g_4[:, :], ALU.mult)\
                            .then_inc(q["tb1"], 1)
                        need(pool, q["tb1"], it)
                        pool.tensor_tensor(tb[it.slot][:, :], tb[it.slot][:, :], sh.ln1_b_f2_4[:, :], ALU.add)\
                            .then_inc(q["tb2"], 1)

                run_steps(pool, count, LAGS, R, step)
                if edges:
                    for k in range(R):
                        pool.wait_ge(scattered[k], 16 * TILES * len(range(k, count, R)))

            @block.tensor
            def _(pe):
                def step(st):
                    if it := st.item(FFN2):
                        gelus = it.n * 4 + 4
                        pe.wait_ge(q["gelu"], gelus)
                        need(pe, q["t2p_done"], it, 1)
                        pairs = [(g[k][it.slot], mat["F2" + "abcd"[k]]) for k in range(4)]
                        if edges:
                            pairs.append((tT[it.slot], sh.ident[:, :]))
                        product_nm(pe, bO, pairs).then_inc(q["mmo"], 1)
                    if edges and (it := st.item(MMS)):
                        need(pe, q["s3T_out"], it)
                        need(pe, q["hmax"], it, 1)
                        pe.matmul(bS[:, :], mat["W_in"], s3T[it.slot][:, :], start=True, stop=True)\
                          .then_inc(q["mms"], 1)
                    if edges and (it := st.item(MD)):
                        need(pe, q["x3T_out"], it)
                        need(pe, q["h_out"], it, 1)
                        pe.matmul(bH[:, :], mat["W_in"], x3T[it.slot][:, :], start=True, stop=True)\
                          .then_inc(q["mmh"], 1)
                    if it := st.item(T_X3):
                        need(pe, q["x3_done"], it)
                        need(pe, q["x3T_out"], it, 1)
                        if edges and (other := st.item(T_S3 + 1)):
                            need(pe, q["s3T_out"], other)
                        transpose4(pe, bT, x3[it.slot], sh.ident[:, :]).then_inc(q["x3_T"], 1)
                    if it := st.item(T_N1):
                        need(pe, q["n1_done"], it)
                        need(pe, q["tT_out"], it, 1)
                        transpose4(pe, bN, n1[it.slot], sh.ident[:, :]).then_inc(q["n1_T"], 1)
                    if it := st.item(FFN1):
                        need(pe, q["tT_out"], it)
                        for k in range(4):
                            gelus = it.n * 4 + k + 1 - len(bG)
                            if not isinstance(gelus, int) or gelus > 0:
                                pe.wait_ge(q["gelu"], gelus)
                            pe.matmul(bG[k % len(bG)][:, :], mat["F1" + "abcd"[k]], tT[it.slot][:, :], start=True,
                                      stop=True).then_inc(q["mmg"], 1)
                    if it := st.item(Y):
                        need(pe, q["x3T_out"], it)
                        need(pe, q["t1p_done"], it, 1)
                        pairs = [(x3T[it.slot], sh.fold_self[:, :])]
                        if edges:
                            need(pe, q["md_done"], it)
                            pairs.append((md[it.slot], sh.fold_bot[:, :]))
                        product_nm(pe, bY, pairs).then_inc(q["mmy"], 1)
                    if edges and (it := st.item(T_S3)):
                        need(pe, q["s3_done"], it)
                        need(pe, q["s3T_out"], it, 1)
                        if other := st.item(T_X3):
                            need(pe, q["x3T_out"], other)
                        transpose4(pe, bT, s3[it.slot], sh.ident[:, :]).then_inc(q["s3_T"], 1)

                run_steps(pe, count, LAGS, R, step)

            @block.scalar
            def _(act):
                def step(st):
                    if edges and (it := st.item(MD)):
                        need(act, q["mmh"], it)
                        need(act, q["md_done"], it, 1)
                        act.activation(hT[:, :], bH[:, :], ACT.Identity, bias=vcol["b_in"]).then_inc(q["h_out"], 1)
                        need(act, q["hmax"], it)
                        need(act, q["mmy"], it, 2)
                        act.activation(md[it.slot][:, :], hmax[it.slot][:, :], ACT.Identity, bias=vcol["b_in"])\
                           .then_inc(q["hmax_b"], 1)
                    if it := st.item(T_X3):
                        need(act, q["x3_T"], it)
                        need(act, q["mmy"], it, depth)
                        act.activation(x3T[it.slot][:, :], bT[:, :], ACT.Copy).then_inc(q["x3T_out"], 1)
                    if it := st.item(T_N1):
                        need(act, q["n1_T"], it)
                        if edges:
                            need(act, q["mmo"], it, R)
                        else:
                            products = (it.n - 1) * 4
                            if not isinstance(products, int) or products > 0:
                                act.wait_ge(q["mmg"], products)
                        act.activation(tT[it.slot][:, :], bN[:, :], ACT.Identity, bias=vcol["ln1_b"],
                                       scale=vcol["ln1_g"]).then_inc(q["tT_out"], 1)
                    if it := st.item(FFN1):
                        need(act, q["mmo"], it, 2)
                        for k in range(4):
                            act.wait_ge(q["mmg"], it.n * 4 + k + 1)
                            act.activation(g[k][it.slot][:, :], bG[k % len(bG)][:, :], ACT.Gelu,
                                           bias=vcol["f1_b" + "abcd"[k]]).then_inc(q["gelu"], 1)
                    if it := st.item(NORM1):
                        norms.ready(act, st)
                        need(act, q["n1_T"], it, 2)
                        if not edges:
                            need(act, q["tb1"], it, 2)
                        norms.apply_scalar(act, st, 1, n1[it.slot], t1p[it.slot]).then_inc(q["n1_done"], 1)
                    if it := st.item(NORM2):
                        norms.ready(act, st)
                        need(act, q["x4p_done"], it, 2)
                        norms.apply_scalar(act, st, 2, n2[it.slot], t2p[it.slot]).then_inc(q["n2_done"], 1)
                    if it := st.item(NORM3):
                        norms.ready(act, st)
                        if before := st.item(NORM3 + 2):
                            if edges:
                                need_dma(act, scattered, before, 0, TILES)
                            else:
                                need_dma(act, out_stored, before)
                        norms.apply_scalar(act, st, 3, x4[it.slot], x4p[it.slot]).then_inc(q["x4_done"], 1)
                    if edges and (it := st.item(T_S3)):
                        need(act, q["s3_T"], it)
                        need(act, q["mms"], it, 2)
                        act.activation(s3T[it.slot][:, :], bT[:, :], ACT.Copy).then_inc(q["s3T_out"], 1)

                run_steps(act, count, LAGS, R, step)

            @block.vector
            def _(ve):
                norms.prepare(ve)

                def step(st):
                    measured = [(q["meas1"], st.item(Y + 1)), (q["meas2"], st.item(FFN2 + 1))]
                    if edges:
                        measured.append((q["meas4"], st.item(S3P + 1)))
                    measured += [(q["meas3"], st.item(X4P + 1)), (q["meas0"], st.item(X3P + 1))]
                    chain = norms.chain(ve, st, measured)
                    for name, lag in (("x4_done", NORM3), ("n2_done", NORM2), ("n1_done", NORM1)):
                        if before := st.item(lag + 2):
                            need(ve, q[name], before)
                            break
                    next(chain, None)
                    if it := st.item(X3P):
                        need(ve, q["z2"], it)
                        need_dma(ve, xh_loaded, it)
                        need(ve, q["x3_done"], it, depth)
                        ve.scalar_tensor_tensor(out=as_tiles(x3p[it.slot]), in0=as_tiles(z[it.slot]), scalar=0.0,
                                                in1=wide(xh[it.slot], 0), op0=ALU.max, op1=ALU.add)\
                          .then_inc(q["x3p_done"], 1)
                        next(chain, None)
                        need(ve, q["x3p_done"], it)
                        norms.take(ve, st, 0, x3p[it.slot], chain).then_inc(q["meas0"], 1)
                        next(chain, None)
                    if it := st.item(X4P):
                        need(ve, q["u_done"], it)
                        need(ve, q["kept"], it)
                        need(ve, q["x4_done"], it, 2)
                        ve.tensor_tensor(x4p[it.slot][:, :], n2[it.slot][:, :], x3l[it.slot][:, :], ALU.add)\
                          .then_inc(q["x4p_done"], 1)
                        next(chain, None)
                        need(ve, q["x4p_done"], it)
                        norms.take(ve, st, 3, x4p[it.slot], chain).then_inc(q["meas3"], 1)
                        next(chain, None)
                    if it := st.item(KEEP):
                        need(ve, q["x3k_done"], it)
                        need(ve, q["x4p_done"], it, R)
                        ve.tensor_copy(x3l[it.slot][:, :], x3k[it.slot][:, :]).then_inc(q["kept"], 1)
                        next(chain, None)
                    if edges and (it := st.item(S3P)):
                        src.wait(ve, it)
                        rows = src.rows[it.slot]
                        need(ve, q["s3p_done"], it, 1)
                        ve.tensor_tensor(as_tiles(sz), wide(rows, 1), as_tiles(sh.bn_scale_4), ALU.mult)\
                          .then_inc(q["sz1"], 1)
                        next(chain, None)
                        need(ve, q["sz1"], it)
                        ve.tensor_tensor(sz[:, :], sz[:, :], sh.bn_shift_4[:, :], ALU.add).then_inc(q["sz2"], 1)
                        next(chain, None)
                        need(ve, q["sz2"], it)
                        need(ve, q["s3_done"], it, R)
                        ve.scalar_tensor_tensor(out=as_tiles(s3p[it.slot]), in0=as_tiles(sz), scalar=0.0,
                                                in1=wide(rows, 0), op0=ALU.max, op1=ALU.add)\
                          .then_inc(q["s3p_done"], 1)
                        next(chain, None)
                        need(ve, q["s3p_done"], it)
                        norms.take(ve, st, 4, s3p[it.slot], chain).then_inc(q["meas4"], 1)
                    if it := st.item(FFN2):
                        need(ve, q["mmo"], it)
                        need(ve, q["n2_done"], it, 2)
                        if not edges:
                            need(ve, q["tb2"], it)
                        ve.tensor_tensor(t2p[it.slot][:, :], bO[:, :],
                                         sh.f2_b_4[:, :] if edges else tb[it.slot][:, :], ALU.add)\
                          .then_inc(q["t2p_done"], 1)
                        next(chain, None)
                        need(ve, q["t2p_done"], it)
                        norms.take(ve, st, 2, t2p[it.slot], chain).then_inc(q["meas2"], 1)
                    if edges and (it := st.item(MMS)):
                        same = sh.same[:, bass.ds(it.n * GROUP, GROUP)]
                        need(ve, q["hmax"], it, 1)
                        ve.tensor_scalar(big[:, :], same, 0.5, 2.0 * BIG, ALU.subtract, ALU.mult)\
                          .then_inc(q["big_done"], 1)
                        next(chain, None)
                        need(ve, q["big_done"], it)
                        need(ve, q["mms"], it)
                        need(ve, q["hmax_b"], it, 2)
                        start = -BIG
                        if not (isinstance(it.n, int) and it.n == 0):
                            start = hmax[it.slot - 1][:, GROUP - 1:GROUP]
                        ve.tensor_tensor_scan(hmax[it.slot][:, :], big[:, :], bS[:, :], start, ALU.min,
                                              ALU.max).then_inc(q["hmax"], 1)
                    for _ in chain:
                        pass
                    if it := st.item(NORM0):
                        norms.ready(ve, st)
                        need(ve, q["x3_T"], it, 2)
                        need(ve, q["x3k_done"], it, 2)
                        norms.apply_vector(ve, st, 0, x3[it.slot], x3p[it.slot]).then_inc(q["x3_done"], 1)
                    if edges and (it := st.item(NORM_S)):
                        norms.ready(ve, st)
                        need(ve, q["s3_T"], it, 2)
                        norms.apply_vector(ve, st, 4, s3[it.slot], s3p[it.slot]).then_inc(q["s3_done"], 1)
                    if edges and (it := st.item(MD)):
                        need(ve, q["hmax_b"], it)
                        need(ve, q["h_out"], it)
                        ve.tensor_tensor(md[it.slot][:, :], md[it.slot][:, :], hT[:, :], ALU.subtract)\
                          .then_inc(q["md_done"], 1)
                    if it := st.item(Y):
                        need(ve, q["mmy"], it)
                        need(ve, q["n1_done"], it, 2)
                        ve.tensor_tensor(t1p[it.slot][:, :], bY[:, :], sh.fold_bias_4[:, :], ALU.add)\
                          .then_inc(q["t1p_done"], 1)
                        need(ve, q["t1p_done"], it)
                        norms.take(ve, st, 1, t1p[it.slot], chain).then_inc(q["meas1"], 1)

                run_steps(ve, count, LAGS, R, step)


def repeat_rows_phase(nc, sh):
    with ExitStack() as stack:
        s = Scope(nc, stack, "rep")
        copied = s.sem("copied")
        with nc.Block() as block:

            @block.vector
            def _(ve):
                link = Link(ve, copied, 0)
                for out, row in ((sh.b2_4, sh.vrow["L0_b2"]), (sh.l1b2_4, sh.vrow["L1_b2"]),
                                 (sh.ln1_g_4, sh.vrow["ln1_g"]), (sh.ln1_b_f2_4, sh.ln1_b_f2[:, :]),
                                 (sh.f2_b_4, sh.vrow["f2_b"]),
                                 (sh.ln2_g_4, sh.vrow["ln2_g"]), (sh.ln2_b_4, sh.vrow["ln2_b"]),
                                 (sh.fold_bias_4, sh.fold_bias[:, :])):
                    for j in range(TILES):
                        link(ve.tensor_copy(tile(out, j), row))
                for name, row in sh.bn_row.items():
                    link(ve.tensor_copy(row, sh.vrow[name]))
                link(ve.memset(sh.sum1[:, :, :], 0.0))
                link(ve.memset(sh.sum2[:, :, :], 0.0))
                link(ve.memset(sh.two[:, :], 2.0))


class Tables:
    pass


def graph_layers(nc, x, src_cols, dst_cols, next_cols, dst_row, edge_attr, mats, vcols, vrows, out):
    dram, sh = Tables(), Shared()
    dram.x, dram.src_cols, dram.dst_cols, dram.next_cols, dram.dst_row = x, src_cols, dst_cols, next_cols, dst_row
    dram.edge_attr, dram.mats, dram.vcols, dram.vrows, dram.out = edge_attr, mats, vcols, vrows, out
    scratch = lambda name, shape: nc.dram_tensor(name, shape, F32, kind="Internal").ap()
    dram.map = scratch("node_map", (NPAD, 2))
    dram.h2 = scratch("h2", (ROWS, P))
    dram.x1 = scratch("x1", (ROWS, P))
    dram.x2h = scratch("x2h", (ROWS, 2 * P))
    dram.x_ends = scratch("x_ends", (EPAD, 2 * P))
    dram.x_own = scratch("x_own", (EPAD, P))
    dram.count_row = scratch("count_row", (1, EPAD))
    with ExitStack() as stack:
        s = Scope(nc, stack, "sh")
        sh.mats = s.sb("mats", [P, len(MATS) * P])
        sh.vcols = s.sb("vcols", [P, len(VECS)])
        sh.mat = {n: sh.mats[:, k * P:(k + 1) * P] for k, n in enumerate(MATS)}
        sh.vcol = {n: sh.vcols[:, k:k + 1] for k, n in enumerate(VECS)}
        sh.ident = s.sb("ident", [P, P])
        sh.started = s.sem("started")
        sh.same = s.sb("same", [P, EPAD], BF16)
        sh.src_cols, sh.dst_cols, sh.rep_rows, sh.src_row, sh.dst_row = (
            s.sb(n, [P, ECOLS], I32) for n in ("src_cols", "dst_cols", "rep_rows", "src_row", "dst_row"))
        sh.is_rep, sh.src_root, sh.dst_root = (s.sb(n, [P, ECOLS]) for n in ("is_rep", "src_root", "dst_root"))
        sh.fold_self, sh.fold_bot = s.sb("fold_self", [P, P]), s.sb("fold_bot", [P, P])
        (sh.ln1_g_4, sh.ln1_b_f2_4, sh.ln2_g_4, sh.ln2_b_4, sh.fold_bias_4, sh.bn_scale_4,
         sh.bn_shift_4, sh.f2_b_4) = (s.sb(n, [P, GROUP]) for n in (
            "ln1_g_4", "ln1_b_f2_4", "ln2_g_4", "ln2_b_4", "fold_bias_4", "bn_scale_4", "bn_shift_4",
            "f2_b_4"))
        with ExitStack() as front_stack:
            f = Scope(nc, front_stack, "shf")
            sh.b2_4, sh.l1b2_4 = f.sb("b2_4", [P, GROUP]), f.sb("l1b2_4", [P, GROUP])
            bn_rows = f.sb("bn_rows", [P, 3, P])
            sh.bn_row = {n: bn_rows[:, k, :] for k, n in enumerate(("bias", "gamma", "beta"))}
            sh.map_rows, sh.src_map, sh.dst_map = (
                f.sb(n, [P, ECOLS, 2]) for n in ("map_rows", "src_map", "dst_map"))
            sh.alone = f.sb("alone", [P, GROUPS * TILES])
            sh.two = f.sb("two", [P, 1])
            sh.sum1, sh.sum2 = f.sb("sum1", [P, TILES, P]), f.sb("sum2", [P, TILES, P])
            sh.att_both = f.sb("att_both", [P, 3, P])
            with ExitStack() as setup_stack:
                first = Scope(nc, setup_stack, "sh0")
                sh.vrows = first.sb("vrows", [P, len(VECS) * P])
                sh.vrow = {n: sh.vrows[:, k * P:(k + 1) * P] for k, n in enumerate(VECS)}
                sh.bc_cols = first.sb("bc_cols", [P, 2, P])
                sh.fold_bias, sh.ln1_b_f2 = first.sb("fold_bias", [P, P]), first.sb("ln1_b_f2", [P, P])
                setup_phase(nc, sh, dram)
                repeat_rows_phase(nc, sh)
            map_phase(nc, sh, dram)
            dense_front_phase(nc, sh, dram)
            edge_gcn1_phase(nc, sh, dram)
            edge_gcn2_phase(nc, sh, dram)
            edge_gine_phase(nc, sh, dram)
            with ExitStack() as gat_stack:
                sh.gat_own = Scope(nc, gat_stack, "g").sb("gat_own", [P, EPAD])
                edge_gat_phase(nc, sh, dram)
                batch_norm_phase(nc, sh, dram)
        back_phase(nc, sh, dram, False)
        back_phase(nc, sh, dram, True)


def kernel(x, src, dst, edge_attr_128, edge_attr_16, **w):
    import numpy as np
    import concourse.bacc as bacc
    from concourse.bass_utils import run_bass_kernel_spmd

    def columns(a):
        return np.ascontiguousarray(a.reshape(ECOLS, P).T)

    def padded(a, fill):
        return np.concatenate([a, np.full((EPAD - EDGES,), fill, a.dtype)])

    W = {k: np.asarray(v) for k, v in w.items()}
    src, dst, x = np.asarray(src), padded(np.asarray(dst), NODES), np.asarray(x)
    x_pad = np.concatenate([x, np.zeros((NPAD - NODES, P), x.dtype)])
    edge_attr = np.asarray(edge_attr_128)
    edge_attr = np.concatenate([edge_attr, np.zeros((EPAD - EDGES, P), edge_attr.dtype)])
    w1t, w2t, upd = W["L0_gnn_W1"].T, W["L0_gnn_W2"].T, W["L3_gnn_W_upd_w"]
    f1, f2 = W["L3_gnn_ffn1_w"], W["L3_gnn_ffn2_w"]
    mats = [w1t[:, :P], w1t[:, P:], w2t[:P], w2t[P:], W["L1_gnn_W1"].T, W["L1_gnn_W2"].T, W["L2_gnn_W"],
            W["L3_gnn_W_in_w"], W["L3_gnn_W_in_w"].T, upd[:P].T, upd[P:].T, W["L3_gnn_W_out_w"]]
    mats += [f1[:, k * P:(k + 1) * P] for k in range(4)] + [f2[k * P:(k + 1) * P] for k in range(4)]
    f1b = W["L3_gnn_ffn1_b"]
    vecs = [W["L0_gnn_b1"][:P], W["L0_gnn_b1"][P:], W["L0_gnn_b2"], W["L1_gnn_b1"], W["L1_gnn_b2"],
            W["L2_gnn_att_src"], W["L2_gnn_att_dst"], W["L2_gnn_bias"], W["L2_gnn_gamma"], W["L2_gnn_beta"],
            W["L3_gnn_W_in_b"], W["L3_gnn_W_upd_b"], W["L3_gnn_W_out_b"], W["L3_gnn_ln1_g"], W["L3_gnn_ln1_b"],
            W["L3_gnn_ln2_g"], W["L3_gnn_ln2_b"]] + [f1b[k * P:(k + 1) * P] for k in range(4)] + [W["L3_gnn_ffn2_b"]]
    arrays = {
        "x": x_pad, "src_cols": columns(padded(src, 0)), "dst_cols": columns(dst),
        "next_cols": columns(np.concatenate([dst[1:], np.full((1,), NODES, dst.dtype)])),
        "dst_row": dst[None, :], "edge_attr": edge_attr,
        "mats": np.ascontiguousarray(np.concatenate(mats, axis=1)),
        "vcols": np.ascontiguousarray(np.stack(vecs, axis=1)), "vrows": np.concatenate(vecs)[None, :],
    }
    nc = bacc.Bacc("TRN2", target_bir_lowering=False, num_devices=1)
    args = [nc.dram_tensor(f"in_{n}", a.shape, mybir.dt.from_np(a.dtype), kind="ExternalInput").ap()
            for n, a in arrays.items()]
    out = nc.dram_tensor("out", (NPAD, P), F32, kind="ExternalOutput").ap()
    graph_layers(nc, *args, out)
    result = run_bass_kernel_spmd(nc, [{f"in_{n}": a for n, a in arrays.items()}], core_ids=[0])
    return result.results[0]["out"][:NODES]
```
